# Optimizing a Trainium2 kernel written in Bass

```python
import numpy as np
import jax
import jax.numpy as jnp

def _softmax(x, axis=-1):
    return jax.nn.softmax(x, axis=axis)

def _gelu(x):
    return jax.nn.gelu(x, approximate=True)

def _silu(x):
    return jax.nn.silu(x)

def _sigmoid(x):
    return jax.nn.sigmoid(x)

def _layernorm(x, axis=-1, eps=1e-05):
    m = jnp.mean(x, axis=axis, keepdims=True)
    v = jnp.var(x, axis=axis, keepdims=True)
    return (x - m) / jnp.sqrt(v + eps)

def _scatter_add(tgt, idx, src, axis=0):
    return tgt.at[idx].add(src)

def _segment_sum(src, seg, n):
    return jax.ops.segment_sum(src, seg, n)
kernel_name = 'mk_xattn_ffn_d2_seqx_r4_27c215'

def setup_inputs(seed: int=0):
    np.random.seed(seed)
    _w = jnp.asarray

    def _rec_inputs():
        import jax
        import jax.numpy as jnp
        _rk = jax.random.key(seed)
        x = 4.136e-05 + 0.9999 * jax.random.normal(jax.random.fold_in(_rk, 1), (16, 256, 256), jnp.float32)
        _lenS = 256 - jax.random.randint(jax.random.fold_in(_rk, 7), (16,), 0, max(1, 256 // 4) + 1, jnp.int32)
        _lenS2 = 256 - jax.random.randint(jax.random.fold_in(_rk, 8), (16,), 0, max(1, 256 // 4) + 1, jnp.int32)
        _ctx_2048P = jax.random.normal(jax.random.fold_in(_rk, 11), (16, 16, 512), jnp.float32)
        _ctx_2048c = jax.random.dirichlet(jax.random.fold_in(_rk, 511), 0.3 * jnp.ones((16,), jnp.float32), (16, 256))
        _ctx_2048t = jnp.einsum('bsk,bkd->bsd', _ctx_2048c, _ctx_2048P)
        _ctx_2048t = _ctx_2048t * jax.lax.rsqrt(jnp.mean(jnp.square(_ctx_2048t)) + 1e-12) * 0.953939
        ctx_2048 = -0.000392918 + 0.999932 * (_ctx_2048t + 0.3 * jax.random.normal(jax.random.fold_in(_rk, 611), (16, 256, 512), jnp.float32))
        itok_Bx1_68_817 = jax.random.randint(jax.random.fold_in(_rk, 12), (16, 1), 68, 818, jnp.int32)
        _validS = jnp.arange(256)[None, :] < _lenS[:, None]
        _validS2 = jnp.arange(256)[None, :] < _lenS2[:, None]
        _causal = jnp.tril(jnp.ones((256, 256), dtype=bool))
        mask_BxS2_if0 = jnp.where(jnp.ones((16, 256), dtype=bool), 4, 0).astype(jnp.int32)
        return (x, ctx_2048, itok_Bx1_68_817, mask_BxS2_if0)
    x, ctx_2048, itok_Bx1_68_817, mask_BxS2_if0 = _rec_inputs()

    def _L0_xattn_setup():
        import jax, jax.numpy as jnp
        import numpy as np
        UNITS = 256
        NUM_HEADS = 16
        MASK_VALUE = -1000000000000.0

        def _split_heads(x, n):
            B, S, D = x.shape
            return x.reshape(B, S, n, D // n).transpose(0, 2, 1, 3)
        key = jax.random.key(seed)
        k1, k2, k3, k4 = jax.random.split(key, 4)
        B, S = (8, 256)
        memory = jax.random.normal(k1, (B, S, 2 * UNITS), dtype=jnp.float32)
        query = jax.random.normal(k2, (B, S, UNITS), dtype=jnp.float32)
        b = jax.random.normal(k3, (S,), dtype=jnp.float32)
        seq_len = jax.random.randint(k4, (B, 1), 0, S, dtype=jnp.int32)
        return {'memory': memory, 'query': query, 'b': b, 'seq_len': seq_len}
    _L0_xattn_all = _L0_xattn_setup()
    _L0_xattn_in = {k: v for k, v in _L0_xattn_all.items() if k in ('b',)}
    del _L0_xattn_all

    def _L0_ffn_setup():
        import jax, jax.numpy as jnp
        import numpy as np
        D_MODEL = 256
        N_HEADS = 16
        HEAD_DIM = D_MODEL // N_HEADS
        FFN_DIM = 1024
        N_EXPERTS = 8
        TOP_K = 2
        BATCH = 4
        SEQ = 256

        def _layernorm(x, w, b, eps=1e-05):
            mu = jnp.mean(x, axis=-1, keepdims=True)
            var = jnp.mean(jnp.square(x - mu), axis=-1, keepdims=True)
            return (x - mu) * jax.lax.rsqrt(var + eps) * w + b

        def _causal_attention(nx, Wqkv, bqkv, Wo, bo):
            B, S, D = nx.shape
            qkv = nx @ Wqkv + bqkv
            q, k, v = jnp.split(qkv, 3, axis=-1)
            q = q.reshape(B, S, N_HEADS, HEAD_DIM)
            k = k.reshape(B, S, N_HEADS, HEAD_DIM)
            v = v.reshape(B, S, N_HEADS, HEAD_DIM)
            scores = jnp.einsum('bqhd,bkhd->bhqk', q, k) / jnp.sqrt(jnp.float32(HEAD_DIM))
            causal = jnp.tril(jnp.ones((S, S), bool))
            scores = jnp.where(causal, scores, jnp.finfo(scores.dtype).min)
            attn = jax.nn.softmax(scores, axis=-1)
            out = jnp.einsum('bhqk,bkhd->bqhd', attn, v).reshape(B, S, D)
            return out @ Wo + bo

        def _moe_ffn(nx, gate_W, fc1_w, fc1_b, fc2_w, fc2_b):
            gate_logits = nx @ gate_W
            topk_vals, topk_idx = jax.lax.top_k(gate_logits, TOP_K)
            gate_w = jax.nn.softmax(topk_vals, axis=-1)
            dense_gates = jnp.sum(jax.nn.one_hot(topk_idx, N_EXPERTS, dtype=nx.dtype) * gate_w[..., None], axis=-2)
            moe_out = jnp.zeros_like(nx)
            for e in range(N_EXPERTS):
                h = jax.nn.gelu(jnp.einsum('bsd,fd->bsf', nx, fc1_w[e]) + fc1_b[e], approximate=False)
                y = jnp.einsum('bsf,df->bsd', h, fc2_w[e]) + fc2_b[e]
                moe_out = moe_out + y * dense_gates[..., e:e + 1]
            return moe_out
        key = jax.random.key(seed)
        ks = jax.random.split(key, 12)
        s = lambda k, shape, scale: jax.random.normal(k, shape, dtype=jnp.float32) * scale
        inp = {'x': s(ks[0], (BATCH, SEQ, D_MODEL), 1.0), 'ln1_w': jnp.ones((D_MODEL,), jnp.float32), 'ln1_b': jnp.zeros((D_MODEL,), jnp.float32), 'ln2_w': jnp.ones((D_MODEL,), jnp.float32), 'ln2_b': jnp.zeros((D_MODEL,), jnp.float32), 'Wqkv': s(ks[1], (D_MODEL, 3 * D_MODEL), 0.02), 'bqkv': jnp.zeros((3 * D_MODEL,), jnp.float32), 'Wo': s(ks[2], (D_MODEL, D_MODEL), 0.02), 'bo': jnp.zeros((D_MODEL,), jnp.float32), 'gate_W': s(ks[3], (D_MODEL, N_EXPERTS), 0.02), 'fc1_w': s(ks[4], (N_EXPERTS, FFN_DIM, D_MODEL), (2.0 / D_MODEL) ** 0.5), 'fc1_b': jnp.zeros((N_EXPERTS, FFN_DIM), jnp.float32), 'fc2_w': s(ks[5], (N_EXPERTS, D_MODEL, FFN_DIM), (1.0 / FFN_DIM) ** 0.5), 'fc2_b': jnp.zeros((N_EXPERTS, D_MODEL), jnp.float32)}
        return inp
    _L0_ffn_all = _L0_ffn_setup()
    _L0_ffn_in = {k: v for k, v in _L0_ffn_all.items() if k in ('ln1_w', 'ln1_b', 'ln2_w', 'ln2_b', 'Wqkv', 'bqkv', 'Wo', 'bo', 'gate_W', 'fc1_w', 'fc1_b', 'fc2_w', 'fc2_b')}
    del _L0_ffn_all

    def _L1_xattn_setup():
        import jax, jax.numpy as jnp
        import numpy as np
        B, L, P = (4, 1024, 256)
        D_MODEL = 256
        D_GLOBAL = 512
        HEADDIM = 32
        EPSILON = 0.001
        RMS_EPS = 1e-05

        def rmsnorm(x, g, eps=RMS_EPS):
            var = jnp.mean(jnp.square(x), axis=-1, keepdims=True)
            return x * jax.lax.rsqrt(var + eps) * g

        def _hnet_depool(h, h_patch_full, patch_lens):
            h_patch = h_patch_full[..., :D_MODEL]
            bsz, plen = (h_patch.shape[0], h_patch.shape[1])
            seqlen = h.shape[1]
            logp = jnp.full((bsz, plen), -EPSILON, dtype=jnp.float32)
            bidx = jnp.cumsum(patch_lens, axis=1) - 1
            boundary_mask = jnp.zeros((bsz, seqlen), dtype=jnp.int32)
            boundary_mask = boundary_mask.at[jnp.arange(bsz)[:, None], bidx].set(1)
            dt = (-jnp.log(-jnp.expm1(logp))).astype(h_patch.dtype)
            x = h_patch / dt[..., None]
            n_heads = D_MODEL // HEADDIM
            A = -jnp.ones((n_heads,), dtype=jnp.float32)
            bcoef = jnp.exp(logp).astype(h_patch.dtype)
            x4 = x.reshape(bsz, plen, n_heads, HEADDIM)
            a = jnp.exp(dt[:, :, None] * A[None, None, :])
            u = (dt * bcoef)[:, :, None, None] * x4
            a_b = jnp.broadcast_to(a[..., None], u.shape)

            def comb(lft, rgt):
                aL, uL = lft
                aR, uR = rgt
                return (aL * aR, uL * aR + uR)
            _, s = jax.lax.associative_scan(comb, (a_b, u), axis=1)
            depool = s.reshape(bsz, plen, D_MODEL)
            plug = jnp.clip(jnp.cumsum(boundary_mask, axis=1) - 1, 0, plen - 1)
            depool_out = depool[jnp.arange(bsz)[:, None], plug]
            return depool_out + h
        key = jax.random.key(seed)
        k1, k2, k3, k4 = jax.random.split(key, 4)
        embeds = jax.random.normal(k1, (B, L, D_MODEL), dtype=jnp.float32)
        patch_embeds = jax.random.normal(k2, (B, P, D_GLOBAL), dtype=jnp.float32)
        patch_lens = jnp.full((B, P), L // P, dtype=jnp.int64)
        W_in = jax.random.normal(k3, (D_MODEL, D_MODEL), dtype=jnp.float32) * 0.02
        b_in = jnp.zeros((D_MODEL,), dtype=jnp.float32)
        g_res = jnp.ones((D_MODEL,), dtype=jnp.float32)
        g_init = jnp.ones((D_GLOBAL,), dtype=jnp.float32)
        return {'embeds': embeds, 'patch_embeds': patch_embeds, 'patch_lens': patch_lens, 'W_in': W_in, 'b_in': b_in, 'g_res': g_res, 'g_init': g_init}
    _L1_xattn_all = _L1_xattn_setup()
    _L1_xattn_in = {k: v for k, v in _L1_xattn_all.items() if k in ('W_in', 'b_in', 'g_res', 'g_init')}
    del _L1_xattn_all

    def _L1_ffn_setup():
        import jax, jax.numpy as jnp
        import numpy as np
        FEATURES = 256
        D_IN = 256

        def fp8_gemm_optimized(x, input_scale, kernel, kernel_scale):
            s_in = input_scale[0]
            s_k = kernel_scale[0]
            x_q = (x.astype(jnp.float32) / s_in).astype(jnp.float8_e4m3fn)
            k_q = (kernel.astype(jnp.float32) / s_k).astype(jnp.float8_e4m3fn)
            y = jnp.dot(x_q.astype(jnp.float32), k_q.astype(jnp.float32), preferred_element_type=jnp.float32)
            return y * (s_in * s_k)
        key = jax.random.key(seed)
        kx, kk, kb = jax.random.split(key, 3)
        x = jax.random.normal(kx, (4, 2048, D_IN), dtype=jnp.float32)
        limit = np.sqrt(6.0 / (D_IN + FEATURES)).astype(np.float32)
        kernel = jax.random.uniform(kk, (D_IN, FEATURES), dtype=jnp.float32, minval=-limit, maxval=limit).astype(jnp.bfloat16)
        input_scale = jnp.ones((1,), dtype=jnp.float32)
        kernel_scale = jnp.ones((1,), dtype=jnp.float32)
        bias = jnp.zeros((FEATURES,), dtype=jnp.bfloat16)
        return {'x': x, 'kernel': kernel, 'input_scale': input_scale, 'kernel_scale': kernel_scale, 'bias': bias}
    _L1_ffn_all = _L1_ffn_setup()
    _L1_ffn_in = {k: v for k, v in _L1_ffn_all.items() if k in ('kernel', 'input_scale', 'kernel_scale', 'bias')}
    del _L1_ffn_all
    return {'x': x, 'ctx_2048': ctx_2048, 'itok_Bx1_68_817': itok_Bx1_68_817, 'mask_BxS2_if0': mask_BxS2_if0, 'L0_xattn_b': _L0_xattn_in['b'], 'L0_ffn_ln1_w': _L0_ffn_in['ln1_w'], 'L0_ffn_ln1_b': _L0_ffn_in['ln1_b'], 'L0_ffn_ln2_w': _L0_ffn_in['ln2_w'], 'L0_ffn_ln2_b': _L0_ffn_in['ln2_b'], 'L0_ffn_Wqkv': _L0_ffn_in['Wqkv'], 'L0_ffn_bqkv': _L0_ffn_in['bqkv'], 'L0_ffn_Wo': _L0_ffn_in['Wo'], 'L0_ffn_bo': _L0_ffn_in['bo'], 'L0_ffn_gate_W': _L0_ffn_in['gate_W'], 'L0_ffn_fc1_w': _L0_ffn_in['fc1_w'], 'L0_ffn_fc1_b': _L0_ffn_in['fc1_b'], 'L0_ffn_fc2_w': _L0_ffn_in['fc2_w'], 'L0_ffn_fc2_b': _L0_ffn_in['fc2_b'], 'L1_xattn_W_in': _L1_xattn_in['W_in'], 'L1_xattn_b_in': _L1_xattn_in['b_in'], 'L1_xattn_g_res': _L1_xattn_in['g_res'], 'L1_xattn_g_init': _L1_xattn_in['g_init'], 'L1_ffn_kernel': _L1_ffn_in['kernel'], 'L1_ffn_input_scale': _L1_ffn_in['input_scale'], 'L1_ffn_kernel_scale': _L1_ffn_in['kernel_scale'], 'L1_ffn_bias': _L1_ffn_in['bias']}

def reference(x, ctx_2048, itok_Bx1_68_817, mask_BxS2_if0, L0_xattn_b, L0_ffn_ln1_w, L0_ffn_ln1_b, L0_ffn_ln2_w, L0_ffn_ln2_b, L0_ffn_Wqkv, L0_ffn_bqkv, L0_ffn_Wo, L0_ffn_bo, L0_ffn_gate_W, L0_ffn_fc1_w, L0_ffn_fc1_b, L0_ffn_fc2_w, L0_ffn_fc2_b, L1_xattn_W_in, L1_xattn_b_in, L1_xattn_g_res, L1_xattn_g_init, L1_ffn_kernel, L1_ffn_input_scale, L1_ffn_kernel_scale, L1_ffn_bias):
    import jax
    import jax.numpy as jnp

    def _L0_xattn_ref(memory, query, b, seq_len):
        import jax, jax.numpy as jnp
        import numpy as np
        UNITS = 256
        NUM_HEADS = 16
        MASK_VALUE = -1000000000000.0

        def _split_heads(x, n):
            B, S, D = x.shape
            return x.reshape(B, S, n, D // n).transpose(0, 2, 1, 3)
        B, S, _ = query.shape
        dh = UNITS // NUM_HEADS
        k_mem, v_mem = jnp.split(memory, 2, axis=2)
        Q = _split_heads(query, NUM_HEADS) * dh ** (-0.5)
        Kh = _split_heads(k_mem, NUM_HEADS)
        Vh = _split_heads(v_mem, NUM_HEADS)
        logits = jnp.einsum('bhqd,bhkd->bhqk', Q, Kh) + b
        valid = (jnp.arange(S)[None, :] < seq_len[:, 0:1]).astype(jnp.float32)
        logits = logits + MASK_VALUE * (1.0 - valid)[:, None, None, :]
        weights = jax.nn.softmax(logits, axis=-1)
        out = jnp.einsum('bhqk,bhkd->bhqd', weights, Vh)
        return out.transpose(0, 2, 1, 3).reshape(B, S, UNITS)

    def _L0_ffn_ref(x, ln1_w, ln1_b, ln2_w, ln2_b, Wqkv, bqkv, Wo, bo, gate_W, fc1_w, fc1_b, fc2_w, fc2_b):
        import jax, jax.numpy as jnp
        import numpy as np
        D_MODEL = 256
        N_HEADS = 16
        HEAD_DIM = D_MODEL // N_HEADS
        FFN_DIM = 1024
        N_EXPERTS = 8
        TOP_K = 2
        BATCH = 4
        SEQ = 256

        def _layernorm(x, w, b, eps=1e-05):
            mu = jnp.mean(x, axis=-1, keepdims=True)
            var = jnp.mean(jnp.square(x - mu), axis=-1, keepdims=True)
            return (x - mu) * jax.lax.rsqrt(var + eps) * w + b

        def _causal_attention(nx, Wqkv, bqkv, Wo, bo):
            B, S, D = nx.shape
            qkv = nx @ Wqkv + bqkv
            q, k, v = jnp.split(qkv, 3, axis=-1)
            q = q.reshape(B, S, N_HEADS, HEAD_DIM)
            k = k.reshape(B, S, N_HEADS, HEAD_DIM)
            v = v.reshape(B, S, N_HEADS, HEAD_DIM)
            scores = jnp.einsum('bqhd,bkhd->bhqk', q, k) / jnp.sqrt(jnp.float32(HEAD_DIM))
            causal = jnp.tril(jnp.ones((S, S), bool))
            scores = jnp.where(causal, scores, jnp.finfo(scores.dtype).min)
            attn = jax.nn.softmax(scores, axis=-1)
            out = jnp.einsum('bhqk,bkhd->bqhd', attn, v).reshape(B, S, D)
            return out @ Wo + bo

        def _moe_ffn(nx, gate_W, fc1_w, fc1_b, fc2_w, fc2_b):
            gate_logits = nx @ gate_W
            topk_vals, topk_idx = jax.lax.top_k(gate_logits, TOP_K)
            gate_w = jax.nn.softmax(topk_vals, axis=-1)
            dense_gates = jnp.sum(jax.nn.one_hot(topk_idx, N_EXPERTS, dtype=nx.dtype) * gate_w[..., None], axis=-2)
            moe_out = jnp.zeros_like(nx)
            for e in range(N_EXPERTS):
                h = jax.nn.gelu(jnp.einsum('bsd,fd->bsf', nx, fc1_w[e]) + fc1_b[e], approximate=False)
                y = jnp.einsum('bsf,df->bsd', h, fc2_w[e]) + fc2_b[e]
                moe_out = moe_out + y * dense_gates[..., e:e + 1]
            return moe_out
        nx = _layernorm(x, ln1_w, ln1_b)
        attn_out = _causal_attention(nx, Wqkv, bqkv, Wo, bo)
        x = x + attn_out
        nx2 = _layernorm(x, ln2_w, ln2_b)
        moe_out = _moe_ffn(nx2, gate_W, fc1_w, fc1_b, fc2_w, fc2_b)
        return x + moe_out

    def _L1_xattn_ref(embeds, patch_embeds, patch_lens, W_in, b_in, g_res, g_init):
        import jax, jax.numpy as jnp
        import numpy as np
        B, L, P = (4, 1024, 256)
        D_MODEL = 256
        D_GLOBAL = 512
        HEADDIM = 32
        EPSILON = 0.001
        RMS_EPS = 1e-05

        def rmsnorm(x, g, eps=RMS_EPS):
            var = jnp.mean(jnp.square(x), axis=-1, keepdims=True)
            return x * jax.lax.rsqrt(var + eps) * g

        def _hnet_depool(h, h_patch_full, patch_lens):
            h_patch = h_patch_full[..., :D_MODEL]
            bsz, plen = (h_patch.shape[0], h_patch.shape[1])
            seqlen = h.shape[1]
            logp = jnp.full((bsz, plen), -EPSILON, dtype=jnp.float32)
            bidx = jnp.cumsum(patch_lens, axis=1) - 1
            boundary_mask = jnp.zeros((bsz, seqlen), dtype=jnp.int32)
            boundary_mask = boundary_mask.at[jnp.arange(bsz)[:, None], bidx].set(1)
            dt = (-jnp.log(-jnp.expm1(logp))).astype(h_patch.dtype)
            x = h_patch / dt[..., None]
            n_heads = D_MODEL // HEADDIM
            A = -jnp.ones((n_heads,), dtype=jnp.float32)
            bcoef = jnp.exp(logp).astype(h_patch.dtype)
            x4 = x.reshape(bsz, plen, n_heads, HEADDIM)
            a = jnp.exp(dt[:, :, None] * A[None, None, :])
            u = (dt * bcoef)[:, :, None, None] * x4
            a_b = jnp.broadcast_to(a[..., None], u.shape)

            def comb(lft, rgt):
                aL, uL = lft
                aR, uR = rgt
                return (aL * aR, uL * aR + uR)
            _, s = jax.lax.associative_scan(comb, (a_b, u), axis=1)
            depool = s.reshape(bsz, plen, D_MODEL)
            plug = jnp.clip(jnp.cumsum(boundary_mask, axis=1) - 1, 0, plen - 1)
            depool_out = depool[jnp.arange(bsz)[:, None], plug]
            return depool_out + h
        h = rmsnorm(embeds, g_res)
        h = jnp.einsum('bld,ed->ble', h, W_in) + b_in
        h_patch = rmsnorm(patch_embeds, g_init)
        return _hnet_depool(h, h_patch, patch_lens)

    def _L1_ffn_ref(x, kernel, input_scale, kernel_scale, bias):
        import jax, jax.numpy as jnp
        import numpy as np
        FEATURES = 256
        D_IN = 256

        def fp8_gemm_optimized(x, input_scale, kernel, kernel_scale):
            s_in = input_scale[0]
            s_k = kernel_scale[0]
            x_q = (x.astype(jnp.float32) / s_in).astype(jnp.float8_e4m3fn)
            k_q = (kernel.astype(jnp.float32) / s_k).astype(jnp.float8_e4m3fn)
            y = jnp.dot(x_q.astype(jnp.float32), k_q.astype(jnp.float32), preferred_element_type=jnp.float32)
            return y * (s_in * s_k)
        dtype = jnp.bfloat16
        x = x.astype(dtype)
        orig_shape = x.shape
        x2 = x.reshape(-1, x.shape[-1])
        y = fp8_gemm_optimized(x2, input_scale, kernel, kernel_scale)
        y = y.astype(dtype) + bias
        return y.reshape(orig_shape[:-1] + (FEATURES,))
    x = x + _L0_xattn_ref(ctx_2048, _layernorm(x, axis=-1), L0_xattn_b, itok_Bx1_68_817)
    x = x + _L0_ffn_ref(_layernorm(x, axis=-1), L0_ffn_ln1_w, L0_ffn_ln1_b, L0_ffn_ln2_w, L0_ffn_ln2_b, L0_ffn_Wqkv, L0_ffn_bqkv, L0_ffn_Wo, L0_ffn_bo, L0_ffn_gate_W, L0_ffn_fc1_w, L0_ffn_fc1_b, L0_ffn_fc2_w, L0_ffn_fc2_b)
    x = x + _L1_xattn_ref(_layernorm(x, axis=-1), ctx_2048, mask_BxS2_if0, L1_xattn_W_in, L1_xattn_b_in, L1_xattn_g_res, L1_xattn_g_init)
    x = x + _L1_ffn_ref(_layernorm(x, axis=-1), L1_ffn_kernel, L1_ffn_input_scale, L1_ffn_kernel_scale, L1_ffn_bias)
    return x

_drawn_inputs = setup_inputs


def setup_inputs(seed=0):
    import zlib

    import numpy as np

    out = dict(_drawn_inputs(seed))
    spreads = {'L0_ffn_ln1_w': (1.0, 0.2),
     'L0_ffn_ln1_b': (0.0, 0.295),
     'L0_ffn_ln2_w': (1.0, 0.2),
     'L0_ffn_ln2_b': (0.0, 0.1),
     'L0_ffn_bqkv': (0.0, 0.1),
     'L0_ffn_bo': (0.0, 0.1),
     'L0_ffn_fc1_b': (0.0, 0.356),
     'L0_ffn_fc2_b': (0.0, 0.1),
     'L1_xattn_b_in': (0.0, 0.1),
     'L1_xattn_g_res': (1.0, 0.6),
     'L1_xattn_g_init': (1.0, 0.2),
     'L1_ffn_bias': (0.0, 0.1)}
    factors = {}
    for name, (base, spread) in spreads.items():
        noise = np.random.default_rng([zlib.crc32(name.encode()), seed]).standard_normal(out[name].shape)
        drawn = base * np.exp(spread * noise) if base else spread * noise
        out[name] = jnp.asarray(drawn.astype(out[name].dtype))
    for name, factor in factors.items():
        out[name] = (out[name] * factor).astype(out[name].dtype)
    return out
```

```python
import math
from contextlib import ExitStack

import concourse.bass as bass
from concourse import mybir

F32 = mybir.dt.float32
BF16 = mybir.dt.bfloat16
I32 = mybir.dt.int32
U32 = mybir.dt.uint32
ALU = mybir.AluOpType
ACT = mybir.ActivationFunctionType
AX = mybir.AxisListType

P = 128
B, S, D = 16, 256, 256
DC = 512
H, DH = 16, 16
NT = B * S // P
QT = S // P
KD = D // P
E, F, TOPK = 8, 1024, 2
FT = F // P
HB = 64
GROUPS = 8
STEPS = 16
NPT = 4
TB = 512
NTB = B * S // TB
EPS = 1e-5
PATCH_EPS = 0.001
NEG_BIG = -1e12
C20 = 1.5 * 2.0 ** 20

CF_ID, CF_IOTA, CF_ROW, CF_TRI, CF_ONE, CF_L0, CF_L1, CF_N = 0, 128, 384, 386, 514, 642, 770, 898
CB_ID, CB_MQ, CB_MK, CB_ONE, CB_N = 0, 128, 384, 640, 768
RW_QKV, RW_O, RW_FC2, RW_IN, RW_N = 0, 768, 1024, 1024 + 8 * 256, 1280 + 8 * 256


class Steps:

    def __init__(self, sem, names):
        self.sem, self.names, self.n = sem, names.split(), len(names.split())

    def at(self, name, b):
        return b * self.n + self.names.index(name) + 1


class Turn:

    def __init__(self, i, ref=None):
        self.i, self.ref = i, i if ref is None else ref
        self.loop = ref is not None

    def b(self, lag):
        return self.i - lag

    def on(self, lag):
        return self.loop or 0 <= self.i - lag < B

    def first(self, lag):
        return self.ref - lag == 0


T_HEAD1 = [("x_kt0", 0), ("x_kt1", 0), ("x_qt0", 0), ("x_qt1", 0), ("c_m0", 2), ("c_m1", 2)]
T_SEG1 = [("c_xt", 1), ("c_qk0", 1), ("c_v", 1), ("c_qk1", 1)]
T_HEAD2 = [("c_kt0", 1), ("c_kt1", 1), ("c_qt0", 1), ("c_qt1", 1), ("x_m0", 0), ("x_m1", 0)]
T_SEG2 = [("c_back0", 2), ("c_back1", 2), ("c_at", 2), ("c_wo", 2), ("c_nt", 2), ("c_gate", 2)]
T_TAIL2 = [("x_back0", 0), ("x_back1", 0)]


def ring_table(uses):
    table, count = {}, 0
    for i in range(B + 2):
        for name, lag in uses:
            if 0 <= i - lag < B:
                table[name, i - lag] = count
                count += 1
    return table


T_USES = T_HEAD1 + T_SEG1 + T_HEAD2 + T_SEG2 + T_TAIL2
O_USES = [("c", 2), ("x", 0)]
S1_USES = [("x", 0), ("c", 1)]
S2_USES = [("c", 2), ("x", 0)]


def attention_phase(nc, io, keep, sem):
    T_TAB = ring_table(T_USES)
    O_TAB, S1_TAB, S2_TAB = (ring_table(u) for u in (O_USES, S1_USES, S2_USES))
    T_PER = len(T_USES)
    bank_of = {name: k % 2 for k, (name, _) in enumerate(T_USES)}

    res, nxh, nxl, logits, cf, cb = keep["res"], keep["nxh"], keep["nxl"], keep["logits"], keep["cf"], keep["cb"]
    rows, kext, any4, lncol = keep["rows"], keep["kext"], keep["any4"], keep["lncol"]

    with ExitStack() as ctx:
        def sb(name, shape, dt=F32):
            return ctx.enter_context(nc.sbuf_tensor(name, shape, dt))

        ctxb = sb("ctxb", [P, QT, DC])
        wqkv = sb("wqkv", [P, KD, 3 * D])
        wo = sb("wo", [P, KD, D])
        wgate = sb("wgate", [P, KD, E])
        halfneg = sb("halfneg", [P, 2])

        qs = {k: sb(f"qs_{k}", [P, QT, H, HB], BF16) for k in "xc"}
        ks = {k: sb(f"ks_{k}", [P, QT, H, HB], BF16) for k in "xc"}
        qt = {k: sb(f"qt_{k}", [P, GROUPS, S], BF16) for k in "xc"}
        kt = {k: sb(f"kt_{k}", [P, GROUPS, S], BF16) for k in "xc"}
        v1 = {k: sb(f"v1_{k}", [P, QT, H, 32]) for k in "xc"}
        qf = {k: sb(f"qf_{k}", [P, QT, D]) for k in "xc"}
        negm = {k: sb(f"negm_{k}", [P, QT, H]) for k in "xc"}
        mres = {k: sb(f"mres_{k}", [P, QT, H]) for k in "xc"}
        att = {k: sb(f"att_{k}", [P, QT, D]) for k in "xc"}
        rden = {k: sb(f"rden_{k}", [P, QT, H]) for k in "xc"}
        ot = {k: sb(f"ot_{k}", [P, 4, S]) for k in "xc"}
        st = {k: sb(f"st_{k}", [P, QT, 6]) for k in "xc"}
        mv = {k: sb(f"mv_{k}", [P, QT, 2]) for k in "xc"}
        rs = {k: sb(f"rs_{k}", [P, 8, QT]) for k in "xc"}
        st2, mv2 = sb("st2", [P, QT, 6]), sb("mv2", [P, QT, 2])
        rs2 = sb("rs2", [P, 2, QT])
        kf = sb("kf", [P, QT, D])
        xin = sb("xin", [P, 2, QT, D])
        xh = sb("xh", [P, QT, D])
        nxt = sb("nxt", [P, KD, S])
        at = sb("at", [P, KD, S])
        xp = sb("xp", [P, QT, D])
        xh2 = sb("xh2", [P, QT, D])
        n2 = sb("n2", [P, KD, S])
        prob = sb("prob", [P, NPT, 2, S])

        tb = [ctx.enter_context(nc.psum_tensor(f"tb{n}", [P, 512], F32)) for n in range(2)]
        s1 = [ctx.enter_context(nc.psum_tensor(f"s1_{n}", [P, 2, S], F32)) for n in range(2)]
        s2 = [ctx.enter_context(nc.psum_tensor(f"s2_{n}", [P, 2, S], F32)) for n in range(2)]
        ob = ctx.enter_context(nc.psum_tensor("ob", [P, 4, S], F32))

        s_load, s_ctx, s_set = sem("a_load"), sem("a_ctx"), sem("a_pool_setup")
        t_full, t_free = [sem(f"t_full{n}") for n in range(2)], [sem(f"t_free{n}") for n in range(2)]
        s1_full, s1_free = sem("s1_full"), sem("s1_free")
        s2_full, s2_free = sem("s2_full"), sem("s2_free")
        p_full, p_free = sem("p_full"), sem("p_free")
        o_free = sem("o_free")
        s_seen = {e.engine: sem(f"a_seen_{n}") for e, n in ((nc.gpsimd, "pool"), (nc.vector, "dve"))}
        XD0 = Steps(sem("x_dve_pre"), "stats aggr q klo qlo")
        XD1 = Steps(sem("x_dve"), "m_hi m_res m_mid m_lo rec0 rec1")
        XP0 = Steps(sem("x_pool_pre"), "veps rstd rq khi2 qhi2 kext")
        XP1 = Steps(sem("x_pool"), "v x1")
        XA0 = Steps(sem("x_act_pre"), "khi qhi")
        CD1 = Steps(sem("c1_dve"), "stats aggr xin xh klo qlo m_hi m_res m_mid m_lo")
        CD2 = Steps(sem("c2_dve"), "rec0 rec1 stats2 aggr2 xh2 nlo")
        CP1 = Steps(sem("c1_pool"), "veps r1 r1sq v2 v2eps r2 r12 khi2 qhi2")
        CP2 = Steps(sem("c2_pool"), "veps2 rstd2 x2")
        CA1 = Steps(sem("c1_act"), "khi qhi")
        CA2 = Steps(sem("c2_act"), "nhi")
        DVE_SPLIT, POOL_SPLIT, ACT_SPLIT = {"x": XD0, "c": CD1}, {"x": XP0, "c": CP1}, {"x": XA0, "c": CA1}
        DVE_MAX, DVE_OUT = {"x": XD1, "c": CD1}, {"x": XD1, "c": CD2}

        def wait(eng, s, value):
            if not isinstance(value, int) or value > 0:
                eng.wait_ge(s, value)

        def passed(eng, steps, name, t, lag, back=0):
            if t.ref - lag - back >= 0:
                eng.wait_ge(steps.sem, steps.at(name, t.b(lag) - back))
                if t.loop and (eng is nc.gpsimd or name in ("stats", "stats2")):
                    eng.sem_inc(s_seen[eng.engine], 1)

        def t_use(t, name, lag, back=0):
            base = T_TAB[name, t.ref - lag - back] // 2
            return base + (t.i - t.ref) * (T_PER // 2) if t.loop else base

        def t_wait_full(eng, t, name, lag, back=0):
            if t.ref - lag - back >= 0:
                eng.wait_ge(t_full[bank_of[name]], t_use(t, name, lag, back) + 1)

        def t_wait_free(eng, t, name, lag):
            wait(eng, t_free[bank_of[name]], t_use(t, name, lag))

        def t_wait_read(eng, t, name, lag, back=0):
            if t.ref - lag - back >= 0:
                eng.wait_ge(t_free[bank_of[name]], t_use(t, name, lag, back) + 1)

        def ring(table, t, kind, lag, k, back=0):
            base = table[kind, t.ref - lag - back]
            return (base + (t.i - t.ref) * 2 if t.loop else base) * STEPS + k

        def products_done(eng, k, t, lag, back=0):
            if t.ref - lag - back >= 0:
                eng.wait_ge(p_free, ring(S2_TAB, t, k, lag, STEPS - 1, back) + 1)

        def o_count(t, k, lag):
            base = O_TAB[k, t.ref - lag]
            return base + (t.i - t.ref) * 2 if t.loop else base

        def heads(g):
            return [4 * (g // 2) + g % 2, 4 * (g // 2) + g % 2 + 2]

        def parity(b):
            return bass.ds(b % 2, 1)

        TOK = lambda t, lag: bass.ds(t.b(lag) * QT, QT)

        block = ctx.enter_context(nc.Block())

        n_load = 3

        @block.sync
        def _(sp):
            for dst, src in (
                (wqkv[:], io["wqkv"].rearrange("(k p) n -> p k n", p=P)),
                (wo[:], io["wo"].rearrange("(k p) n -> p k n", p=P)),
                (wgate[:], io["wgate"].rearrange("(k p) n -> p k n", p=P)),
            ):
                sp.dma_start(dst, src).then_inc(s_load, 16)

            def load_ctx(t, lag):
                passed(sp, XD0, "klo", t, lag, 1)
                passed(sp, XP1, "v", t, lag, 1)
                sp.dma_start(ctxb[:], io["ctx"][bass.ds(t.b(lag), 1)].rearrange("o (t p) d -> p (o t) d", p=P)).then_inc(s_ctx, 16)

            for b in range(2):
                load_ctx(Turn(b), 0)
            with sp.Fori(2, B) as b:
                load_ctx(Turn(b, 2), 0)

        @block.gpsimd
        def _(pool):
            for k in "xc":
                pool.memset(qs[k][:], 0.0)
                pool.memset(ks[k][:], 0.0)
                pool.memset(v1[k][:], 0.0).then_inc(s_set, 1)
            pool.wait_ge(s_set, 2)
            for k in "xc":
                pool.memset(qs[k][:, :, :, 48:52], 1.0)
                pool.memset(ks[k][:, :, :, 52:55], 1.0)
                pool.memset(v1[k][:, :, :, DH:DH + 1], 1.0)
            pool.memset(halfneg[:], -0.5).then_inc(s_set, 1)
            pool.wait_ge(s_set, 3)
            def x_norm(t, lag):
                r = rs["x"]
                passed(pool, XD0, "aggr", t, lag)
                pool.tensor_scalar(r[:, 0, :], mv["x"][:, :, 1], EPS, None, ALU.add).then_inc(XP0.sem, 1)
                passed(pool, XP0, "veps", t, lag)
                pool.tensor_tensor(r[:, 1, :], r[:, 0, :], halfneg[:], ALU.pow).then_inc(XP0.sem, 1)
                passed(pool, XP0, "rstd", t, lag)
                pool.tensor_tensor(r[:, 2, :], r[:, 1, :], any4[:, bass.ds(t.b(lag), 1)].broadcast_to((P, QT)), ALU.mult).then_inc(XP0.sem, 1)

            def split_copies(k, t, lag, order):
                for w in order:
                    if w == "k":
                        passed(pool, ACT_SPLIT[k], "khi", t, lag)
                        pool.tensor_copy(ks[k][:, :, :, DH:2 * DH], ks[k][:, :, :, 0:DH]).then_inc(POOL_SPLIT[k].sem, 1)
                    else:
                        passed(pool, ACT_SPLIT[k], "qhi", t, lag)
                        pool.tensor_copy(qs[k][:, :, :, 2 * DH:3 * DH], qs[k][:, :, :, 0:DH]).then_inc(POOL_SPLIT[k].sem, 1)

            def x_kext(t, lag):
                src = kext[:, bass.ds(t.b(lag), 1), :, :]
                for tt in range(QT):
                    last = pool.tensor_copy(ks["x"][:, tt, :, 48:52], src[:, :, tt, :].broadcast_to((P, H, 4)))
                last.then_inc(XP0.sem, 1)

            def x_v(t, lag):
                pool.wait_ge(s_ctx, (t.b(lag) + 1) * 16)
                products_done(pool, "x", t, lag, 1)
                pool.sem_inc(s_seen[pool.engine], 1)
                pool.tensor_copy(v1["x"][:, :, :, 0:DH],
                                 ctxb[:, :, D:DC].rearrange("p t (h d) -> p t h d", h=H)).then_inc(XP1.sem, 1)

            def x_sum(t, lag):
                t_wait_read(pool, t, "x_back1", lag)
                pool.tensor_tensor(res[:, TOK(t, lag), :], res[:, TOK(t, lag), :], att["x"][:], ALU.add).then_inc(XP1.sem, 1)

            def c_norm(t, lag):
                r, v = rs["c"], mv["c"][:, :, 1]
                passed(pool, CD1, "aggr", t, lag)
                pool.tensor_scalar(r[:, 0, :], v, EPS, None, ALU.add).then_inc(CP1.sem, 1)
                passed(pool, CP1, "veps", t, lag)
                pool.tensor_tensor(r[:, 1, :], r[:, 0, :], halfneg[:], ALU.pow).then_inc(CP1.sem, 1)
                passed(pool, CP1, "r1", t, lag)
                pool.tensor_tensor(r[:, 2, :], r[:, 1, :], r[:, 1, :], ALU.mult).then_inc(CP1.sem, 1)
                passed(pool, CP1, "r1sq", t, lag)
                pool.tensor_tensor(r[:, 3, :], r[:, 2, :], v, ALU.mult).then_inc(CP1.sem, 1)
                passed(pool, CP1, "v2", t, lag)
                pool.tensor_scalar(r[:, 4, :], r[:, 3, :], EPS, None, ALU.add).then_inc(CP1.sem, 1)
                passed(pool, CP1, "v2eps", t, lag)
                pool.tensor_tensor(r[:, 5, :], r[:, 4, :], halfneg[:], ALU.pow).then_inc(CP1.sem, 1)
                passed(pool, CP1, "r2", t, lag)
                pool.tensor_tensor(r[:, 6, :], r[:, 5, :], r[:, 1, :], ALU.mult).then_inc(CP1.sem, 1)

            def c_norm2(t, lag):
                passed(pool, CD2, "aggr2", t, lag)
                pool.tensor_scalar(rs2[:, 0, :], mv2[:, :, 1], EPS, None, ALU.add).then_inc(CP2.sem, 1)
                passed(pool, CP2, "veps2", t, lag)
                pool.tensor_tensor(rs2[:, 1, :], rs2[:, 0, :], halfneg[:], ALU.pow).then_inc(CP2.sem, 1)

            def c_sum(t, lag):
                t_wait_read(pool, t, "c_wo", lag)
                pool.tensor_tensor(res[:, TOK(t, lag), :], res[:, TOK(t, lag), :], xp[:], ALU.add).then_inc(CP2.sem, 1)

            def turn(t):
                if t.on(0):
                    x_v(t, 0)
                if t.on(1):
                    c_norm(t, 1)
                    split_copies("c", t, 1, "kq")
                if t.on(-1):
                    x_norm(t, -1)
                    split_copies("x", t, -1, "kq")
                    x_kext(t, -1)
                if t.on(2):
                    c_norm2(t, 2)
                    c_sum(t, 2)
                if t.on(0):
                    x_sum(t, 0)

            run_turns(pool, turn, lambda t: (x_norm(t, 0), split_copies("x", t, 0, "kq"), x_kext(t, 0)))

        @block.scalar
        def _(act):
            act.wait_ge(s_set, 3)

            def split_hi(k, t, lag, which):
                if which == "k":
                    if k == "x":
                        act.wait_ge(s_ctx, (t.b(lag) + 1) * 16)
                    else:
                        t_wait_read(act, t, "c_qk1", lag)
                    t_wait_full(act, t, f"{k}_kt1", lag, 1)
                    src = ctxb[:, :, 0:D] if k == "x" else kf[:]
                    act.activation(ks[k][:, :, :, 0:DH], src.rearrange("p t (h d) -> p t h d", h=H), ACT.Copy).then_inc(ACT_SPLIT[k].sem, 1)
                else:
                    if k == "x":
                        passed(act, XD0, "q", t, lag)
                    else:
                        t_wait_read(act, t, "c_qk1", lag)
                    t_wait_full(act, t, f"{k}_m1", lag, 1)
                    act.activation(qs[k][:, :, :, 0:DH], qf[k][:].rearrange("p t (h d) -> p t h d", h=H), ACT.Copy).then_inc(ACT_SPLIT[k].sem, 1)

            def evac_pairs(dst, t, name, lag, half):
                t_wait_full(act, t, name, lag)
                act.activation(dst[:, 4 * half:4 * half + 4, :].rearrange("p g s -> p (g s)"),
                               tb[bank_of[name]][:].bitcast(BF16), ACT.Copy).then_inc(t_free[bank_of[name]], 1)

            def exps(k, t, lag, n):
                kk, c = n % 2, ring(S2_TAB, t, k, lag, n)
                act.wait_ge(s2_full, c + 1)
                wait(act, p_free, c + 1 - NPT)
                lo = P if k == "c" and kk else 0
                act.activation(prob[:, n % NPT, :, lo:S], s2[n % 2][:, :, lo:S], ACT.Exp).then_inc(p_full, 1)

            def o_evac(k, t, lag):
                products_done(act, k, t, lag)
                t_wait_full(act, t, f"{k}_back1", lag, 1)
                for n in range(2):
                    last = act.activation(ot[k][:, 2 * n:2 * n + 2, :], ob[:, 2 * n:2 * n + 2, :], ACT.Copy)
                last.then_inc(o_free, 1)

            def c_qk(t, lag, tt):
                name = f"c_qk{tt}"
                t_wait_full(act, t, name, lag)
                if tt == 0:
                    passed(act, CD1, "qlo", t, lag, 1)
                act.activation(qf["c"][:, tt, :], tb[bank_of[name]][:, 0:D], ACT.Copy, scale=DH ** -0.5)
                act.activation(kf[:, tt, :], tb[bank_of[name]][:, D:2 * D], ACT.Copy).then_inc(t_free[bank_of[name]], 1)

            def c_at(t, lag):
                t_wait_full(act, t, "c_at", lag)
                act.activation(at[:].rearrange("p k s -> p (k s)"), tb[bank_of["c_at"]][:], ACT.Copy).then_inc(t_free[bank_of["c_at"]], 1)

            def c_nhi(t, lag):
                t_wait_read(act, t, "c_nt", lag)
                act.activation(nxh[:, :, bass.ds(t.b(lag) * S, S)], n2[:], ACT.Copy).then_inc(CA2.sem, 1)

            def c_gate(t, lag):
                t_wait_full(act, t, "c_gate", lag)
                act.activation(logits[:, TOK(t, lag), :], tb[bank_of["c_gate"]][:, 0:QT * E].rearrange("p (t e) -> p t e", e=E),
                               ACT.Copy).then_inc(t_free[bank_of["c_gate"]], 1)

            def turn(t):
                x, c1, c2, x_next = t.on(0), t.on(1), t.on(2), t.loop or 0 <= t.i + 1 < B
                if x:
                    evac_pairs(kt["x"], t, "x_kt1", 0, 1)
                    evac_pairs(qt["x"], t, "x_qt1", 0, 1)
                if c2:
                    evac_pairs(qt["c"], t, "c_m1", 2, 1)
                for n in range(STEPS):
                    if c2:
                        exps("c", t, 2, n)
                    if c1 and n == 9:
                        c_qk(t, 1, 0)
                if c2:
                    o_evac("c", t, 2)
                if c1:
                    c_qk(t, 1, 1)
                    split_hi("c", t, 1, "k")
                    split_hi("c", t, 1, "q")
                    evac_pairs(kt["c"], t, "c_kt1", 1, 1)
                    evac_pairs(qt["c"], t, "c_qt1", 1, 1)
                if x:
                    evac_pairs(qt["x"], t, "x_m1", 0, 1)
                for n in range(STEPS):
                    if x:
                        exps("x", t, 0, n)
                    if x_next and n == 5:
                        split_hi("x", t, -1, "k")
                    if x_next and n == 7:
                        split_hi("x", t, -1, "q")
                    if c2 and n == 6:
                        c_at(t, 2)
                if x:
                    o_evac("x", t, 0)
                if c2:
                    c_nhi(t, 2)
                    c_gate(t, 2)

            run_turns(act, turn, lambda t: (split_hi("x", t, 0, "k"), split_hi("x", t, 0, "q")))

        @block.vector
        def _(v):
            v.wait_ge(s_set, 3)

            def stats(k, t, lag):
                for tt in range(QT):
                    last = v.bn_stats(st[k][:, tt, :], res[:, bass.ds(t.b(lag) * QT + tt, 1), :].rearrange("p o d -> p (o d)"))
                last.then_inc(DVE_SPLIT[k].sem, 1)
                passed(v, DVE_SPLIT[k], "stats", t, lag)
                for tt in range(QT):
                    last = v.bn_aggr(mv[k][:, tt, :], st[k][:, tt, :])
                last.then_inc(DVE_SPLIT[k].sem, 1)

            def x_q(t, lag):
                passed(v, XP0, "rq", t, lag)
                passed(v, XA0, "qhi", t, lag, 1)
                for tt in range(QT):
                    last = v.tensor_scalar(qf["x"][:, tt, :], res[:, bass.ds(t.b(lag) * QT + tt, 1), :], mv["x"][:, tt, 0:1],
                                           rs["x"][:, 2, tt:tt + 1], ALU.subtract, ALU.mult)
                last.then_inc(XD0.sem, 1)

            def split_lo(k, t, lag, which):
                if which == "k":
                    passed(v, ACT_SPLIT[k], "khi", t, lag)
                    src = ctxb[:, :, 0:D] if k == "x" else kf[:]
                    v.tensor_tensor(ks[k][:, :, :, 2 * DH:3 * DH], src.rearrange("p t (h d) -> p t h d", h=H),
                                    ks[k][:, :, :, 0:DH], ALU.subtract).then_inc(DVE_SPLIT[k].sem, 1)
                else:
                    passed(v, ACT_SPLIT[k], "qhi", t, lag)
                    v.tensor_tensor(qs[k][:, :, :, DH:2 * DH], qf[k][:].rearrange("p t (h d) -> p t h d", h=H),
                                    qs[k][:, :, :, 0:DH], ALU.subtract).then_inc(DVE_SPLIT[k].sem, 1)

            def evac_pairs(dst, t, name, lag, half):
                t_wait_full(v, t, name, lag)
                v.tensor_copy(dst[:, 4 * half:4 * half + 4, :].rearrange("p g s -> p (g s)"),
                              tb[bank_of[name]][:].bitcast(BF16)).then_inc(t_free[bank_of[name]], 1)

            def maxes(k, t, lag, n):
                qq, g = n // GROUPS, n % GROUPS
                v.wait_ge(s1_full, ring(S1_TAB, t, k, lag, n) + 1)
                keys = P if k == "c" and qq == 0 else S
                h0 = heads(g)[0]
                v.tensor_reduce(negm[k][:, qq, h0:h0 + 3:2], s1[n % 2][:, :, 0:keys], AX.X, ALU.max, negate=True).then_inc(s1_free, 1)

            def max_parts(k, t, lag):
                steps = DVE_MAX[k]
                hi, mid, lo = (qs[k][:, :, :, 52 + n] for n in range(3))
                v.wait_ge(s1_free, ring(S1_TAB, t, k, lag, STEPS - 1) + 1)
                v.tensor_copy(hi, negm[k][:]).then_inc(steps.sem, 1)
                passed(v, steps, "m_hi", t, lag)
                v.tensor_tensor(mres[k][:], negm[k][:], hi, ALU.subtract).then_inc(steps.sem, 1)
                passed(v, steps, "m_res", t, lag)
                v.tensor_copy(mid, mres[k][:]).then_inc(steps.sem, 1)
                passed(v, steps, "m_mid", t, lag)
                v.tensor_tensor(lo, mres[k][:], mid, ALU.subtract).then_inc(steps.sem, 1)

            def normalize(k, t, lag):
                for qq in range(QT):
                    name = f"{k}_back{qq}"
                    t_wait_full(v, t, name, lag)
                    if qq == 0 and k == "x":
                        passed(v, XP1, "x1", t, lag, 1)
                    view = tb[bank_of[name]][:].rearrange("p (h d) -> p h d", d=32)
                    v.reciprocal(rden[k][:, qq, :], view[:, :, DH]).then_inc(DVE_OUT[k].sem, 1)
                    passed(v, DVE_OUT[k], f"rec{qq}", t, lag)
                    v.tensor_tensor(att[k][:, qq, :].rearrange("p (h d) -> p h d", h=H), view[:, :, 0:DH],
                                    rden[k][:, qq, :].unsqueeze(2).broadcast_to((P, H, DH)), ALU.mult).then_inc(t_free[bank_of[name]], 1)

            def c_stats(t, lag):
                passed(v, XP1, "x1", t, lag)
                stats("c", t, lag)

            def c_xin(t, lag):
                passed(v, CP1, "r12", t, lag)
                for dst, r in ((xin[:, parity(t.b(lag))], 1), (xh[:].unsqueeze(1), 6)):
                    for tt in range(QT):
                        last = v.tensor_scalar(dst[:, :, tt, :], res[:, bass.ds(t.b(lag) * QT + tt, 1), :], mv["c"][:, tt, 0:1],
                                               rs["c"][:, r, tt:tt + 1], ALU.subtract, ALU.mult)
                    last.then_inc(CD1.sem, 1)

            def weigh(name, dst, w, t, lag):
                t_wait_full(v, t, name, lag)
                if name == "c_nt":
                    t_wait_full(v, t, "c_gate", lag, 1)
                src = tb[bank_of[name]][:].rearrange("p (k s) -> p k s", k=KD)
                for k in range(KD):
                    last = v.tensor_scalar(dst[:, k, :], src[:, k, :], lncol[:, w, k:k + 1], lncol[:, w + 1, k:k + 1], ALU.mult, ALU.add)
                last.then_inc(t_free[bank_of[name]], 1)

            def c_v(t, lag):
                t_wait_full(v, t, "c_v", lag)
                products_done(v, "c", t, lag, 1)
                v.tensor_copy(v1["c"][:, :, :, 0:DH], tb[bank_of["c_v"]][:].rearrange("p (t h d) -> p t h d", t=QT, h=H))\
                    .then_inc(t_free[bank_of["c_v"]], 1)

            def c_xp(t, lag):
                t_wait_full(v, t, "c_wo", lag)
                passed(v, CP2, "x2", t, lag, 1)
                v.tensor_tensor(xp[:].rearrange("p t d -> p (t d)").unsqueeze(1), tb[bank_of["c_wo"]][:].unsqueeze(1),
                                xin[:, parity(t.b(lag))].rearrange("p o t d -> p o (t d)"), ALU.add).then_inc(t_free[bank_of["c_wo"]], 1)
                t_wait_read(v, t, "c_wo", lag)
                for tt in range(QT):
                    last = v.bn_stats(st2[:, tt, :], xp[:, tt, :])
                last.then_inc(CD2.sem, 1)
                passed(v, CD2, "stats2", t, lag)
                for tt in range(QT):
                    last = v.bn_aggr(mv2[:, tt, :], st2[:, tt, :])
                last.then_inc(CD2.sem, 1)

            def c_xh2(t, lag):
                passed(v, CP2, "rstd2", t, lag)
                for tt in range(QT):
                    last = v.tensor_scalar(xh2[:, tt, :], xp[:, tt, :], mv2[:, tt, 0:1], rs2[:, 1, tt:tt + 1], ALU.subtract, ALU.mult)
                last.then_inc(CD2.sem, 1)

            def c_nlo(t, lag):
                passed(v, CA2, "nhi", t, lag)
                cols = bass.ds(t.b(lag) * S, S)
                v.tensor_tensor(nxl[:, :, cols], n2[:], nxh[:, :, cols], ALU.subtract).then_inc(CD2.sem, 1)

            def turn(t):
                x, c1, c2, x_next = t.on(0), t.on(1), t.on(2), t.loop or 0 <= t.i + 1 < B
                if x:
                    evac_pairs(kt["x"], t, "x_kt0", 0, 0)
                    evac_pairs(qt["x"], t, "x_qt0", 0, 0)
                if c2:
                    evac_pairs(qt["c"], t, "c_m0", 2, 0)
                if c1:
                    c_stats(t, 1)
                for n in range(STEPS):
                    if x:
                        maxes("x", t, 0, n)
                    if c1 and n == 4:
                        c_xin(t, 1)
                    if c1 and n == 7:
                        weigh("c_xt", nxt, 0, t, 1)
                if x:
                    max_parts("x", t, 0)
                if c1:
                    c_v(t, 1)
                    split_lo("c", t, 1, "k")
                    split_lo("c", t, 1, "q")
                    evac_pairs(kt["c"], t, "c_kt0", 1, 0)
                    evac_pairs(qt["c"], t, "c_qt0", 1, 0)
                if x:
                    evac_pairs(qt["x"], t, "x_m0", 0, 0)
                for n in range(STEPS):
                    if c1:
                        maxes("c", t, 1, n)
                    if x_next and n == 0:
                        stats("x", t, -1)
                    if c2 and n == 2:
                        normalize("c", t, 2)
                    if x_next and n == 4:
                        x_q(t, -1)
                    if x_next and n == 9:
                        split_lo("x", t, -1, "k")
                        split_lo("x", t, -1, "q")
                    if c2 and n == 10:
                        c_xp(t, 2)
                    if c2 and n == 13:
                        c_xh2(t, 2)
                if c1:
                    max_parts("c", t, 1)
                if c2:
                    weigh("c_nt", n2, 2, t, 2)
                    c_nlo(t, 2)
                if x:
                    normalize("x", t, 0)

            run_turns(v, turn, lambda t: (stats("x", t, 0), x_q(t, 0), split_lo("x", t, 0, "k"), split_lo("x", t, 0, "q")))

        @block.tensor
        def _(pe):
            idb = cb[:, CB_ID:CB_ID + P]
            idf = cf[:, CF_ID:CF_ID + P]
            ones3 = cb[0:3, CB_ONE:CB_ONE + P]
            pe.wait_ge(s_load, 16 * n_load)
            pe.wait_ge(s_set, 3)

            def pairs(src, t, name, lag, half, waits):
                waits()
                t_wait_free(pe, t, name, lag)
                dst = tb[bank_of[name]][:].bitcast(BF16).rearrange("p (g s) -> p g s", g=4)
                for g in range(4):
                    for tt in range(QT):
                        pair = 4 * half + g
                        last = pe.transpose(dst[:, g, tt * P:(tt + 1) * P],
                                            src[:, tt, 2 * pair:2 * pair + 2, :].rearrange("p h r -> p (h r)"), idb)
                last.then_inc(t_full[bank_of[name]], 1)

            def k_pairs(k, t, lag):
                passed(pe, DVE_SPLIT[k], "klo", t, lag)
                passed(pe, POOL_SPLIT[k], "kext" if k == "x" else "khi2", t, lag)
                for half in range(2):
                    pairs(ks[k], t, f"{k}_kt{half}", lag, half, lambda: None)

            def q_pairs(k, t, lag):
                passed(pe, DVE_SPLIT[k], "qlo", t, lag)
                passed(pe, POOL_SPLIT[k], "qhi2", t, lag)
                for half in range(2):
                    pairs(qs[k], t, f"{k}_qt{half}", lag, half, lambda: None)

            def m_pairs(k, t, lag):
                passed(pe, DVE_MAX[k], "m_lo", t, lag)
                for half in range(2):
                    pairs(qs[k], t, f"{k}_m{half}", lag, half, lambda: None)

            def s1_step(k, t, lag, n):
                qq, g = n // GROUPS, n % GROUPS
                c = ring(S1_TAB, t, k, lag, n)
                if n == 0:
                    for w in ("qt0", "qt1"):
                        t_wait_read(pe, t, f"{k}_{w}", lag)
                wait(pe, s1_free, c - 1)
                out = s1[n % 2]
                r0 = HB * (g % 2)
                if k == "c":
                    cols = slice(qq * P, (qq + 1) * P)
                    pe.matmul(out[:, :, cols], idb, cb[:, CB_MQ:CB_MQ + 2 * P].rearrange("p (h s) -> p h s", h=2), start=True, stop=False)
                for j, h in enumerate(heads(g)):
                    q = qt[k][r0:r0 + 52, h // 2, qq * P:(qq + 1) * P]
                    for kk in range(QT):
                        if k == "c" and kk > qq:
                            continue
                        ks_ = slice(kk * P, (kk + 1) * P)
                        if k == "x":
                            if kk == 0:
                                last = pe.matmul(out[:, j, :], q, kt[k][r0:r0 + 52, h // 2, :], start=True, stop=True)
                        else:
                            last = pe.matmul(out[:, j, ks_], q, kt[k][r0:r0 + 52, h // 2, ks_], start=False, stop=j == 1 and kk == qq)
                last.then_inc(s1_full, 1)

            def s2_step(k, t, lag, n):
                g, kk = n // 2, n % 2
                c = ring(S2_TAB, t, k, lag, n)
                if n == 0:
                    t_wait_read(pe, t, f"{k}_m0", lag)
                    t_wait_read(pe, t, f"{k}_m1", lag)
                wait(pe, p_full, c - 1)
                out = s2[n % 2]
                r0 = HB * (g % 2)
                if k == "c":
                    pe.matmul(out[:, :, kk * P:(kk + 1) * P], idb, cb[:, CB_MK:CB_MK + 2 * P].rearrange("p (h s) -> p h s", h=2),
                              start=True, stop=False)
                for j, h in enumerate(heads(g)):
                    key = kt[k][r0:r0 + HB, h // 2, kk * P:(kk + 1) * P]
                    if k == "x":
                        last = pe.matmul(out[:, j, :], key, qt[k][r0:r0 + HB, h // 2, :], start=True, stop=True)
                    else:
                        for qq in range(kk, QT):
                            qs_ = slice(qq * P, (qq + 1) * P)
                            last = pe.matmul(out[:, j, qs_], key, qt[k][r0:r0 + HB, h // 2, qs_], start=False, stop=j == 1 and qq == QT - 1)
                last.then_inc(s2_full, 1)

            def pv_step(k, t, lag, n):
                g, kk = n // 2, n % 2
                c = ring(S2_TAB, t, k, lag, n)
                pe.wait_ge(p_full, c + 1)
                if n == 0:
                    if k == "x":
                        passed(pe, XP1, "v", t, lag)
                    else:
                        t_wait_read(pe, t, "c_v", lag)
                    wait(pe, o_free, o_count(t, k, lag))
                lo = P if k == "c" and kk else 0
                for j, h in enumerate(heads(g)):
                    col = 32 * (h % 4)
                    last = pe.matmul(ob[col:col + 32, h // 4, lo:S], v1[k][:, kk, h, :], prob[:, n % NPT, j, lo:S],
                                     start=kk == 0, stop=kk == 1)
                last.then_inc(p_free, 1)

            def back(k, t, lag):
                pe.wait_ge(o_free, o_count(t, k, lag) + 1)
                for qq in range(QT):
                    name = f"{k}_back{qq}"
                    t_wait_free(pe, t, name, lag)
                    for j in range(4):
                        last = pe.transpose(tb[bank_of[name]][:, j * P:(j + 1) * P], ot[k][:, j, qq * P:(qq + 1) * P], idf)
                    last.then_inc(t_full[bank_of[name]], 1)

            def turn_over(src, t, name, lag, waits):
                waits()
                t_wait_free(pe, t, name, lag)
                for k in range(KD):
                    for tt in range(QT):
                        last = pe.transpose(tb[bank_of[name]][:, k * S + tt * P:k * S + (tt + 1) * P], src[:, tt, k * P:(k + 1) * P], idf)
                last.then_inc(t_full[bank_of[name]], 1)

            def project(t, name, lag, out, lhs, w, tt, lo, n, row):
                for k in range(KD):
                    pe.matmul(out, lhs[:, k, tt * P:(tt + 1) * P], w[:, k, lo:lo + n], start=k == 0, stop=False)
                return pe.matmul(out, ones3, rows[:, row:row + n], start=False, stop=True)

            def c_qk(t, lag, tt):
                name = f"c_qk{tt}"
                if tt == 0:
                    t_wait_read(pe, t, "c_xt", lag)
                t_wait_free(pe, t, name, lag)
                project(t, name, lag, tb[bank_of[name]][:, 0:2 * D], nxt, wqkv, tt, 0, 2 * D, RW_QKV).then_inc(t_full[bank_of[name]], 1)

            def c_v(t, lag):
                t_wait_free(pe, t, "c_v", lag)
                for tt in range(QT):
                    last = project(t, "c_v", lag, tb[bank_of["c_v"]][:, tt * D:(tt + 1) * D], nxt, wqkv, tt, 2 * D, D, RW_QKV + 2 * D)
                last.then_inc(t_full[bank_of["c_v"]], 1)

            def c_wo(t, lag):
                t_wait_read(pe, t, "c_at", lag)
                t_wait_free(pe, t, "c_wo", lag)
                for tt in range(QT):
                    last = project(t, "c_wo", lag, tb[bank_of["c_wo"]][:, tt * D:(tt + 1) * D], at, wo, tt, 0, D, RW_O)
                last.then_inc(t_full[bank_of["c_wo"]], 1)

            def c_gate(t, lag):
                t_wait_read(pe, t, "c_nt", lag)
                t_wait_free(pe, t, "c_gate", lag)
                for tt in range(QT):
                    for k in range(KD):
                        last = pe.matmul(tb[bank_of["c_gate"]][:, tt * E:(tt + 1) * E], n2[:, k, tt * P:(tt + 1) * P], wgate[:, k, :],
                                         start=k == 0, stop=k == KD - 1)
                last.then_inc(t_full[bank_of["c_gate"]], 1)

            def turn(t):
                x, c1, c2 = t.on(0), t.on(1), t.on(2)
                if x:
                    k_pairs("x", t, 0)
                    q_pairs("x", t, 0)
                if c2:
                    m_pairs("c", t, 2)
                for n in range(STEPS):
                    if x:
                        s1_step("x", t, 0, n)
                    if c2:
                        s2_step("c", t, 2, n)
                        if n >= 1:
                            pv_step("c", t, 2, n - 1)
                    if c1 and n == 6:
                        turn_over(xh, t, "c_xt", 1, lambda: passed(pe, CD1, "xh", t, 1))
                    if c1 and n == 9:
                        c_qk(t, 1, 0)
                if c2:
                    pv_step("c", t, 2, STEPS - 1)
                if c1:
                    c_v(t, 1)
                    c_qk(t, 1, 1)
                    k_pairs("c", t, 1)
                    q_pairs("c", t, 1)
                if x:
                    m_pairs("x", t, 0)
                for n in range(STEPS):
                    if c1:
                        s1_step("c", t, 1, n)
                    if x:
                        s2_step("x", t, 0, n)
                        if n >= 1:
                            pv_step("x", t, 0, n - 1)
                    if c2 and n == 1:
                        back("c", t, 2)
                    if c2 and n == 5:
                        turn_over(att["c"], t, "c_at", 2, lambda: (t_wait_read(pe, t, "c_back1", 2), t_wait_read(pe, t, "c_back0", 2)))
                    if c2 and n == 8:
                        c_wo(t, 2)
                if x:
                    pv_step("x", t, 0, STEPS - 1)
                if c2:
                    turn_over(xh2, t, "c_nt", 2, lambda: passed(pe, CD2, "xh2", t, 2))
                    c_gate(t, 2)
                if x:
                    back("x", t, 0)

            run_turns(pe, turn, lambda t: None)


def run_turns(eng, turn, first):
    first(Turn(0))
    for i in range(3):
        turn(Turn(i))
    with eng.Fori(3, B - 1) as i:
        turn(Turn(i, 3))
    for i in range(B - 1, B + 2):
        turn(Turn(i))


def setup_phase(nc, io, keep, sem):
    cf, cb, rows, res = keep["cf"], keep["cb"], keep["rows"], keep["res"]
    kext, any4, kq, bounds = keep["kext"], keep["any4"], keep["kq"], keep["bounds"]
    with ExitStack() as ctx:
        def sb(name, shape, dt=F32):
            return ctx.enter_context(nc.sbuf_tensor(name, shape, dt))

        rows_f, rows_r = sb("rows_f", [3, RW_N]), sb("rows_r", [3, RW_N])
        rows_m = sb("rows_m", [3, RW_N], BF16)
        seq_i, seq_f = sb("seq_i", [P, B], I32), sb("seq_f", [P, B])
        any_f = sb("any_f", [P, B])
        bcol, bpf, bres = sb("bcol", [P, QT]), sb("bpf", [P, 3, QT]), sb("bres", [P, QT])
        bpart = sb("bpart", [P, 3, QT], BF16)
        msk = sb("msk", [P, QT, B])
        scales = sb("scales", [P, 2])
        rscale = sb("rscale", [P, 2])
        kw = sb("kw", [P, KD, D], BF16)
        kwf, kexp, kbig, ksum = sb("kwf", [P, KD, D]), sb("kexp", [P, KD, D]), sb("kbig", [P, KD, D]), sb("ksum", [P, KD, D])
        len_i, len_f = sb("len_i", [P, QT, B], I32), sb("len_f", [P, QT, B])
        ginit = sb("ginit", [P, D])
        ends = ctx.enter_context(nc.psum_tensor("ends", [P, QT, B], F32))
        s_load, s_dve, s_ends = sem("setup_load"), sem("setup_dve"), sem("setup_ends")
        loads = (
            (cf[:], io["cf"]), (cb[:], io["cb"]),
            (rows_f[:], io["rows"]), (seq_i[:], io["seq"].partition_broadcast(P)),
            (bcol[:], io["b"]),
            (scales[:, 0:1], io["s_in"].partition_broadcast(P)), (scales[:, 1:2], io["s_k"].partition_broadcast(P)),
            (kw[:], io["kern"].rearrange("(k p) n -> p k n", p=P)),
            (len_i[:], io["lens"]),
            (ginit[:], io["ginit"].partition_broadcast(P)),
            (keep["bias"][:], io["bias"].partition_broadcast(P)),
            (keep["lncol"][:], io["lncol"]),
            (res[:], io["x"].rearrange("b (t p) d -> p (b t) d", p=P)),
        )
        block = ctx.enter_context(nc.Block())

        @block.sync
        def _(sp):
            for dst, src in loads:
                sp.dma_start(dst, src).then_inc(s_load, 16)
            sp.wait_ge(s_load, 16 * len(loads))

        @block.tensor
        def _(pe):
            pe.wait_ge(s_dve, 1)
            tri, one = cf[:, CF_TRI:CF_TRI + P], cf[:, CF_ONE:CF_ONE + P]
            pe.matmul(ends[:, 0, :], tri, len_f[:, 0, :], start=True, stop=True)
            pe.matmul(ends[:, 1, :], one, len_f[:, 0, :], start=True, stop=False)
            pe.matmul(ends[:, 1, :], tri, len_f[:, 1, :], start=False, stop=True).then_inc(s_ends, 1)

        @block.vector
        def _(v):
            count = [0]

            def after(ins):
                count[0] += 1
                ins.then_inc(s_dve, 1)
                v.wait_ge(s_dve, count[0])

            v.wait_ge(s_load, 16 * len(loads))
            after(v.tensor_copy(len_f[:], len_i[:]))
            after(v.tensor_copy(seq_f[:], seq_i[:]))
            after(v.tensor_scalar(any4[:], seq_f[:], 0.0, DH ** -0.5, ALU.is_gt, ALU.mult))
            after(v.tensor_scalar(any_f[:], seq_f[:], 0.0, None, ALU.is_gt))
            after(v.tensor_copy(bpart[:, 0, :], bcol[:]))
            after(v.tensor_tensor(bres[:], bcol[:], bpart[:, 0, :], ALU.subtract))
            after(v.tensor_copy(bpart[:, 1, :], bres[:]))
            after(v.tensor_tensor(bpart[:, 2, :], bres[:], bpart[:, 1, :], ALU.subtract))
            after(v.tensor_copy(bpf[:], bpart[:]))
            for tt in range(QT):
                after(v.tensor_scalar(msk[:, tt, :], seq_f[:], cf[:, CF_ROW + tt:CF_ROW + tt + 1], NEG_BIG, ALU.is_le, ALU.mult))
                for part in range(3):
                    after(v.tensor_scalar(kext[:, :, tt, part], any_f[:], bpf[:, part, tt:tt + 1], None, ALU.mult))
                after(v.tensor_tensor(kext[:, :, tt, 3], msk[:, tt, :], any_f[:], ALU.mult))
            sel = [cf[0:3, CF_ID + p:CF_ID + p + 1] for p in range(3)]
            after(v.tensor_copy(rows_m[:], rows_f[:]))
            after(v.tensor_scalar(rows[:], rows_m[:], sel[0], None, ALU.mult))
            after(v.tensor_tensor(rows_r[:], rows_f[:], rows_m[:], ALU.subtract))
            after(v.tensor_copy(rows_m[:], rows_r[:]))
            after(v.scalar_tensor_tensor(out=rows[:], in0=rows_m[:], scalar=sel[1], in1=rows[:], op0=ALU.mult, op1=ALU.add))
            after(v.tensor_tensor(rows_r[:], rows_r[:], rows_m[:], ALU.subtract))
            after(v.scalar_tensor_tensor(out=rows[:], in0=rows_r[:], scalar=sel[2], in1=rows[:], op0=ALU.mult, op1=ALU.add))
            after(v.reciprocal(rscale[:], scales[:]))
            after(v.tensor_copy(keep["r_in"][:], rscale[:, 0:1]))
            after(v.tensor_tensor(keep["s_out"][:], scales[:, 0:1], scales[:, 1:2], ALU.mult))
            after(v.tensor_scalar(kwf[:], kw[:], rscale[:, 1:2], None, ALU.mult))
            after(v.tensor_single_scalar(kexp[:].bitcast(I32), kwf[:].bitcast(I32), 0x7F800000, op=ALU.bitwise_and))
            after(v.tensor_scalar(kbig[:], kexp[:], 2.0 ** -6, C20, ALU.max, ALU.mult))
            after(v.tensor_tensor(ksum[:], kwf[:], kbig[:], ALU.add))
            after(v.tensor_tensor(kq[:], ksum[:], kbig[:], ALU.subtract))
            after(v.tensor_scalar(keep["ginit"][:], ginit[:], math.exp(-PATCH_EPS), None, ALU.mult))
            v.wait_ge(s_ends, 1)
            after(v.tensor_scalar(bounds[:, 0], ends[:], -1.0, None, ALU.add))
            after(v.tensor_scalar(bounds[:, 1], ends[:], -1.0 + S, None, ALU.add))


def expert_phase(nc, io, keep, sem):
    res, nxh, nxl, logits, cf, cb, rows = (keep[n] for n in ("res", "nxh", "nxl", "logits", "cf", "cb", "rows"))
    NH, NY = 4, TB // P
    with ExitStack() as ctx:
        def sb(name, shape, dt=F32):
            return ctx.enter_context(nc.sbuf_tensor(name, shape, dt))

        wf1, wf2 = sb("wf1", [P, KD, F]), sb("wf2", [P, FT, D])
        w1 = [sb(f"w1_{p}", [P, 2, KD, F], BF16) for p in "hl"]
        w2 = [sb(f"w2_{p}", [P, 2, FT, D], BF16) for p in "hl"]
        b1 = sb("b1", [P, E * FT])
        hf = sb("hf", [P, NH, TB])
        hid = [sb(f"hid_{p}", [P, FT, TB], BF16) for p in "hl"]
        top = sb("top", [P, NT, 8])
        idx = sb("idx", [P, NT, 8], U32)
        idf = sb("idf", [P, TOPK, NT])
        gap, eg, den, g1, g2 = (sb(n, [P, NT]) for n in ("gap", "eg", "den", "g1", "g2"))
        gates, gate_b = sb("gates", [P, NT * E]), sb("gate_b", [P, NT, E])
        hb = [ctx.enter_context(nc.psum_tensor(f"hb{n}", [P, TB], F32)) for n in range(NH)]
        yb = [ctx.enter_context(nc.psum_tensor(f"yb{n}", [P, 512], F32)) for n in range(NY)]

        s_b1, s_w, s_split, s_wfree = sem("b1_load"), sem("w_load"), sem("w_split"), sem("w_used")
        s_gate, s_eg = sem("gate_dve"), sem("gate_exp")
        s_h, s_gelu, s_hi, s_lo = sem("h_full"), sem("gelu"), sem("h_high"), sem("h_low")
        s_y, s_yread = sem("y_full"), sem("y_read")
        s_seen_pe, s_seen_pool = sem("e_seen_pe"), sem("e_seen_pool")
        block = ctx.enter_context(nc.Block())

        def wait(eng, s, value):
            if not isinstance(value, int) or value > 0:
                eng.wait_ge(s, value)

        def blocks(eng, body):
            body(0, 0, 0)
            with eng.Fori(1, NTB) as t:
                body(0, t, t)
            with eng.Fori(1, E) as e:
                with eng.Fori(0, NTB) as t:
                    body(e, t, e * NTB + t)

        @block.sync
        def _(sp):
            sp.dma_start(b1[:], io["fc1b"]).then_inc(s_b1, 16)

            def load(e):
                wait(sp, s_split, e * 4)
                sp.dma_start(wf1[:], io["fc1"][bass.ds(e, 1)].rearrange("o (k p) f -> p (o k) f", p=P)).then_inc(s_w, 16)
                sp.dma_start(wf2[:], io["fc2"][bass.ds(e, 1)].rearrange("o (k p) f -> p (o k) f", p=P)).then_inc(s_w, 16)

            load(0)
            with sp.Fori(1, E) as e:
                load(e)

        @block.gpsimd
        def _(pool):
            def split(e, peel):
                buf = bass.ds(e % 2, 1)
                pool.wait_ge(s_w, e * 32 + 32)
                if not peel:
                    pool.wait_ge(s_y, (e - 1) * NTB * NY)
                pool.sem_inc(s_seen_pool, 1)
                flat = lambda a: a.unsqueeze(1)
                pool.tensor_copy(w1[0][:, buf], flat(wf1[:])).then_inc(s_split, 1)
                pool.tensor_copy(w2[0][:, buf], flat(wf2[:])).then_inc(s_split, 1)
                pool.wait_ge(s_split, e * 4 + 1)
                pool.tensor_tensor(w1[1][:, buf], flat(wf1[:]), w1[0][:, buf], ALU.subtract).then_inc(s_split, 1)
                pool.wait_ge(s_split, e * 4 + 2)
                pool.tensor_tensor(w2[1][:, buf], flat(wf2[:]), w2[0][:, buf], ALU.subtract).then_inc(s_split, 1)

            split(0, True)
            split(1, True)
            with pool.Fori(2, E) as e:
                split(e, False)

        @block.scalar
        def _(act):
            act.wait_ge(s_gate, 2)
            act.activation(eg[:], gap[:], ACT.Exp).then_inc(s_eg, 1)
            act.wait_ge(s_b1, 16)

            def body(e, t, g):
                for f in range(FT):
                    act.wait_ge(s_h, g * FT + f + 1)
                    wait(act, s_lo, g * FT + f + 1 - NH)
                    act.activation(hf[:, f % NH, :], hb[f % NH][:], ACT.Gelu, bias=b1[:, bass.ds(e * FT + f, 1)]).then_inc(s_gelu, 1)

            blocks(act, body)

        @block.vector
        def _(v):
            for k in range(NT):
                last = v.max(top[:, k, :], logits[:, k, :])
            last.then_inc(s_gate, 1)
            v.wait_ge(s_gate, 1)
            v.tensor_tensor(gap[:], top[:, :, 1], top[:, :, 0], ALU.subtract).then_inc(s_gate, 1)
            for k in range(NT):
                last = v.max_index(idx[:, k, :], top[:, k, :], logits[:, k, :])
            last.then_inc(s_gate, 1)
            v.wait_ge(s_gate, 3)
            v.tensor_copy(idf[:], idx[:, :, 0:TOPK].rearrange("p t k -> p k t")).then_inc(s_gate, 1)
            v.wait_ge(s_eg, 1)
            v.tensor_scalar(den[:], eg[:], 1.0, None, ALU.add).then_inc(s_gate, 1)
            v.wait_ge(s_gate, 5)
            v.reciprocal(g1[:], den[:]).then_inc(s_gate, 1)
            v.wait_ge(s_gate, 6)
            v.tensor_tensor(g2[:], eg[:], g1[:], ALU.mult).then_inc(s_gate, 1)
            ga = gates[:].rearrange("p (t e) -> p t e", e=E)
            iota = cf[:, CF_IOTA:CF_IOTA + E].unsqueeze(1).broadcast_to((P, NT, E))
            spread = lambda a: a.unsqueeze(2).broadcast_to((P, NT, E))
            v.tensor_tensor(ga, iota, spread(idf[:, 0, :]), ALU.is_equal).then_inc(s_gate, 1)
            v.tensor_tensor(gate_b[:], iota, spread(idf[:, 1, :]), ALU.is_equal).then_inc(s_gate, 1)
            v.wait_ge(s_gate, 9)
            v.tensor_tensor(ga, ga, spread(g1[:]), ALU.mult).then_inc(s_gate, 1)
            v.tensor_tensor(gate_b[:], gate_b[:], spread(g2[:]), ALU.mult).then_inc(s_gate, 1)
            v.wait_ge(s_gate, 11)
            v.tensor_tensor(ga, ga, gate_b[:], ALU.add).then_inc(s_gate, 1)
            v.wait_ge(s_gate, 12)

            def body(e, t, g):
                wait(v, s_y, g * NY)
                for f in range(FT + 1):
                    if f < FT:
                        v.wait_ge(s_gelu, g * FT + f + 1)
                        v.tensor_copy(hid[0][:, f, :], hf[:, f % NH, :]).then_inc(s_hi, 1)
                    if f >= 1:
                        v.wait_ge(s_hi, g * FT + f)
                        v.tensor_tensor(hid[1][:, f - 1, :], hf[:, (f - 1) % NH, :], hid[0][:, f - 1, :], ALU.subtract).then_inc(s_lo, 1)
                for n in range(NY):
                    v.wait_ge(s_y, g * NY + n + 1)
                    tok = t * NY + n
                    rr = res[:, bass.ds(tok, 1), :].rearrange("p o d -> p (o d)")
                    v.scalar_tensor_tensor(out=rr, in0=yb[n][:, 0:D], scalar=gates[:, bass.ds(tok * E + e, 1)], in1=rr,
                                           op0=ALU.mult, op1=ALU.add).then_inc(s_yread, 1)

            blocks(v, body)

        @block.tensor
        def _(pe):
            ones3 = cb[0:3, CB_ONE:CB_ONE + P]

            def body(e, t, g):
                buf = bass.ds(e % 2, 1)
                pe.wait_ge(s_split, e * 4 + 4)
                tok = bass.ds(t * TB, TB)
                for f in range(FT):
                    wait(pe, s_gelu, g * FT + f + 1 - NH)
                    n = 0
                    for k in range(KD):
                        for wp, xpart in ((0, nxh), (0, nxl), (1, nxh)):
                            last = pe.matmul(hb[f % NH][:], w1[wp][:, buf, k, f * P:(f + 1) * P].rearrange("p o f -> p (o f)"),
                                             xpart[:, k, tok], start=n == 0, stop=n == 3 * KD - 1)
                            n += 1
                    last.then_inc(s_h, 1)
                for n in range(NY):
                    wait(pe, s_yread, g * NY + n + 1 - NY)
                    out = yb[n][:, 0:D]
                    pe.sem_inc(s_seen_pe, 1)
                    pe.matmul(out, ones3, rows[:, bass.ds(RW_FC2 + e * D, D)], start=True, stop=False)
                    for f in range(FT):
                        if n == 0:
                            pe.wait_ge(s_lo, g * FT + f + 1)
                        for hp, wp in ((0, 0), (0, 1), (1, 0)):
                            last = pe.matmul(out, hid[hp][:, f, n * P:(n + 1) * P],
                                             w2[wp][:, buf, f, :].rearrange("p o d -> p (o d)"), start=False, stop=f == FT - 1 and hp == 1)
                    last.then_inc(s_y, 1)

            blocks(pe, body)


def last_phase(nc, io, keep, sem):
    res, cf, cb, rows, bounds, kq, lncol = (keep[n] for n in ("res", "cf", "cb", "rows", "bounds", "kq", "lncol"))
    with ExitStack() as ctx:
        def sb(name, shape, dt=F32):
            return ctx.enter_context(nc.sbuf_tensor(name, shape, dt))

        win = sb("win", [P, KD, D])
        ones = sb("ones", [P, S])
        halfneg = sb("halfneg_c", [P, QT])
        cx, junk = sb("cx", [P, QT, DC]), sb("junk", [P, QT, DC])
        ss, ra = sb("ss", [P, QT]), sb("ra", [P, 2, QT])
        u = sb("u", [P, 2, QT, D])
        eq, bnd_in = sb("eq", [P, QT, S]), sb("bnd_in", [P, QT, S], BF16)
        bnd, cum, plug = sb("bnd", [P, S]), sb("cum", [P, S]), sb("plug", [P, S])
        take = sb("take", [P, QT, S])
        mt = sb("mt", [P, QT, S])
        sth, mvh, rh = sb("sth", [P, QT, 6]), sb("mvh", [P, QT, 2]), sb("rh", [P, 7, QT])
        xh, nt = sb("xh_c", [P, QT, D]), sb("nt", [P, KD, S])
        x3 = sb("x3", [P, 2, QT, D])
        stq, mvq, rq = sb("stq", [P, QT, 6]), sb("mvq", [P, QT, 2]), sb("rq", [P, 2, QT])
        xb = sb("xb", [P, QT, D], BF16)
        qv, qe, qb, qsum = (sb(n, [P, QT, D]) for n in ("qv", "qe", "qb", "qsum"))
        qq = sb("qq", [P, QT, D], BF16)
        qt = sb("qt", [P, KD, S], BF16)
        y, ybias = sb("y", [P, QT, D], BF16), sb("ybias", [P, QT, D], BF16)
        out = sb("out_t", [P, QT, D])
        p_cnt, p_mt, p_t, p_h, p_q, p_y = (ctx.enter_context(nc.psum_tensor(n, [P, 512], F32)) for n in ("p_cnt", "p_mt", "p_t", "p_h", "p_q", "p_y"))

        s_load, s_cx, s_set, s_out = sem("l_load"), sem("l_ctx"), sem("l_set"), sem("l_out")
        s_seen = {e.engine: sem(f"l_seen_{n}") for e, n in ((nc.gpsimd, "pool"), (nc.vector, "dve"))}
        AD = Steps(sem("a_dve"), "eq bound u bnd cum plug take")
        AP_ = Steps(sem("a_pool"), "ms rms")
        AA = Steps(sem("a_act"), "square mt")
        AE = Steps(sem("a_pe"), "cnt mt")
        HD = Steps(sem("h_dve"), "stats aggr xh nt x3")
        HP = Steps(sem("h_pool"), "veps r1 r1sq v2 v2eps r2 r12")
        HE = Steps(sem("h_pe"), "t h")
        QD = Steps(sem("q_dve"), "stats aggr xb v exp big sum q")
        QP = Steps(sem("q_pool"), "veps rstd bias out")
        QA = Steps(sem("q_act"), "qt y")
        QE = Steps(sem("q_pe"), "t y")

        def passed(eng, steps, name, t, lag, back=0):
            if t.ref - lag - back >= 0:
                eng.wait_ge(steps.sem, steps.at(name, t.b(lag) - back))
                if t.loop and (eng is nc.gpsimd or name == "stats"):
                    eng.sem_inc(s_seen[eng.engine], 1)

        def parity(b):
            return bass.ds(b % 2, 1)

        block = ctx.enter_context(nc.Block())

        @block.sync
        def _(sp):
            sp.dma_start(win[:], io["win"].rearrange("(k p) n -> p k n", p=P)).then_inc(s_load, 16)

            def turn(t):
                if t.on(0):
                    passed(sp, AD, "u", t, 0, 1)
                    sp.dma_start(cx[:], io["ctx"][bass.ds(t.b(0), 1)].rearrange("o (t p) d -> p (o t) d", p=P)).then_inc(s_cx, 16)
                if t.on(2):
                    passed(sp, QP, "out", t, 2)
                    sp.dma_start(io["out"][bass.ds(t.b(2), 1)].rearrange("o (t p) d -> p (o t) d", p=P), out[:]).then_inc(s_out, 16)

            run_turns(sp, turn, lambda t: None)
            sp.wait_ge(s_out, 16 * B)

        @block.gpsimd
        def _(pool):
            pool.memset(halfneg[:], -0.5)
            pool.memset(ones[:], 1.0).then_inc(s_set, 1)
            pool.wait_ge(s_set, 1)

            def add_eps(dst, src, scale, steps, name):
                pool.tensor_scalar(dst, src, scale, EPS, ALU.mult, ALU.add).then_inc(steps.sem, 1)

            def turn(t):
                if t.on(2):
                    passed(pool, QD, "aggr", t, 2)
                    pool.tensor_scalar(rq[:, 0, :], mvq[:, :, 1], EPS, None, ALU.add).then_inc(QP.sem, 1)
                    passed(pool, QP, "veps", t, 2)
                    pool.tensor_tensor(rq[:, 1, :], rq[:, 0, :], halfneg[:], ALU.pow).then_inc(QP.sem, 1)
                if t.on(1):
                    v = mvh[:, :, 1]
                    passed(pool, HD, "aggr", t, 1)
                    pool.tensor_scalar(rh[:, 0, :], v, EPS, None, ALU.add).then_inc(HP.sem, 1)
                    passed(pool, HP, "veps", t, 1)
                    pool.tensor_tensor(rh[:, 1, :], rh[:, 0, :], halfneg[:], ALU.pow).then_inc(HP.sem, 1)
                    passed(pool, HP, "r1", t, 1)
                    pool.tensor_tensor(rh[:, 2, :], rh[:, 1, :], rh[:, 1, :], ALU.mult).then_inc(HP.sem, 1)
                    passed(pool, HP, "r1sq", t, 1)
                    pool.tensor_tensor(rh[:, 3, :], rh[:, 2, :], v, ALU.mult).then_inc(HP.sem, 1)
                    passed(pool, HP, "v2", t, 1)
                    pool.tensor_scalar(rh[:, 4, :], rh[:, 3, :], EPS, None, ALU.add).then_inc(HP.sem, 1)
                    passed(pool, HP, "v2eps", t, 1)
                    pool.tensor_tensor(rh[:, 5, :], rh[:, 4, :], halfneg[:], ALU.pow).then_inc(HP.sem, 1)
                    passed(pool, HP, "r2", t, 1)
                    pool.tensor_tensor(rh[:, 6, :], rh[:, 5, :], rh[:, 1, :], ALU.mult).then_inc(HP.sem, 1)
                if t.on(0):
                    passed(pool, AA, "square", t, 0)
                    pool.tensor_scalar(ra[:, 0, :], ss[:], 1.0 / DC, EPS, ALU.mult, ALU.add).then_inc(AP_.sem, 1)
                    passed(pool, AP_, "ms", t, 0)
                    pool.tensor_tensor(ra[:, 1, :], ra[:, 0, :], halfneg[:], ALU.pow).then_inc(AP_.sem, 1)
                if t.on(2):
                    passed(pool, QA, "y", t, 2)
                    pool.tensor_tensor(ybias[:], y[:], keep["bias"][:].unsqueeze(1).broadcast_to((P, QT, D)), ALU.add).then_inc(QP.sem, 1)
                    passed(pool, QP, "bias", t, 2)
                    if t.ref - 2 >= 1:
                        pool.wait_ge(s_out, t.b(2) * 16)
                    pool.tensor_tensor(out[:].unsqueeze(1), x3[:, parity(t.b(2))], ybias[:].unsqueeze(1), ALU.add).then_inc(QP.sem, 1)

            run_turns(pool, turn, lambda t: None)

        @block.scalar
        def _(act):
            def turn(t):
                if t.on(0):
                    act.wait_ge(s_cx, (t.b(0) + 1) * 16)
                    passed(act, AP_, "ms", t, 0, 1)
                    for tt in range(QT):
                        last = act.activation(junk[:, tt, :], cx[:, tt, :], ACT.Square, accum_out=ss[:, tt:tt + 1])
                    last.then_inc(AA.sem, 1)
                if t.on(2):
                    passed(act, QE, "t", t, 2)
                    act.activation(qt[:].rearrange("p k s -> p (k s)"), p_q[:].bitcast(BF16)[:, 0:2 * S], ACT.Copy).then_inc(QA.sem, 1)
                if t.on(0):
                    passed(act, AE, "mt", t, 0)
                    passed(act, HE, "h", t, 0, 1)
                    act.activation(mt[:].rearrange("p t s -> p (t s)"), p_mt[:], ACT.Copy).then_inc(AA.sem, 1)
                if t.on(2):
                    passed(act, QE, "y", t, 2)
                    passed(act, QP, "bias", t, 2, 1)
                    act.activation(y[:].rearrange("p t d -> p (t d)"), p_y[:], ACT.Copy, scale=keep["s_out"][:, 0:1]).then_inc(QA.sem, 1)

            run_turns(act, turn, lambda t: None)

        @block.vector
        def _(v):
            v.wait_ge(s_set, 1)

            def turn(t):
                a, h, q = t.on(0), t.on(1), t.on(2)
                if q:
                    x3q = x3[:, parity(t.b(2))]
                    passed(v, HD, "x3", t, 2)
                    for tt in range(QT):
                        last = v.bn_stats(stq[:, tt, :], x3q[:, :, tt, :].rearrange("p o d -> p (o d)"))
                    last.then_inc(QD.sem, 1)
                if h:
                    tok = [res[:, bass.ds(t.b(1) * QT + tt, 1), :] for tt in range(QT)]
                    for tt in range(QT):
                        last = v.bn_stats(sth[:, tt, :], tok[tt].rearrange("p o d -> p (o d)"))
                    last.then_inc(HD.sem, 1)
                if q:
                    passed(v, QD, "stats", t, 2)
                    for tt in range(QT):
                        last = v.bn_aggr(mvq[:, tt, :], stq[:, tt, :])
                    last.then_inc(QD.sem, 1)
                if h:
                    passed(v, HD, "stats", t, 1)
                    for tt in range(QT):
                        last = v.bn_aggr(mvh[:, tt, :], sth[:, tt, :])
                    last.then_inc(HD.sem, 1)
                if a:
                    iota = cf[:, CF_IOTA:CF_IOTA + S]
                    where = lambda side, tt: bounds[:, side, tt, bass.ds(t.b(0), 1)]
                    passed(v, AE, "cnt", t, 0, 1)
                    for tt in range(QT):
                        last = v.tensor_scalar(eq[:, tt, :], iota, where(0, tt), None, ALU.is_equal)
                    last.then_inc(AD.sem, 1)
                    passed(v, AD, "eq", t, 0)
                    for tt in range(QT):
                        last = v.scalar_tensor_tensor(out=bnd_in[:, tt, :], in0=iota, scalar=where(1, tt), in1=eq[:, tt, :],
                                                      op0=ALU.is_equal, op1=ALU.add)
                    last.then_inc(AD.sem, 1)
                if q:
                    passed(v, QP, "rstd", t, 2)
                    for tt in range(QT):
                        last = v.tensor_scalar(xb[:, tt, :].unsqueeze(1), x3q[:, :, tt, :], mvq[:, tt, 0:1], rq[:, 1, tt:tt + 1], ALU.subtract, ALU.mult)
                    last.then_inc(QD.sem, 1)
                    passed(v, QD, "xb", t, 2)
                    v.tensor_scalar(qv[:], xb[:], keep["r_in"][:, 0:1], None, ALU.mult).then_inc(QD.sem, 1)
                if h:
                    passed(v, HP, "r12", t, 1)
                    passed(v, HE, "t", t, 1, 1)
                    for tt in range(QT):
                        last = v.tensor_scalar(xh[:, tt, :].unsqueeze(1), tok[tt], mvh[:, tt, 0:1], rh[:, 6, tt:tt + 1], ALU.subtract, ALU.mult)
                    last.then_inc(HD.sem, 1)
                if q:
                    passed(v, QD, "v", t, 2)
                    v.tensor_single_scalar(qe[:].bitcast(I32), qv[:].bitcast(I32), 0x7F800000, op=ALU.bitwise_and).then_inc(QD.sem, 1)
                    passed(v, QD, "exp", t, 2)
                    v.tensor_scalar(qb[:], qe[:], 2.0 ** -6, C20, ALU.max, ALU.mult).then_inc(QD.sem, 1)
                    passed(v, QD, "big", t, 2)
                    v.tensor_tensor(qsum[:], qv[:], qb[:], ALU.add).then_inc(QD.sem, 1)
                    passed(v, QD, "sum", t, 2)
                    passed(v, QE, "t", t, 2, 1)
                    v.tensor_tensor(qq[:], qsum[:], qb[:], ALU.subtract).then_inc(QD.sem, 1)
                if a:
                    passed(v, AP_, "rms", t, 0)
                    passed(v, HE, "h", t, 0, 2)
                    for tt in range(QT):
                        last = v.scalar_tensor_tensor(out=u[:, parity(t.b(0)), tt, :].rearrange("p o d -> p (o d)"), in0=cx[:, tt, 0:D],
                                                      scalar=ra[:, 1, tt:tt + 1], in1=keep["ginit"][:], op0=ALU.mult, op1=ALU.mult)
                    last.then_inc(AD.sem, 1)
                    passed(v, AE, "cnt", t, 0)
                    v.tensor_scalar(bnd[:], p_cnt[:, 0:S], 1.0, None, ALU.min).then_inc(AD.sem, 1)
                if h:
                    passed(v, HE, "t", t, 1)
                    pt = p_t[:].rearrange("p (k s) -> p k s", k=KD)
                    for k in range(KD):
                        last = v.tensor_scalar(nt[:, k, :], pt[:, k, :], lncol[:, 4, k:k + 1], None, ALU.mult)
                    last.then_inc(HD.sem, 1)
                if a:
                    passed(v, AD, "bnd", t, 0)
                    v.tensor_tensor_scan(cum[:], ones[:], bnd[:], 0.0, ALU.mult, ALU.add).then_inc(AD.sem, 1)
                    passed(v, AD, "cum", t, 0)
                    v.tensor_scalar(plug[:], cum[:], -1.0, 0.0, ALU.add, ALU.max).then_inc(AD.sem, 1)
                    passed(v, AD, "plug", t, 0)
                    passed(v, AE, "mt", t, 0, 1)
                    for tt in range(QT):
                        last = v.tensor_scalar(take[:, tt, :], plug[:], cf[:, CF_ROW + tt:CF_ROW + tt + 1], None, ALU.is_equal)
                    last.then_inc(AD.sem, 1)
                if h:
                    passed(v, HE, "h", t, 1)
                    passed(v, QP, "out", t, 1, 2)
                    v.tensor_tensor(x3[:, parity(t.b(1))].rearrange("p o t d -> p o (t d)"),
                                    p_h[:].unsqueeze(1),
                                    res[:, bass.ds(t.b(1) * QT, QT), :].rearrange("p t d -> p (t d)").unsqueeze(1), ALU.add).then_inc(HD.sem, 1)

            run_turns(v, turn, lambda t: None)

        @block.tensor
        def _(pe):
            idb, idf = cb[:, CB_ID:CB_ID + P], cf[:, CF_ID:CF_ID + P]
            ones3, onesb = cb[0:3, CB_ONE:CB_ONE + P], cb[:, CB_ONE:CB_ONE + P]
            pe.wait_ge(s_load, 16)

            def turn(t):
                a, h, q = t.on(0), t.on(1), t.on(2)
                if a:
                    passed(pe, AD, "bound", t, 0)
                    passed(pe, AD, "bnd", t, 0, 1)
                    for tt in range(QT):
                        last = pe.matmul(p_cnt[:, 0:S], onesb, bnd_in[:, tt, :], start=tt == 0, stop=tt == QT - 1)
                    last.then_inc(AE.sem, 1)
                if h:
                    passed(pe, HD, "xh", t, 1)
                    passed(pe, HD, "nt", t, 1, 1)
                    for k in range(KD):
                        for tt in range(QT):
                            last = pe.transpose(p_t[:, k * S + tt * P:k * S + (tt + 1) * P], xh[:, tt, k * P:(k + 1) * P], idf)
                    last.then_inc(HE.sem, 1)
                if q:
                    passed(pe, QD, "q", t, 2)
                    passed(pe, QA, "qt", t, 2, 1)
                    pq = p_q[:].bitcast(BF16)
                    for k in range(KD):
                        for tt in range(QT):
                            last = pe.transpose(pq[:, k * S + tt * P:k * S + (tt + 1) * P], qq[:, tt, k * P:(k + 1) * P], idb)
                    last.then_inc(QE.sem, 1)
                if h:
                    passed(pe, HD, "nt", t, 1)
                    passed(pe, AA, "mt", t, 1)
                    passed(pe, AD, "u", t, 1)
                    passed(pe, HD, "x3", t, 1, 1)
                    half = parity(t.b(1))
                    for tt in range(QT):
                        o = p_h[:, tt * D:(tt + 1) * D]
                        ts_ = slice(tt * P, (tt + 1) * P)
                        pe.matmul(o, ones3, rows[:, RW_IN:RW_IN + D], start=True, stop=False)
                        for k in range(KD):
                            pe.matmul(o, nt[:, k, ts_], win[:, k, :], start=False, stop=False)
                        for k in range(QT):
                            last = pe.matmul(o, mt[:, k, ts_], u[:, half, k, :].rearrange("p o d -> p (o d)"),
                                             start=False, stop=k == QT - 1)
                    last.then_inc(HE.sem, 1)
                if a:
                    passed(pe, AD, "take", t, 0)
                    passed(pe, AA, "mt", t, 0, 1)
                    l0, l1 = cf[:, CF_L0:CF_L0 + P], cf[:, CF_L1:CF_L1 + P]
                    pe.matmul(p_mt[:, 0:S], l0, take[:, 0, :], start=True, stop=False)
                    pe.matmul(p_mt[:, 0:S], l1, take[:, 1, :], start=False, stop=True)
                    pe.matmul(p_mt[:, S:2 * S], l0, take[:, 1, :], start=True, stop=True).then_inc(AE.sem, 1)
                if q:
                    passed(pe, QA, "qt", t, 2)
                    passed(pe, QA, "y", t, 2, 1)
                    for tt in range(QT):
                        for k in range(KD):
                            last = pe.matmul(p_y[:, tt * D:(tt + 1) * D], qt[:, k, tt * P:(tt + 1) * P], kq[:, k, :], start=k == 0, stop=k == KD - 1)
                    last.then_inc(QE.sem, 1)

            run_turns(pe, turn, lambda t: None)


def build(nc, io):
    with ExitStack() as ctx:
        def sb(name, shape, dt=F32):
            return ctx.enter_context(nc.sbuf_tensor(name, shape, dt))

        def sem(name):
            return ctx.enter_context(nc.semaphore(name))

        keep = {
            "res": sb("res", [P, NT, D]),
            "nxh": sb("nxh", [P, KD, B * S], BF16), "nxl": sb("nxl", [P, KD, B * S], BF16),
            "logits": sb("logits", [P, NT, E]),
            "cf": sb("cf", [P, CF_N]), "cb": sb("cb", [P, CB_N], BF16), "rows": sb("rows", [3, RW_N], BF16),
            "kext": sb("kext", [P, B, QT, 4], BF16),
            "any4": sb("any4", [P, B]), "kq": sb("kq", [P, KD, D], BF16), "bounds": sb("bounds", [P, 2, QT, B]),
            "bias": sb("bias", [P, D], BF16), "lncol": sb("lncol", [P, 5, KD]),
            "r_in": sb("r_in", [P, 1]), "s_out": sb("s_out", [P, 1]), "ginit": sb("ginit_s", [P, D]),
        }
        setup_phase(nc, io, keep, sem)
        attention_phase(nc, io, keep, sem)
        expert_phase(nc, io, keep, sem)
        last_phase(nc, io, keep, sem)


def constants(np, bf16):
    cf = np.zeros((P, CF_N), np.float32)
    i = np.arange(P)
    cf[:, CF_ID:CF_ID + P] = np.eye(P)
    cf[:, CF_IOTA:CF_IOTA + S] = np.arange(S)
    for t in range(QT):
        cf[:, CF_ROW + t] = i + t * P
    cf[:, CF_TRI:CF_TRI + P] = i[:, None] <= i[None, :]
    cf[:, CF_ONE:CF_ONE + P] = 1
    decay = -math.expm1(-PATCH_EPS)
    for at, off in ((CF_L0, 0), (CF_L1, P)):
        d = i[:, None] - i[None, :] + off
        cf[:, at:at + P] = np.where(d >= 0, decay ** np.clip(d, 0, 300).astype(np.float64), 0)
    cb = np.zeros((P, CB_N), np.float32)
    cb[:, CB_ID:CB_ID + P] = np.eye(P)
    later = np.where(i[:, None] < i[None, :], -1e30, 0)
    cb[:, CB_MQ:CB_MQ + 2 * P] = np.tile(later, 2)
    cb[:, CB_MK:CB_MK + 2 * P] = np.tile(later.T, 2)
    cb[:, CB_ONE:CB_ONE + P] = 1
    return cf, cb.astype(bf16)


def kernel(**inputs):
    import numpy as np
    import concourse.bacc as bacc
    from concourse.bass_utils import run_bass_kernel_spmd as run

    a = {k: np.asarray(v) for k, v in inputs.items()}
    cf, cb = constants(np, a["L1_ffn_kernel"].dtype)
    rows = np.concatenate([a["L0_ffn_bqkv"], a["L0_ffn_bo"], a["L0_ffn_fc2_b"].reshape(-1), a["L1_xattn_b_in"]])
    data = {
        "cf": cf, "cb": cb, "x": a["x"], "ctx": a["ctx_2048"], "seq": a["itok_Bx1_68_817"].reshape(-1),
        "lens": a["mask_BxS2_if0"].T.reshape(QT, P, B).transpose(1, 0, 2), "b": a["L0_xattn_b"].reshape(QT, P).T, "rows": np.stack([rows] * 3),
        "wqkv": a["L0_ffn_Wqkv"], "wo": a["L0_ffn_Wo"], "wgate": a["L0_ffn_gate_W"],
        "lncol": np.stack([a["L0_ffn_ln1_w"], a["L0_ffn_ln1_b"], a["L0_ffn_ln2_w"], a["L0_ffn_ln2_b"], a["L1_xattn_g_res"]]).reshape(5, KD, P).transpose(2, 0, 1),
        "fc1": a["L0_ffn_fc1_w"].transpose(0, 2, 1), "fc1b": a["L0_ffn_fc1_b"].reshape(E * FT, P).T, "fc2": a["L0_ffn_fc2_w"].transpose(0, 2, 1),
        "win": a["L1_xattn_W_in"].T, "ginit": a["L1_xattn_g_init"][0:D],
        "kern": a["L1_ffn_kernel"], "s_in": a["L1_ffn_input_scale"], "s_k": a["L1_ffn_kernel_scale"], "bias": a["L1_ffn_bias"],
    }
    data = {k: np.ascontiguousarray(v) for k, v in data.items()}
    nc = bacc.Bacc("TRN2", target_bir_lowering=False, num_devices=1)
    io = {k: nc.dram_tensor(f"in_{k}", v.shape, mybir.dt.from_np(v.dtype), kind="ExternalInput").ap() for k, v in data.items()}
    io["out"] = nc.dram_tensor("out", (B, S, D), F32, kind="ExternalOutput").ap()
    build(nc, io)
    r = run(nc, [{f"in_{k}": v for k, v in data.items()}], core_ids=[0])
    return r.results[0]["out"]
```

```python
import math
from contextlib import ExitStack

import concourse.bass as bass
from concourse import mybir

F32 = mybir.dt.float32
BF16 = mybir.dt.bfloat16
I32 = mybir.dt.int32
U32 = mybir.dt.uint32
ALU = mybir.AluOpType
ACT = mybir.ActivationFunctionType
AX = mybir.AxisListType

P = 128
B, S, D = 16, 256, 256
DC = 512
H, DH = 16, 16
NT = B * S // P
QT = S // P
KD = D // P
E, F, TOPK = 8, 1024, 2
FT = F // P
HB = 64
GROUPS = 8
STEPS = 16
NPT = 4
SLOTS = 256
ST = SLOTS // P
NTILE = (TOPK * B * S + E * (SLOTS - 1)) // SLOTS
REGION = B * S + SLOTS
NROWS = E * REGION + NTILE * SLOTS
EPS = 1e-5
PATCH_EPS = 0.001
NEG_BIG = -1e12
C20 = 1.5 * 2.0 ** 20

CF_ID, CF_IOTA, CF_ROW, CF_TRI, CF_ONE, CF_L0, CF_L1, CF_REG, CF_N = 0, 128, 384, 386, 514, 642, 770, 898, 907
CB_ID, CB_MQ, CB_MK, CB_ONE, CB_TRI, CB_N = 0, 128, 384, 640, 768, 896
RW_QKV, RW_O, RW_FC2, RW_IN, RW_N = 0, 768, 1024, 1024 + 8 * 256, 1280 + 8 * 256


class Steps:

    def __init__(self, sem, names):
        self.sem, self.names, self.n = sem, names.split(), len(names.split())

    def at(self, name, b):
        return b * self.n + self.names.index(name) + 1


class Turn:

    def __init__(self, i, ref=None):
        self.i, self.ref = i, i if ref is None else ref
        self.loop = ref is not None

    def b(self, lag):
        return self.i - lag

    def on(self, lag):
        return self.loop or 0 <= self.i - lag < B

    def first(self, lag):
        return self.ref - lag == 0


T_USES = [
    ("x_kt0", 0, 0), ("x_kt1", 0, 1), ("x_qt0", 0, 0), ("x_qt1", 0, 1), ("c_m0", 2, 0), ("c_m1", 2, 1),
    ("r_cnt", 3, 1), ("c_xt", 1, 0), ("c_qk0", 1, 1), ("c_v", 1, 0), ("c_qk1", 1, 1),
    ("c_kt0", 1, 0), ("c_kt1", 1, 1), ("c_qt0", 1, 0), ("c_qt1", 1, 1), ("x_m0", 0, 0), ("x_m1", 0, 1),
    ("c_back0", 2, 0), ("c_back1", 2, 1), ("c_at", 2, 0), ("c_wo", 2, 1), ("c_nt", 2, 0), ("c_gate", 2, 1),
    ("x_back0", 0, 0), ("x_back1", 0, 1),
]


LAGS = 3


def ring_table(uses):
    table, count = {}, {}
    for i in range(B + LAGS):
        for name, lag, bank in uses:
            if 0 <= i - lag < B:
                table[name, i - lag] = count.get(bank, 0)
                count[bank] = count.get(bank, 0) + 1
    return table


O_USES = [("c", 2, 0), ("x", 0, 0)]
S1_USES = [("x", 0, 0), ("c", 1, 0)]
S2_USES = [("c", 2, 0), ("x", 0, 0)]


def attention_phase(nc, io, keep, sem):
    T_TAB = ring_table(T_USES)
    O_TAB, S1_TAB, S2_TAB = (ring_table(u) for u in (O_USES, S1_USES, S2_USES))
    bank_of = {name: bank for name, _, bank in T_USES}
    T_PER = [sum(bank == n for _, _, bank in T_USES) for n in range(2)]

    res, gap, place, base, cf, cb = (keep[n] for n in ("res", "gap", "place", "base", "cf", "cb"))
    xs = keep["xs"]
    rows, kext, any4, lncol = keep["rows"], keep["kext"], keep["any4"], keep["lncol"]

    with ExitStack() as ctx:
        def sb(name, shape, dt=F32):
            return ctx.enter_context(nc.sbuf_tensor(name, shape, dt))

        ctxb = sb("ctxb", [P, QT, DC])
        wqkv = sb("wqkv", [P, KD, 3 * D])
        wo = sb("wo", [P, KD, D])
        wgate = sb("wgate", [P, KD, E])
        halfneg = sb("halfneg", [P, 2])

        qs = {k: sb(f"qs_{k}", [P, QT, H, HB], BF16) for k in "xc"}
        ks = {k: sb(f"ks_{k}", [P, QT, H, HB], BF16) for k in "xc"}
        qt = {k: sb(f"qt_{k}", [P, GROUPS, S], BF16) for k in "xc"}
        kt = {k: sb(f"kt_{k}", [P, GROUPS, S], BF16) for k in "xc"}
        v1 = {k: sb(f"v1_{k}", [P, QT, H, 32]) for k in "xc"}
        qf = {k: sb(f"qf_{k}", [P, QT, D]) for k in "xc"}
        negm = {k: sb(f"negm_{k}", [P, QT, H]) for k in "xc"}
        mres = {k: sb(f"mres_{k}", [P, QT, H]) for k in "xc"}
        att = {k: sb(f"att_{k}", [P, QT, D]) for k in "xc"}
        rden = {k: sb(f"rden_{k}", [P, QT, H]) for k in "xc"}
        ot = {k: sb(f"ot_{k}", [P, 4, S]) for k in "xc"}
        st = {k: sb(f"st_{k}", [P, QT, 6]) for k in "xc"}
        mv = {k: sb(f"mv_{k}", [P, QT, 2]) for k in "xc"}
        rs = {k: sb(f"rs_{k}", [P, 8, QT]) for k in "xc"}
        st2, mv2 = sb("st2", [P, QT, 6]), sb("mv2", [P, QT, 2])
        rs2 = sb("rs2", [P, 2, QT])
        kf = sb("kf", [P, QT, D])
        xin = sb("xin", [P, 2, QT, D])
        xh = sb("xh", [P, QT, D])
        nxt = sb("nxt", [P, KD, S])
        at = sb("at", [P, KD, S])
        xp = sb("xp", [P, QT, D])
        xh2 = sb("xh2", [P, QT, D])
        n2 = sb("n2", [P, KD, S])
        prob = sb("prob", [P, NPT, 2, S])
        logits = sb("logits", [P, QT, E])
        top, idx = sb("top", [P, QT, 8]), sb("idx", [P, QT, 8], U32)
        idf = sb("idf", [P, TOPK, QT])
        chosen, hot = sb("chosen", [P, TOPK, QT, E]), sb("hot", [P, QT, E], BF16)
        rank, picked = sb("rank", [P, QT, E]), sb("picked", [P, TOPK, QT, E])
        placef, placeu = sb("placef", [P, TOPK * QT]), sb("placeu", [P, TOPK * QT], U32)

        tb = [ctx.enter_context(nc.psum_tensor(f"tb{n}", [P, 512], F32)) for n in range(2)]
        s1 = [ctx.enter_context(nc.psum_tensor(f"s1_{n}", [P, 2, S], F32)) for n in range(2)]
        s2 = [ctx.enter_context(nc.psum_tensor(f"s2_{n}", [P, 2, S], F32)) for n in range(2)]
        ob = ctx.enter_context(nc.psum_tensor("ob", [P, 4, S], F32))

        s_load, s_ctx, s_set = sem("a_load"), sem("a_ctx"), sem("a_pool_setup")
        t_full, t_free = [sem(f"t_full{n}") for n in range(2)], [sem(f"t_free{n}") for n in range(2)]
        s1_full, s1_free = sem("s1_full"), sem("s1_free")
        s2_full, s2_free = sem("s2_full"), sem("s2_free")
        p_full, p_free = sem("p_full"), sem("p_free")
        o_free = sem("o_free")
        s_seen = {e.engine: sem(f"a_seen_{n}") for e, n in ((nc.gpsimd, "pool"), (nc.vector, "dve"))}
        XD0 = Steps(sem("x_dve_pre"), "stats aggr q klo qlo")
        XD1 = Steps(sem("x_dve"), "m_hi m_res m_mid m_lo rec0 rec1")
        XP0 = Steps(sem("x_pool_pre"), "veps rstd rq khi2 qhi2 kext")
        XP1 = Steps(sem("x_pool"), "v x1")
        XA0 = Steps(sem("x_act_pre"), "khi qhi")
        CD1 = Steps(sem("c1_dve"), "stats aggr xin xh klo qlo m_hi m_res m_mid m_lo")
        CD2 = Steps(sem("c2_dve"), "rec0 rec1 stats2 aggr2 xh2")
        CP1 = Steps(sem("c1_pool"), "veps r1 r1sq v2 v2eps r2 r12 khi2 qhi2")
        CP2 = Steps(sem("c2_pool"), "veps2 rstd2 x2")
        CA1 = Steps(sem("c1_act"), "khi qhi")
        RD = Steps(sem("r_dve"), "top idx idf gap chosen hot rank picked placef placeu place")
        s_rows = sem("rows_scattered")
        DVE_SPLIT, POOL_SPLIT, ACT_SPLIT = {"x": XD0, "c": CD1}, {"x": XP0, "c": CP1}, {"x": XA0, "c": CA1}
        DVE_MAX, DVE_OUT = {"x": XD1, "c": CD1}, {"x": XD1, "c": CD2}

        def wait(eng, s, value):
            if not isinstance(value, int) or value > 0:
                eng.wait_ge(s, value)

        def passed(eng, steps, name, t, lag, back=0):
            if t.ref - lag - back >= 0:
                eng.wait_ge(steps.sem, steps.at(name, t.b(lag) - back))
                if t.loop and (eng is nc.gpsimd or name in ("stats", "stats2")):
                    eng.sem_inc(s_seen[eng.engine], 1)

        def t_use(t, name, lag, back=0):
            base = T_TAB[name, t.ref - lag - back]
            return base + (t.i - t.ref) * T_PER[bank_of[name]] if t.loop else base

        def t_wait_full(eng, t, name, lag, back=0):
            if t.ref - lag - back >= 0:
                eng.wait_ge(t_full[bank_of[name]], t_use(t, name, lag, back) + 1)

        def t_wait_free(eng, t, name, lag):
            wait(eng, t_free[bank_of[name]], t_use(t, name, lag))

        def t_wait_read(eng, t, name, lag, back=0):
            if t.ref - lag - back >= 0:
                eng.wait_ge(t_free[bank_of[name]], t_use(t, name, lag, back) + 1)

        def ring(table, t, kind, lag, k, back=0):
            base = table[kind, t.ref - lag - back]
            return (base + (t.i - t.ref) * 2 if t.loop else base) * STEPS + k

        def products_done(eng, k, t, lag, back=0):
            if t.ref - lag - back >= 0:
                eng.wait_ge(p_free, ring(S2_TAB, t, k, lag, STEPS - 1, back) + 1)

        def o_count(t, k, lag):
            base = O_TAB[k, t.ref - lag]
            return base + (t.i - t.ref) * 2 if t.loop else base

        def heads(g):
            return [4 * (g // 2) + g % 2, 4 * (g // 2) + g % 2 + 2]

        def parity(b):
            return bass.ds(b % 2, 1)

        TOK = lambda t, lag: bass.ds(t.b(lag) * QT, QT)

        block = ctx.enter_context(nc.Block())

        n_load = 3

        @block.sync
        def _(sp):
            for dst, src in (
                (wqkv[:], io["wqkv"].rearrange("(k p) n -> p k n", p=P)),
                (wo[:], io["wo"].rearrange("(k p) n -> p k n", p=P)),
                (wgate[:], io["wgate"].rearrange("(k p) n -> p k n", p=P)),
            ):
                sp.dma_start(dst, src).then_inc(s_load, 16)

            def load_ctx(t, lag):
                passed(sp, XD0, "klo", t, lag, 1)
                passed(sp, XP1, "v", t, lag, 1)
                sp.dma_start(ctxb[:], io["ctx"][bass.ds(t.b(lag), 1)].rearrange("o (t p) d -> p (o t) d", p=P)).then_inc(s_ctx, 16)

            for b in range(2):
                load_ctx(Turn(b), 0)
            with sp.Fori(2, B) as b:
                load_ctx(Turn(b, 2), 0)

        @block.gpsimd
        def _(pool):
            for k in "xc":
                pool.memset(qs[k][:], 0.0)
                pool.memset(ks[k][:], 0.0)
                pool.memset(v1[k][:], 0.0).then_inc(s_set, 1)
            pool.wait_ge(s_set, 2)
            for k in "xc":
                pool.memset(qs[k][:, :, :, 48:52], 1.0)
                pool.memset(ks[k][:, :, :, 52:55], 1.0)
                pool.memset(v1[k][:, :, :, DH:DH + 1], 1.0)
            pool.memset(halfneg[:], -0.5).then_inc(s_set, 1)
            pool.wait_ge(s_set, 3)
            def x_norm(t, lag):
                r = rs["x"]
                passed(pool, XD0, "aggr", t, lag)
                pool.tensor_scalar(r[:, 0, :], mv["x"][:, :, 1], EPS, None, ALU.add).then_inc(XP0.sem, 1)
                passed(pool, XP0, "veps", t, lag)
                pool.tensor_tensor(r[:, 1, :], r[:, 0, :], halfneg[:], ALU.pow).then_inc(XP0.sem, 1)
                passed(pool, XP0, "rstd", t, lag)
                pool.tensor_tensor(r[:, 2, :], r[:, 1, :], any4[:, bass.ds(t.b(lag), 1)].broadcast_to((P, QT)), ALU.mult).then_inc(XP0.sem, 1)

            def split_copies(k, t, lag, order):
                for w in order:
                    if w == "k":
                        passed(pool, ACT_SPLIT[k], "khi", t, lag)
                        pool.tensor_copy(ks[k][:, :, :, DH:2 * DH], ks[k][:, :, :, 0:DH]).then_inc(POOL_SPLIT[k].sem, 1)
                    else:
                        passed(pool, ACT_SPLIT[k], "qhi", t, lag)
                        pool.tensor_copy(qs[k][:, :, :, 2 * DH:3 * DH], qs[k][:, :, :, 0:DH]).then_inc(POOL_SPLIT[k].sem, 1)

            def x_kext(t, lag):
                src = kext[:, bass.ds(t.b(lag), 1), :, :]
                for tt in range(QT):
                    last = pool.tensor_copy(ks["x"][:, tt, :, 48:52], src[:, :, tt, :].broadcast_to((P, H, 4)))
                last.then_inc(XP0.sem, 1)

            def x_v(t, lag):
                pool.wait_ge(s_ctx, (t.b(lag) + 1) * 16)
                products_done(pool, "x", t, lag, 1)
                pool.sem_inc(s_seen[pool.engine], 1)
                pool.tensor_copy(v1["x"][:, :, :, 0:DH],
                                 ctxb[:, :, D:DC].rearrange("p t (h d) -> p t h d", h=H)).then_inc(XP1.sem, 1)

            def x_sum(t, lag):
                t_wait_read(pool, t, "x_back1", lag)
                pool.tensor_tensor(res[:, TOK(t, lag), :], res[:, TOK(t, lag), :], att["x"][:], ALU.add).then_inc(XP1.sem, 1)

            def c_norm(t, lag):
                r, v = rs["c"], mv["c"][:, :, 1]
                passed(pool, CD1, "aggr", t, lag)
                pool.tensor_scalar(r[:, 0, :], v, EPS, None, ALU.add).then_inc(CP1.sem, 1)
                passed(pool, CP1, "veps", t, lag)
                pool.tensor_tensor(r[:, 1, :], r[:, 0, :], halfneg[:], ALU.pow).then_inc(CP1.sem, 1)
                passed(pool, CP1, "r1", t, lag)
                pool.tensor_tensor(r[:, 2, :], r[:, 1, :], r[:, 1, :], ALU.mult).then_inc(CP1.sem, 1)
                passed(pool, CP1, "r1sq", t, lag)
                pool.tensor_tensor(r[:, 3, :], r[:, 2, :], v, ALU.mult).then_inc(CP1.sem, 1)
                passed(pool, CP1, "v2", t, lag)
                pool.tensor_scalar(r[:, 4, :], r[:, 3, :], EPS, None, ALU.add).then_inc(CP1.sem, 1)
                passed(pool, CP1, "v2eps", t, lag)
                pool.tensor_tensor(r[:, 5, :], r[:, 4, :], halfneg[:], ALU.pow).then_inc(CP1.sem, 1)
                passed(pool, CP1, "r2", t, lag)
                pool.tensor_tensor(r[:, 6, :], r[:, 5, :], r[:, 1, :], ALU.mult).then_inc(CP1.sem, 1)

            def c_norm2(t, lag):
                passed(pool, CD2, "aggr2", t, lag)
                pool.tensor_scalar(rs2[:, 0, :], mv2[:, :, 1], EPS, None, ALU.add).then_inc(CP2.sem, 1)
                passed(pool, CP2, "veps2", t, lag)
                pool.tensor_tensor(rs2[:, 1, :], rs2[:, 0, :], halfneg[:], ALU.pow).then_inc(CP2.sem, 1)

            def c_sum(t, lag):
                t_wait_read(pool, t, "c_wo", lag)
                pool.tensor_tensor(res[:, TOK(t, lag), :], res[:, TOK(t, lag), :], xp[:], ALU.add).then_inc(CP2.sem, 1)

            def r_scatter(t, lag):
                passed(pool, RD, "placeu", t, lag)
                for k in range(TOPK):
                    for tt in range(QT):
                        n = k * QT + tt
                        pool.indirect_dma_start(xs[:, :], bass.IndirectOffsetOnAxis(placeu[:, n:n + 1], 0), xh2[:, tt, :], None)\
                            .then_inc(s_rows, 16)

            def turn(t):
                if t.on(0):
                    x_v(t, 0)
                if t.on(1):
                    c_norm(t, 1)
                if t.on(3):
                    r_scatter(t, 3)
                if t.on(1):
                    split_copies("c", t, 1, "kq")
                if t.on(-1):
                    x_norm(t, -1)
                    split_copies("x", t, -1, "kq")
                    x_kext(t, -1)
                if t.on(2):
                    c_norm2(t, 2)
                    c_sum(t, 2)
                if t.on(0):
                    x_sum(t, 0)

            run_turns(pool, turn, lambda t: (x_norm(t, 0), split_copies("x", t, 0, "kq"), x_kext(t, 0)))

        @block.scalar
        def _(act):
            act.wait_ge(s_set, 3)

            def split_hi(k, t, lag, which):
                if which == "k":
                    if k == "x":
                        act.wait_ge(s_ctx, (t.b(lag) + 1) * 16)
                    else:
                        t_wait_read(act, t, "c_qk1", lag)
                    t_wait_full(act, t, f"{k}_kt1", lag, 1)
                    src = ctxb[:, :, 0:D] if k == "x" else kf[:]
                    act.activation(ks[k][:, :, :, 0:DH], src.rearrange("p t (h d) -> p t h d", h=H), ACT.Copy).then_inc(ACT_SPLIT[k].sem, 1)
                else:
                    if k == "x":
                        passed(act, XD0, "q", t, lag)
                    else:
                        t_wait_read(act, t, "c_qk1", lag)
                    t_wait_full(act, t, f"{k}_m1", lag, 1)
                    act.activation(qs[k][:, :, :, 0:DH], qf[k][:].rearrange("p t (h d) -> p t h d", h=H), ACT.Copy).then_inc(ACT_SPLIT[k].sem, 1)

            def evac_pairs(dst, t, name, lag, half):
                t_wait_full(act, t, name, lag)
                act.activation(dst[:, 4 * half:4 * half + 4, :].rearrange("p g s -> p (g s)"),
                               tb[bank_of[name]][:].bitcast(BF16), ACT.Copy).then_inc(t_free[bank_of[name]], 1)

            def exps(k, t, lag, n):
                kk, c = n % 2, ring(S2_TAB, t, k, lag, n)
                act.wait_ge(s2_full, c + 1)
                wait(act, p_free, c + 1 - NPT)
                lo = P if k == "c" and kk else 0
                act.activation(prob[:, n % NPT, :, lo:S], s2[n % 2][:, :, lo:S], ACT.Exp).then_inc(p_full, 1)

            def o_evac(k, t, lag):
                products_done(act, k, t, lag)
                t_wait_full(act, t, f"{k}_back1", lag, 1)
                for n in range(2):
                    last = act.activation(ot[k][:, 2 * n:2 * n + 2, :], ob[:, 2 * n:2 * n + 2, :], ACT.Copy)
                last.then_inc(o_free, 1)

            def c_qk(t, lag, tt):
                name = f"c_qk{tt}"
                t_wait_full(act, t, name, lag)
                if tt == 0:
                    passed(act, CD1, "qlo", t, lag, 1)
                act.activation(qf["c"][:, tt, :], tb[bank_of[name]][:, 0:D], ACT.Copy, scale=DH ** -0.5)
                act.activation(kf[:, tt, :], tb[bank_of[name]][:, D:2 * D], ACT.Copy).then_inc(t_free[bank_of[name]], 1)

            def c_at(t, lag):
                t_wait_full(act, t, "c_at", lag)
                act.activation(at[:].rearrange("p k s -> p (k s)"), tb[bank_of["c_at"]][:], ACT.Copy).then_inc(t_free[bank_of["c_at"]], 1)

            def c_gate(t, lag):
                t_wait_full(act, t, "c_gate", lag)
                passed(act, RD, "idx", t, lag, 1)
                act.activation(logits[:], tb[bank_of["c_gate"]][:, 0:QT * E].rearrange("p (t e) -> p t e", e=E),
                               ACT.Copy).then_inc(t_free[bank_of["c_gate"]], 1)

            def turn(t):
                x, c1, c2, x_next = t.on(0), t.on(1), t.on(2), t.on(-1)
                if x:
                    evac_pairs(kt["x"], t, "x_kt1", 0, 1)
                    evac_pairs(qt["x"], t, "x_qt1", 0, 1)
                if c2:
                    evac_pairs(qt["c"], t, "c_m1", 2, 1)
                for n in range(STEPS):
                    if c2:
                        exps("c", t, 2, n)
                    if c1 and n == 9:
                        c_qk(t, 1, 0)
                if c2:
                    o_evac("c", t, 2)
                if c1:
                    c_qk(t, 1, 1)
                    split_hi("c", t, 1, "k")
                    split_hi("c", t, 1, "q")
                    evac_pairs(kt["c"], t, "c_kt1", 1, 1)
                    evac_pairs(qt["c"], t, "c_qt1", 1, 1)
                if x:
                    evac_pairs(qt["x"], t, "x_m1", 0, 1)
                for n in range(STEPS):
                    if x:
                        exps("x", t, 0, n)
                    if x_next and n == 5:
                        split_hi("x", t, -1, "k")
                    if x_next and n == 7:
                        split_hi("x", t, -1, "q")
                    if c2 and n == 6:
                        c_at(t, 2)
                if x:
                    o_evac("x", t, 0)
                if c2:
                    c_gate(t, 2)

            run_turns(act, turn, lambda t: (split_hi("x", t, 0, "k"), split_hi("x", t, 0, "q")))

        @block.vector
        def _(v):
            v.wait_ge(s_set, 3)

            def stats(k, t, lag):
                for tt in range(QT):
                    last = v.bn_stats(st[k][:, tt, :], res[:, bass.ds(t.b(lag) * QT + tt, 1), :].rearrange("p o d -> p (o d)"))
                last.then_inc(DVE_SPLIT[k].sem, 1)
                passed(v, DVE_SPLIT[k], "stats", t, lag)
                for tt in range(QT):
                    last = v.bn_aggr(mv[k][:, tt, :], st[k][:, tt, :])
                last.then_inc(DVE_SPLIT[k].sem, 1)

            def x_q(t, lag):
                passed(v, XP0, "rq", t, lag)
                passed(v, XA0, "qhi", t, lag, 1)
                for tt in range(QT):
                    last = v.tensor_scalar(qf["x"][:, tt, :], res[:, bass.ds(t.b(lag) * QT + tt, 1), :], mv["x"][:, tt, 0:1],
                                           rs["x"][:, 2, tt:tt + 1], ALU.subtract, ALU.mult)
                last.then_inc(XD0.sem, 1)

            def split_lo(k, t, lag, which):
                if which == "k":
                    passed(v, ACT_SPLIT[k], "khi", t, lag)
                    src = ctxb[:, :, 0:D] if k == "x" else kf[:]
                    v.tensor_tensor(ks[k][:, :, :, 2 * DH:3 * DH], src.rearrange("p t (h d) -> p t h d", h=H),
                                    ks[k][:, :, :, 0:DH], ALU.subtract).then_inc(DVE_SPLIT[k].sem, 1)
                else:
                    passed(v, ACT_SPLIT[k], "qhi", t, lag)
                    v.tensor_tensor(qs[k][:, :, :, DH:2 * DH], qf[k][:].rearrange("p t (h d) -> p t h d", h=H),
                                    qs[k][:, :, :, 0:DH], ALU.subtract).then_inc(DVE_SPLIT[k].sem, 1)

            def evac_pairs(dst, t, name, lag, half):
                t_wait_full(v, t, name, lag)
                v.tensor_copy(dst[:, 4 * half:4 * half + 4, :].rearrange("p g s -> p (g s)"),
                              tb[bank_of[name]][:].bitcast(BF16)).then_inc(t_free[bank_of[name]], 1)

            def maxes(k, t, lag, n):
                qq, g = n // GROUPS, n % GROUPS
                v.wait_ge(s1_full, ring(S1_TAB, t, k, lag, n) + 1)
                keys = P if k == "c" and qq == 0 else S
                h0 = heads(g)[0]
                v.tensor_reduce(negm[k][:, qq, h0:h0 + 3:2], s1[n % 2][:, :, 0:keys], AX.X, ALU.max, negate=True).then_inc(s1_free, 1)

            def max_parts(k, t, lag):
                steps = DVE_MAX[k]
                hi, mid, lo = (qs[k][:, :, :, 52 + n] for n in range(3))
                v.wait_ge(s1_free, ring(S1_TAB, t, k, lag, STEPS - 1) + 1)
                v.tensor_copy(hi, negm[k][:]).then_inc(steps.sem, 1)
                passed(v, steps, "m_hi", t, lag)
                v.tensor_tensor(mres[k][:], negm[k][:], hi, ALU.subtract).then_inc(steps.sem, 1)
                passed(v, steps, "m_res", t, lag)
                v.tensor_copy(mid, mres[k][:]).then_inc(steps.sem, 1)
                passed(v, steps, "m_mid", t, lag)
                v.tensor_tensor(lo, mres[k][:], mid, ALU.subtract).then_inc(steps.sem, 1)

            def normalize(k, t, lag):
                for qq in range(QT):
                    name = f"{k}_back{qq}"
                    t_wait_full(v, t, name, lag)
                    if qq == 0 and k == "x":
                        passed(v, XP1, "x1", t, lag, 1)
                    view = tb[bank_of[name]][:].rearrange("p (h d) -> p h d", d=32)
                    v.reciprocal(rden[k][:, qq, :], view[:, :, DH]).then_inc(DVE_OUT[k].sem, 1)
                    passed(v, DVE_OUT[k], f"rec{qq}", t, lag)
                    v.tensor_tensor(att[k][:, qq, :].rearrange("p (h d) -> p h d", h=H), view[:, :, 0:DH],
                                    rden[k][:, qq, :].unsqueeze(2).broadcast_to((P, H, DH)), ALU.mult).then_inc(t_free[bank_of[name]], 1)

            def c_stats(t, lag):
                passed(v, XP1, "x1", t, lag)
                stats("c", t, lag)

            def c_xin(t, lag):
                passed(v, CP1, "r12", t, lag)
                for dst, r in ((xin[:, parity(t.b(lag))], 1), (xh[:].unsqueeze(1), 6)):
                    for tt in range(QT):
                        last = v.tensor_scalar(dst[:, :, tt, :], res[:, bass.ds(t.b(lag) * QT + tt, 1), :], mv["c"][:, tt, 0:1],
                                               rs["c"][:, r, tt:tt + 1], ALU.subtract, ALU.mult)
                    last.then_inc(CD1.sem, 1)

            def weigh(name, dst, w, t, lag):
                t_wait_full(v, t, name, lag)
                if name == "c_nt":
                    t_wait_full(v, t, "c_gate", lag, 1)
                src = tb[bank_of[name]][:].rearrange("p (k s) -> p k s", k=KD)
                for k in range(KD):
                    last = v.tensor_scalar(dst[:, k, :], src[:, k, :], lncol[:, w, k:k + 1], lncol[:, w + 1, k:k + 1], ALU.mult, ALU.add)
                last.then_inc(t_free[bank_of[name]], 1)

            def c_v(t, lag):
                t_wait_full(v, t, "c_v", lag)
                products_done(v, "c", t, lag, 1)
                v.tensor_copy(v1["c"][:, :, :, 0:DH], tb[bank_of["c_v"]][:].rearrange("p (t h d) -> p t h d", t=QT, h=H))\
                    .then_inc(t_free[bank_of["c_v"]], 1)

            def c_xp(t, lag):
                t_wait_full(v, t, "c_wo", lag)
                passed(v, CP2, "x2", t, lag, 1)
                v.tensor_tensor(xp[:].rearrange("p t d -> p (t d)").unsqueeze(1), tb[bank_of["c_wo"]][:].unsqueeze(1),
                                xin[:, parity(t.b(lag))].rearrange("p o t d -> p o (t d)"), ALU.add).then_inc(t_free[bank_of["c_wo"]], 1)
                t_wait_read(v, t, "c_wo", lag)
                for tt in range(QT):
                    last = v.bn_stats(st2[:, tt, :], xp[:, tt, :])
                last.then_inc(CD2.sem, 1)
                passed(v, CD2, "stats2", t, lag)
                for tt in range(QT):
                    last = v.bn_aggr(mv2[:, tt, :], st2[:, tt, :])
                last.then_inc(CD2.sem, 1)

            def c_xh2(t, lag):
                passed(v, CP2, "rstd2", t, lag)
                if t.ref - lag >= 1:
                    v.wait_ge(s_rows, t.b(lag) * (16 * TOPK * QT))
                for tt in range(QT):
                    last = v.tensor_scalar(xh2[:, tt, :], xp[:, tt, :], mv2[:, tt, 0:1], rs2[:, 1, tt:tt + 1], ALU.subtract, ALU.mult)
                last.then_inc(CD2.sem, 1)

            def r_first(t, lag):
                t_wait_read(v, t, "c_gate", lag)
                if t.loop:
                    v.sem_inc(s_seen[v.engine], 1)
                for tt in range(QT):
                    last = v.max(top[:, tt, :], logits[:, tt, :])
                last.then_inc(RD.sem, 1)
                v.wait_ge(RD.sem, RD.at("top", t.b(lag)))
                v.sem_inc(s_seen[v.engine], 1)
                for tt in range(QT):
                    last = v.max_index(idx[:, tt, :], top[:, tt, :], logits[:, tt, :])
                last.then_inc(RD.sem, 1)
                passed(v, RD, "idx", t, lag)
                v.tensor_copy(idf[:], idx[:, :, 0:TOPK].rearrange("p t k -> p k t")).then_inc(RD.sem, 1)
                v.tensor_tensor(gap[:, TOK(t, lag)], top[:, :, 1], top[:, :, 0], ALU.subtract).then_inc(RD.sem, 1)
                passed(v, RD, "idf", t, lag)
                v.tensor_tensor(chosen[:].rearrange("p k t e -> p (k t) e"),
                                cf[:, CF_IOTA:CF_IOTA + E].unsqueeze(1).broadcast_to((P, TOPK * QT, E)),
                                idf[:].rearrange("p k t -> p (k t)").unsqueeze(2).broadcast_to((P, TOPK * QT, E)), ALU.is_equal).then_inc(RD.sem, 1)
                passed(v, RD, "chosen", t, lag)
                v.tensor_tensor(hot[:], chosen[:, 0], chosen[:, 1], ALU.add).then_inc(RD.sem, 1)

            def r_second(t, lag):
                t_wait_full(v, t, "r_cnt", lag)
                cnt = tb[bank_of["r_cnt"]][:, 0:(QT + 1) * E].rearrange("p (t e) -> p t e", e=E)
                t_wait_read(v, t, "r_cnt", lag, 1)
                v.tensor_tensor(rank[:], cnt[:, 0:QT, :], base[:].unsqueeze(1).broadcast_to((P, QT, E)), ALU.add).then_inc(RD.sem, 1)
                passed(v, RD, "rank", t, lag)
                v.tensor_tensor(base[:], cnt[:, QT, :], base[:], ALU.add).then_inc(t_free[bank_of["r_cnt"]], 1)
                for k in range(TOPK):
                    last = v.tensor_tensor(picked[:, k], chosen[:, k], rank[:], ALU.mult)
                last.then_inc(RD.sem, 1)
                passed(v, RD, "picked", t, lag)
                v.tensor_reduce(placef[:], picked[:].rearrange("p k t e -> p (k t) e"), AX.X, ALU.add).then_inc(RD.sem, 1)
                passed(v, RD, "placef", t, lag)
                if t.ref - lag >= 1:
                    v.wait_ge(s_rows, t.b(lag) * (16 * TOPK * QT))
                v.tensor_scalar(placeu[:], placef[:], -1.0, None, ALU.add).then_inc(RD.sem, 1)
                v.tensor_scalar(place[:, bass.ds(t.b(lag), 1), :], placef[:].unsqueeze(1), -1.0, None, ALU.add).then_inc(RD.sem, 1)

            def turn(t):
                x, c1, c2, r, x_next = t.on(0), t.on(1), t.on(2), t.on(3), t.on(-1)
                if x:
                    evac_pairs(kt["x"], t, "x_kt0", 0, 0)
                    evac_pairs(qt["x"], t, "x_qt0", 0, 0)
                if c2:
                    evac_pairs(qt["c"], t, "c_m0", 2, 0)
                if c1:
                    c_stats(t, 1)
                for n in range(STEPS):
                    if x:
                        maxes("x", t, 0, n)
                    if r and n == 1:
                        r_first(t, 3)
                    if r and n == 6:
                        r_second(t, 3)
                    if c1 and n == 4:
                        c_xin(t, 1)
                    if c1 and n == 7:
                        weigh("c_xt", nxt, 0, t, 1)
                if x:
                    max_parts("x", t, 0)
                if c1:
                    c_v(t, 1)
                    split_lo("c", t, 1, "k")
                    split_lo("c", t, 1, "q")
                    evac_pairs(kt["c"], t, "c_kt0", 1, 0)
                    evac_pairs(qt["c"], t, "c_qt0", 1, 0)
                if x:
                    evac_pairs(qt["x"], t, "x_m0", 0, 0)
                for n in range(STEPS):
                    if c1:
                        maxes("c", t, 1, n)
                    if x_next and n == 0:
                        stats("x", t, -1)
                    if c2 and n == 2:
                        normalize("c", t, 2)
                    if x_next and n == 4:
                        x_q(t, -1)
                    if x_next and n == 9:
                        split_lo("x", t, -1, "k")
                        split_lo("x", t, -1, "q")
                    if c2 and n == 10:
                        c_xp(t, 2)
                    if c2 and n == 13:
                        c_xh2(t, 2)
                if c1:
                    max_parts("c", t, 1)
                if c2:
                    weigh("c_nt", n2, 2, t, 2)
                if x:
                    normalize("x", t, 0)

            run_turns(v, turn, lambda t: (stats("x", t, 0), x_q(t, 0), split_lo("x", t, 0, "k"), split_lo("x", t, 0, "q")))

        @block.tensor
        def _(pe):
            idb = cb[:, CB_ID:CB_ID + P]
            idf = cf[:, CF_ID:CF_ID + P]
            ones3 = cb[0:3, CB_ONE:CB_ONE + P]
            pe.wait_ge(s_load, 16 * n_load)
            pe.wait_ge(s_set, 3)

            def pairs(src, t, name, lag, half, waits):
                waits()
                t_wait_free(pe, t, name, lag)
                dst = tb[bank_of[name]][:].bitcast(BF16).rearrange("p (g s) -> p g s", g=4)
                for g in range(4):
                    for tt in range(QT):
                        pair = 4 * half + g
                        last = pe.transpose(dst[:, g, tt * P:(tt + 1) * P],
                                            src[:, tt, 2 * pair:2 * pair + 2, :].rearrange("p h r -> p (h r)"), idb)
                last.then_inc(t_full[bank_of[name]], 1)

            def k_pairs(k, t, lag):
                passed(pe, DVE_SPLIT[k], "klo", t, lag)
                passed(pe, POOL_SPLIT[k], "kext" if k == "x" else "khi2", t, lag)
                for half in range(2):
                    pairs(ks[k], t, f"{k}_kt{half}", lag, half, lambda: None)

            def q_pairs(k, t, lag):
                passed(pe, DVE_SPLIT[k], "qlo", t, lag)
                passed(pe, POOL_SPLIT[k], "qhi2", t, lag)
                for half in range(2):
                    pairs(qs[k], t, f"{k}_qt{half}", lag, half, lambda: None)

            def m_pairs(k, t, lag):
                passed(pe, DVE_MAX[k], "m_lo", t, lag)
                for half in range(2):
                    pairs(qs[k], t, f"{k}_m{half}", lag, half, lambda: None)

            def s1_step(k, t, lag, n):
                qq, g = n // GROUPS, n % GROUPS
                c = ring(S1_TAB, t, k, lag, n)
                if n == 0:
                    for w in ("qt0", "qt1"):
                        t_wait_read(pe, t, f"{k}_{w}", lag)
                wait(pe, s1_free, c - 1)
                out = s1[n % 2]
                r0 = HB * (g % 2)
                if k == "c":
                    cols = slice(qq * P, (qq + 1) * P)
                    pe.matmul(out[:, :, cols], idb, cb[:, CB_MQ:CB_MQ + 2 * P].rearrange("p (h s) -> p h s", h=2), start=True, stop=False)
                for j, h in enumerate(heads(g)):
                    q = qt[k][r0:r0 + 52, h // 2, qq * P:(qq + 1) * P]
                    for kk in range(QT):
                        if k == "c" and kk > qq:
                            continue
                        ks_ = slice(kk * P, (kk + 1) * P)
                        if k == "x":
                            if kk == 0:
                                last = pe.matmul(out[:, j, :], q, kt[k][r0:r0 + 52, h // 2, :], start=True, stop=True)
                        else:
                            last = pe.matmul(out[:, j, ks_], q, kt[k][r0:r0 + 52, h // 2, ks_], start=False, stop=j == 1 and kk == qq)
                last.then_inc(s1_full, 1)

            def s2_step(k, t, lag, n):
                g, kk = n // 2, n % 2
                c = ring(S2_TAB, t, k, lag, n)
                if n == 0:
                    t_wait_read(pe, t, f"{k}_m0", lag)
                    t_wait_read(pe, t, f"{k}_m1", lag)
                wait(pe, p_full, c - 1)
                out = s2[n % 2]
                r0 = HB * (g % 2)
                if k == "c":
                    pe.matmul(out[:, :, kk * P:(kk + 1) * P], idb, cb[:, CB_MK:CB_MK + 2 * P].rearrange("p (h s) -> p h s", h=2),
                              start=True, stop=False)
                for j, h in enumerate(heads(g)):
                    key = kt[k][r0:r0 + HB, h // 2, kk * P:(kk + 1) * P]
                    if k == "x":
                        last = pe.matmul(out[:, j, :], key, qt[k][r0:r0 + HB, h // 2, :], start=True, stop=True)
                    else:
                        for qq in range(kk, QT):
                            qs_ = slice(qq * P, (qq + 1) * P)
                            last = pe.matmul(out[:, j, qs_], key, qt[k][r0:r0 + HB, h // 2, qs_], start=False, stop=j == 1 and qq == QT - 1)
                last.then_inc(s2_full, 1)

            def pv_step(k, t, lag, n):
                g, kk = n // 2, n % 2
                c = ring(S2_TAB, t, k, lag, n)
                pe.wait_ge(p_full, c + 1)
                if n == 0:
                    if k == "x":
                        passed(pe, XP1, "v", t, lag)
                    else:
                        t_wait_read(pe, t, "c_v", lag)
                    wait(pe, o_free, o_count(t, k, lag))
                lo = P if k == "c" and kk else 0
                for j, h in enumerate(heads(g)):
                    col = 32 * (h % 4)
                    last = pe.matmul(ob[col:col + 32, h // 4, lo:S], v1[k][:, kk, h, :], prob[:, n % NPT, j, lo:S],
                                     start=kk == 0, stop=kk == 1)
                last.then_inc(p_free, 1)

            def back(k, t, lag):
                pe.wait_ge(o_free, o_count(t, k, lag) + 1)
                for qq in range(QT):
                    name = f"{k}_back{qq}"
                    t_wait_free(pe, t, name, lag)
                    for j in range(4):
                        last = pe.transpose(tb[bank_of[name]][:, j * P:(j + 1) * P], ot[k][:, j, qq * P:(qq + 1) * P], idf)
                    last.then_inc(t_full[bank_of[name]], 1)

            def turn_over(src, t, name, lag, waits):
                waits()
                t_wait_free(pe, t, name, lag)
                for k in range(KD):
                    for tt in range(QT):
                        last = pe.transpose(tb[bank_of[name]][:, k * S + tt * P:k * S + (tt + 1) * P], src[:, tt, k * P:(k + 1) * P], idf)
                last.then_inc(t_full[bank_of[name]], 1)

            def project(t, name, lag, out, lhs, w, tt, lo, n, row):
                for k in range(KD):
                    pe.matmul(out, lhs[:, k, tt * P:(tt + 1) * P], w[:, k, lo:lo + n], start=k == 0, stop=False)
                return pe.matmul(out, ones3, rows[:, row:row + n], start=False, stop=True)

            def c_qk(t, lag, tt):
                name = f"c_qk{tt}"
                if tt == 0:
                    t_wait_read(pe, t, "c_xt", lag)
                t_wait_free(pe, t, name, lag)
                project(t, name, lag, tb[bank_of[name]][:, 0:2 * D], nxt, wqkv, tt, 0, 2 * D, RW_QKV).then_inc(t_full[bank_of[name]], 1)

            def c_v(t, lag):
                t_wait_free(pe, t, "c_v", lag)
                for tt in range(QT):
                    last = project(t, "c_v", lag, tb[bank_of["c_v"]][:, tt * D:(tt + 1) * D], nxt, wqkv, tt, 2 * D, D, RW_QKV + 2 * D)
                last.then_inc(t_full[bank_of["c_v"]], 1)

            def c_wo(t, lag):
                t_wait_read(pe, t, "c_at", lag)
                t_wait_free(pe, t, "c_wo", lag)
                for tt in range(QT):
                    last = project(t, "c_wo", lag, tb[bank_of["c_wo"]][:, tt * D:(tt + 1) * D], at, wo, tt, 0, D, RW_O)
                last.then_inc(t_full[bank_of["c_wo"]], 1)

            def c_gate(t, lag):
                t_wait_read(pe, t, "c_nt", lag)
                t_wait_free(pe, t, "c_gate", lag)
                for tt in range(QT):
                    for k in range(KD):
                        last = pe.matmul(tb[bank_of["c_gate"]][:, tt * E:(tt + 1) * E], n2[:, k, tt * P:(tt + 1) * P], wgate[:, k, :],
                                         start=k == 0, stop=k == KD - 1)
                last.then_inc(t_full[bank_of["c_gate"]], 1)

            def r_count(t, lag):
                passed(pe, RD, "hot", t, lag)
                t_wait_free(pe, t, "r_cnt", lag)
                tri, one = cb[:, CB_TRI:CB_TRI + P], cb[:, CB_ONE:CB_ONE + P]
                out = tb[bank_of["r_cnt"]]
                pe.matmul(out[:, 0:E], tri, hot[:, 0, :], start=True, stop=True)
                pe.matmul(out[:, E:2 * E], one, hot[:, 0, :], start=True, stop=False)
                pe.matmul(out[:, E:2 * E], tri, hot[:, 1, :], start=False, stop=True)
                pe.matmul(out[:, 2 * E:3 * E], one, hot[:, 0, :], start=True, stop=False)
                pe.matmul(out[:, 2 * E:3 * E], one, hot[:, 1, :], start=False, stop=True).then_inc(t_full[bank_of["r_cnt"]], 1)

            def turn(t):
                x, c1, c2 = t.on(0), t.on(1), t.on(2)
                if x:
                    k_pairs("x", t, 0)
                    q_pairs("x", t, 0)
                if c2:
                    m_pairs("c", t, 2)
                for n in range(STEPS):
                    if x:
                        s1_step("x", t, 0, n)
                    if c2:
                        s2_step("c", t, 2, n)
                        if n >= 1:
                            pv_step("c", t, 2, n - 1)
                    if t.on(3) and n == 4:
                        r_count(t, 3)
                    if c1 and n == 6:
                        turn_over(xh, t, "c_xt", 1, lambda: passed(pe, CD1, "xh", t, 1))
                    if c1 and n == 9:
                        c_qk(t, 1, 0)
                if c2:
                    pv_step("c", t, 2, STEPS - 1)
                if c1:
                    c_v(t, 1)
                    c_qk(t, 1, 1)
                    k_pairs("c", t, 1)
                    q_pairs("c", t, 1)
                if x:
                    m_pairs("x", t, 0)
                for n in range(STEPS):
                    if c1:
                        s1_step("c", t, 1, n)
                    if x:
                        s2_step("x", t, 0, n)
                        if n >= 1:
                            pv_step("x", t, 0, n - 1)
                    if c2 and n == 1:
                        back("c", t, 2)
                    if c2 and n == 5:
                        turn_over(att["c"], t, "c_at", 2, lambda: (t_wait_read(pe, t, "c_back1", 2), t_wait_read(pe, t, "c_back0", 2)))
                    if c2 and n == 8:
                        c_wo(t, 2)
                if x:
                    pv_step("x", t, 0, STEPS - 1)
                if c2:
                    turn_over(xh2, t, "c_nt", 2, lambda: passed(pe, CD2, "xh2", t, 2))
                    c_gate(t, 2)
                if x:
                    back("x", t, 0)

            run_turns(pe, turn, lambda t: None)


def run_turns(eng, turn, first):
    first(Turn(0))
    for i in range(LAGS + 1):
        turn(Turn(i))
    with eng.Fori(LAGS + 1, B - 1) as i:
        turn(Turn(i, LAGS + 1))
    for i in range(B - 1, B + LAGS):
        turn(Turn(i))


def setup_phase(nc, io, keep, sem):
    cf, cb, rows, res = keep["cf"], keep["cb"], keep["rows"], keep["res"]
    kext, any4, kq, bounds = keep["kext"], keep["any4"], keep["kq"], keep["bounds"]
    with ExitStack() as ctx:
        def sb(name, shape, dt=F32):
            return ctx.enter_context(nc.sbuf_tensor(name, shape, dt))

        rows_f, rows_r = sb("rows_f", [3, RW_N]), sb("rows_r", [3, RW_N])
        rows_m = sb("rows_m", [3, RW_N], BF16)
        seq_i, seq_f = sb("seq_i", [P, B], I32), sb("seq_f", [P, B])
        any_f = sb("any_f", [P, B])
        bcol, bpf, bres = sb("bcol", [P, QT]), sb("bpf", [P, 3, QT]), sb("bres", [P, QT])
        bpart = sb("bpart", [P, 3, QT], BF16)
        msk = sb("msk", [P, QT, B])
        scales = sb("scales", [P, 2])
        rscale = sb("rscale", [P, 2])
        kw = sb("kw", [P, KD, D], BF16)
        kwf, kexp, kbig, ksum = sb("kwf", [P, KD, D]), sb("kexp", [P, KD, D]), sb("kbig", [P, KD, D]), sb("ksum", [P, KD, D])
        len_i, len_f = sb("len_i", [P, QT, B], I32), sb("len_f", [P, QT, B])
        ginit = sb("ginit", [P, D])
        ends = ctx.enter_context(nc.psum_tensor("ends", [P, QT, B], F32))
        s_load, s_dve, s_ends = sem("setup_load"), sem("setup_dve"), sem("setup_ends")
        loads = (
            (cf[:], io["cf"]), (cb[:], io["cb"]),
            (rows_f[:], io["rows"]), (seq_i[:], io["seq"].partition_broadcast(P)),
            (bcol[:], io["b"]),
            (scales[:, 0:1], io["s_in"].partition_broadcast(P)), (scales[:, 1:2], io["s_k"].partition_broadcast(P)),
            (kw[:], io["kern"].rearrange("(k p) n -> p k n", p=P)),
            (len_i[:], io["lens"]),
            (ginit[:], io["ginit"].partition_broadcast(P)),
            (keep["bias"][:], io["bias"].partition_broadcast(P)),
            (keep["lncol"][:], io["lncol"]),
            (res[:], io["x"].rearrange("b (t p) d -> p (b t) d", p=P)),
        )
        block = ctx.enter_context(nc.Block())

        @block.sync
        def _(sp):
            for dst, src in loads:
                sp.dma_start(dst, src).then_inc(s_load, 16)
            sp.wait_ge(s_load, 16 * len(loads))

        @block.tensor
        def _(pe):
            pe.wait_ge(s_dve, 1)
            tri, one = cf[:, CF_TRI:CF_TRI + P], cf[:, CF_ONE:CF_ONE + P]
            pe.matmul(ends[:, 0, :], tri, len_f[:, 0, :], start=True, stop=True)
            pe.matmul(ends[:, 1, :], one, len_f[:, 0, :], start=True, stop=False)
            pe.matmul(ends[:, 1, :], tri, len_f[:, 1, :], start=False, stop=True).then_inc(s_ends, 1)

        @block.vector
        def _(v):
            count = [0]

            def after(ins):
                count[0] += 1
                ins.then_inc(s_dve, 1)
                v.wait_ge(s_dve, count[0])

            v.wait_ge(s_load, 16 * len(loads))
            after(v.tensor_copy(len_f[:], len_i[:]))
            after(v.tensor_copy(seq_f[:], seq_i[:]))
            after(v.tensor_scalar(any4[:], seq_f[:], 0.0, DH ** -0.5, ALU.is_gt, ALU.mult))
            after(v.tensor_scalar(any_f[:], seq_f[:], 0.0, None, ALU.is_gt))
            after(v.tensor_copy(bpart[:, 0, :], bcol[:]))
            after(v.tensor_tensor(bres[:], bcol[:], bpart[:, 0, :], ALU.subtract))
            after(v.tensor_copy(bpart[:, 1, :], bres[:]))
            after(v.tensor_tensor(bpart[:, 2, :], bres[:], bpart[:, 1, :], ALU.subtract))
            after(v.tensor_copy(bpf[:], bpart[:]))
            for tt in range(QT):
                after(v.tensor_scalar(msk[:, tt, :], seq_f[:], cf[:, CF_ROW + tt:CF_ROW + tt + 1], NEG_BIG, ALU.is_le, ALU.mult))
                for part in range(3):
                    after(v.tensor_scalar(kext[:, :, tt, part], any_f[:], bpf[:, part, tt:tt + 1], None, ALU.mult))
                after(v.tensor_tensor(kext[:, :, tt, 3], msk[:, tt, :], any_f[:], ALU.mult))
            sel = [cf[0:3, CF_ID + p:CF_ID + p + 1] for p in range(3)]
            after(v.tensor_copy(rows_m[:], rows_f[:]))
            after(v.tensor_scalar(rows[:], rows_m[:], sel[0], None, ALU.mult))
            after(v.tensor_tensor(rows_r[:], rows_f[:], rows_m[:], ALU.subtract))
            after(v.tensor_copy(rows_m[:], rows_r[:]))
            after(v.scalar_tensor_tensor(out=rows[:], in0=rows_m[:], scalar=sel[1], in1=rows[:], op0=ALU.mult, op1=ALU.add))
            after(v.tensor_tensor(rows_r[:], rows_r[:], rows_m[:], ALU.subtract))
            after(v.scalar_tensor_tensor(out=rows[:], in0=rows_r[:], scalar=sel[2], in1=rows[:], op0=ALU.mult, op1=ALU.add))
            after(v.tensor_copy(keep["base"][:], cf[:, CF_REG:CF_REG + E]))
            after(v.reciprocal(rscale[:], scales[:]))
            after(v.tensor_copy(keep["r_in"][:], rscale[:, 0:1]))
            after(v.tensor_tensor(keep["s_out"][:], scales[:, 0:1], scales[:, 1:2], ALU.mult))
            after(v.tensor_scalar(kwf[:], kw[:], rscale[:, 1:2], None, ALU.mult))
            after(v.tensor_single_scalar(kexp[:].bitcast(I32), kwf[:].bitcast(I32), 0x7F800000, op=ALU.bitwise_and))
            after(v.tensor_scalar(kbig[:], kexp[:], 2.0 ** -6, C20, ALU.max, ALU.mult))
            after(v.tensor_tensor(ksum[:], kwf[:], kbig[:], ALU.add))
            after(v.tensor_tensor(kq[:], ksum[:], kbig[:], ALU.subtract))
            after(v.tensor_scalar(keep["ginit"][:], ginit[:], math.exp(-PATCH_EPS), None, ALU.mult))
            v.wait_ge(s_ends, 1)
            after(v.tensor_scalar(bounds[:, 0], ends[:], -1.0, None, ALU.add))
            after(v.tensor_scalar(bounds[:, 1], ends[:], -1.0 + S, None, ALU.add))


def expert_phase(nc, io, keep, sem):
    cf, cb, rows, lncol, base, xs, ys = (keep[n] for n in ("cf", "cb", "rows", "lncol", "base", "xs", "ys"))
    NH = 4
    CHUNK = F
    PARTS = (KD * F + FT * D) // CHUNK
    PEEL = 3
    with ExitStack() as ctx:
        def sb(name, shape, dt=F32):
            return ctx.enter_context(nc.sbuf_tensor(name, shape, dt))

        wf = sb("wf", [P, CHUNK])
        w1 = [sb(f"w1_{p}", [P, E, KD, F], BF16) for p in "hl"]
        w2 = [sb(f"w2_{p}", [P, E, FT, D], BF16) for p in "hl"]
        b1 = sb("b1", [P, E * FT])
        eg, den = sb("eg", [P, NT]), sb("den", [P, NT])
        fill, tiles_i, tiles, ends, starts = sb("region_fill", [P, E]), sb("tiles_i", [P, E], I32), sb("tiles", [P, E]), sb("tile_ends", [P, E]), sb("starts", [P, E + 1])
        one8, shift = sb("one8", [P, E]), sb("shift", [P, E])
        ex, is_ex, ex7, row = sb("ex", [1, NTILE]), sb("is_ex", [1, NTILE, E + 1]), sb("ex7", [1, NTILE], U32), sb("row", [1, NTILE])
        ended = is_ex[:, :, 0:E]
        row_u, pad_u = sb("row_u", [1, NTILE], U32), sb("pad_u", [1, E], U32)
        zeros = sb("zeros", [P, D])
        xt = [sb(f"xt{n}", [P, ST, D]) for n in range(2)]
        nf = sb("nf", [P, KD, SLOTS])
        move, moved = (nf[:, n, 0:B * TOPK * QT] for n in range(2))
        nx = [sb(f"nx_{p}", [P, KD, SLOTS], BF16) for p in "hl"]
        hf = sb("hf", [P, NH, SLOTS])
        hid = [sb(f"hid_{p}", [P, FT, SLOTS], BF16) for p in "hl"]
        yt = [sb(f"yt{n}", [P, ST, D]) for n in range(2)]
        pt = ctx.enter_context(nc.psum_tensor("pt", [P, KD, SLOTS], F32))
        hb = [ctx.enter_context(nc.psum_tensor(f"hb{n}", [P, 512], F32)) for n in range(NH)]
        yb = [ctx.enter_context(nc.psum_tensor(f"yb{n}", [P, 512], F32)) for n in range(ST)]

        s_b1, s_w, s_split, s_zero, s_padded = sem("b1_load"), sem("w_load"), sem("w_split"), sem("zeros_set"), sem("rows_padded")
        s_gate, s_eg, s_tab = sem("gate_dve"), sem("gate_exp"), sem("tile_table")
        s_xt, s_t, s_nf, s_nh, s_nl = [sem(f"x_tile{n}") for n in range(2)], sem("x_turned"), sem("x_weighed"), sem("x_high"), sem("x_low")
        s_h, s_gelu, s_hi, s_lo = sem("h_full"), sem("gelu"), sem("h_high"), sem("h_low")
        s_y, s_yt, s_out = sem("y_full"), sem("y_read"), [sem(f"y_stored{n}") for n in range(2)]
        s_seen_pe, s_w_seen = sem("e_seen_pe"), sem("e_seen_pool")
        block = ctx.enter_context(nc.Block())

        def wait(eng, s, value):
            if not isinstance(value, int) or value > 0:
                eng.wait_ge(s, value)

        def tiles_loop(eng, body):
            for j in range(PEEL):
                body(j, j % 2, j // 2)
            with eng.Fori(0, (NTILE - PEEL) // 2) as m:
                for k in range(2):
                    body(m * 2 + (PEEL + k), (PEEL + k) % 2, m + (PEEL + k) // 2)
            assert (NTILE - PEEL) % 2 == 0

        def rows_of(a, r, n):
            return a[bass.ds(r, n), :].rearrange("(s p) d -> p s d", p=P)

        @block.sync
        def _(sp):
            sp.dma_start(b1[:], io["fc1b"]).then_inc(s_b1, 16)
            sp.wait_ge(s_zero, 1)
            for n in range(0, NTILE - TOPK * B * S // SLOTS):
                sp.dma_start(rows_of(xs, E * REGION + n * SLOTS, SLOTS), zeros[:].unsqueeze(1).broadcast_to((P, ST, D))).then_inc(s_padded, 16)
            sp.wait_ge(s_tab, 20)
            for e in range(E):
                r = sp.value_load(pad_u[0:1, e:e + 1], min_val=e * REGION, max_val=e * REGION + B * S)
                sp.dma_start(rows_of(xs, r, SLOTS), zeros[:].unsqueeze(1).broadcast_to((P, ST, D))).then_inc(s_padded, 16)
            sp.wait_ge(s_padded, 16 * (E + NTILE - TOPK * B * S // SLOTS))

            def load_x(j, n, h):
                r = sp.value_load(row_u[0:1, bass.ds(j, 1)], min_val=0, max_val=NROWS - SLOTS)
                wait(sp, s_t, j - 1)
                sp.dma_start(xt[n][:], rows_of(xs, r, SLOTS)).then_inc(s_xt[n], 16)

            tiles_loop(sp, load_x)
            for n in range(2):
                sp.wait_ge(s_out[n], 16 * ((NTILE + 1 - n) // 2))

        @block.gpsimd
        def _(pool):
            pool.memset(zeros[:], 0.0).then_inc(s_zero, 1)

            def split_weights(e, first):
                one = bass.ds(e, 1)
                parts = [(io["fc1"][one, k * P:(k + 1) * P, :].rearrange("o p f -> p (o f)"), [w[:, one, k, :] for w in w1]) for k in range(KD)]
                rows_each = FT // (PARTS - KD)
                for n in range(0, FT, rows_each):
                    parts.append((io["fc2"][one, n * P:(n + rows_each) * P, :].rearrange("o (k p) d -> p (o k) d", p=P),
                                  [w[:, one, n:n + rows_each, :] for w in w2]))
                for n, (src, (high, low)) in enumerate(parts):
                    done = e * (2 * PARTS) + 2 * n
                    dst, got = wf[:], wf[:].unsqueeze(1)
                    if n >= KD:
                        dst, got = dst.rearrange("p (k d) -> p k d", d=D), got.rearrange("p o (k d) -> p o k d", d=D)
                    if not first or n > 0:
                        pool.wait_ge(s_split, done)
                        pool.sem_inc(s_w_seen, 1)
                    pool.dma_start(dst, src).then_inc(s_w, 16)
                    pool.wait_ge(s_w, e * (16 * PARTS) + 16 * (n + 1))
                    pool.sem_inc(s_w_seen, 1)
                    pool.tensor_copy(high, got).then_inc(s_split, 1)
                    pool.wait_ge(s_split, done + 1)
                    pool.sem_inc(s_w_seen, 1)
                    pool.tensor_tensor(low, got, high, ALU.subtract).then_inc(s_split, 1)

            split_weights(0, True)
            with pool.Fori(1, E) as e:
                split_weights(e, False)

        @block.scalar
        def _(act):
            act.activation(eg[:], keep["gap"][:], ACT.Exp).then_inc(s_eg, 1)
            act.wait_ge(s_b1, 16)

            def body(j, n, h):
                act.wait_ge(s_nf, j + 1)
                act.activation(nx[0][:], nf[:], ACT.Copy).then_inc(s_nh, 1)
                act.wait_ge(s_tab, 20)
                e = act.value_load(ex7[0:1, bass.ds(j, 1)], min_val=0, max_val=E - 1)
                for f in range(FT):
                    act.wait_ge(s_h, j * FT + f + 1)
                    wait(act, s_lo, j * FT + f + 1 - NH)
                    act.activation(hf[:, f % NH, :], hb[f % NH][:, 0:SLOTS], ACT.Gelu, bias=b1[:, bass.ds(e * FT + f, 1)]).then_inc(s_gelu, 1)
                wait(act, s_out[n], h * 16)
                for k in range(ST):
                    act.wait_ge(s_y, j * ST + k + 1)
                    act.activation(yt[n][:, k, :], yb[k][:, 0:D], ACT.Copy).then_inc(s_yt, 1)
                act.wait_ge(s_yt, j * ST + ST)
                act.dma_start(rows_of(ys, j * SLOTS, SLOTS), yt[n][:]).then_inc(s_out[n], 16)

            tiles_loop(act, body)

        @block.vector
        def _(v):
            count = [0]

            def after(ins):
                count[0] += 1
                ins.then_inc(s_tab, 1)
                v.wait_ge(s_tab, count[0])

            after(v.memset(one8[:], 1.0))
            after(v.tensor_tensor(fill[:], base[:], cf[:, CF_REG:CF_REG + E], ALU.subtract))
            after(v.tensor_copy(pad_u[:], base[0:1, :]))
            after(v.tensor_scalar(tiles_i[:], fill[:], float(SLOTS - 1), None, ALU.add))
            after(v.tensor_single_scalar(tiles_i[:], tiles_i[:], SLOTS.bit_length() - 1, op=ALU.arith_shift_right))
            after(v.tensor_copy(tiles[:], tiles_i[:]))
            after(v.tensor_tensor_scan(ends[:], one8[:], tiles[:], 0.0, ALU.mult, ALU.add))
            after(v.tensor_copy(starts[:, 0:1], cf[:, CF_REG:CF_REG + 1]))
            after(v.scalar_tensor_tensor(out=starts[:, 1:E + 1], in0=ends[:], scalar=-float(SLOTS), in1=cf[:, CF_REG + 1:CF_REG + E + 1],
                                         op0=ALU.mult, op1=ALU.add))
            number = cf[0:1, CF_IOTA:CF_IOTA + NTILE]
            after(v.tensor_tensor(ended, number.unsqueeze(2).broadcast_to((1, NTILE, E)),
                                  ends[0:1, :].unsqueeze(1).broadcast_to((1, NTILE, E)), ALU.is_ge))
            after(v.tensor_reduce(ex[:], ended, AX.X, ALU.add))
            after(v.tensor_tensor(is_ex[:], cf[0:1, CF_IOTA:CF_IOTA + E + 1].unsqueeze(1).broadcast_to((1, NTILE, E + 1)),
                                  ex[:].unsqueeze(2).broadcast_to((1, NTILE, E + 1)), ALU.is_equal))
            after(v.tensor_tensor(is_ex[:], is_ex[:], starts[0:1, :].unsqueeze(1).broadcast_to((1, NTILE, E + 1)), ALU.mult))
            after(v.tensor_reduce(row[:], is_ex[:], AX.X, ALU.add))
            after(v.scalar_tensor_tensor(out=row[:], in0=number, scalar=float(SLOTS), in1=row[:], op0=ALU.mult, op1=ALU.add))
            after(v.tensor_copy(row_u[:], row[:]))
            after(v.tensor_scalar(ex7[:], ex[:], float(E - 1), None, ALU.min))
            v.wait_ge(s_eg, 1)
            after(v.tensor_scalar(den[:], eg[:], 1.0, None, ALU.add))
            after(v.reciprocal(keep["g1"][:], den[:]))
            after(v.tensor_tensor(keep["g2"][:], eg[:], keep["g1"][:], ALU.mult))
            assert count[0] == 20
            place = keep["place"][:].rearrange("p b n -> p (b n)")
            after(v.tensor_scalar(shift[:], tiles[:], float(SLOTS), -float(REGION), ALU.mult, ALU.add))
            after(v.tensor_copy(moved, place))
            for e in range(1, E):
                after(v.tensor_scalar(move, place, float(e * REGION), shift[:, e - 1:e], ALU.is_ge, ALU.mult))
                after(v.tensor_tensor(moved, moved, move, ALU.add))
            after(v.tensor_copy(keep["place_y"][:].rearrange("p b n -> p (b n)"), moved))

            def weigh(j):
                v.wait_ge(s_t, j + 1)
                for k in range(KD):
                    last = v.tensor_scalar(nf[:, k, :], pt[:, k, :], lncol[:, 2, k:k + 1], lncol[:, 3, k:k + 1], ALU.mult, ALU.add)
                last.then_inc(s_nf, 1)
                v.wait_ge(s_nh, j + 1)
                v.tensor_tensor(nx[1][:], nf[:], nx[0][:], ALU.subtract).then_inc(s_nl, 1)

            def body(j, n, h):
                weigh(j)
                wait(v, s_y, j * ST)
                for f in range(FT + 1):
                    if f < FT:
                        v.wait_ge(s_gelu, j * FT + f + 1)
                        v.tensor_copy(hid[0][:, f, :], hf[:, f % NH, :]).then_inc(s_hi, 1)
                    if f >= 1:
                        v.wait_ge(s_hi, j * FT + f)
                        v.tensor_tensor(hid[1][:, f - 1, :], hf[:, (f - 1) % NH, :], hid[0][:, f - 1, :], ALU.subtract).then_inc(s_lo, 1)

            tiles_loop(v, body)

        @block.tensor
        def _(pe):
            ones3, idf = cb[0:3, CB_ONE:CB_ONE + P], cf[:, CF_ID:CF_ID + P]

            def turn_tile(j, n, h):
                pe.wait_ge(s_xt[n], h * 16 + 16)
                wait(pe, s_nf, j)
                for k in range(KD):
                    for s in range(ST):
                        last = pe.transpose(pt[:, k, s * P:(s + 1) * P], xt[n][:, s, k * P:(k + 1) * P], idf)
                last.then_inc(s_t, 1)

            pe.wait_ge(s_tab, 20)

            def body(j, n, h):
                e = pe.value_load(ex7[0:1, bass.ds(j, 1)], min_val=0, max_val=E - 1)
                one = bass.ds(e, 1)
                turn_tile(j, n, h)
                pe.wait_ge(s_split, (e + 1) * (2 * PARTS))
                pe.sem_inc(s_seen_pe, 1)
                pe.wait_ge(s_nl, j + 1)
                for f in range(FT):
                    wait(pe, s_gelu, j * FT + f + 1 - NH)
                    i = 0
                    for k in range(KD):
                        for wp, xp in ((0, 0), (0, 1), (1, 0)):
                            last = pe.matmul(hb[f % NH][:, 0:SLOTS], w1[wp][:, one, k, f * P:(f + 1) * P].rearrange("p o f -> p (o f)"),
                                             nx[xp][:, k, :], start=i == 0, stop=i == 3 * KD - 1)
                            i += 1
                    last.then_inc(s_h, 1)
                for k in range(ST):
                    wait(pe, s_yt, (j - 1) * ST + k + 1)
                    out = yb[k][:, 0:D]
                    pe.sem_inc(s_seen_pe, 1)
                    pe.matmul(out, ones3, rows[:, bass.ds(e * D + RW_FC2, D)], start=True, stop=False)
                    for f in range(FT):
                        if k == 0:
                            pe.wait_ge(s_lo, j * FT + f + 1)
                        for hp, wp in ((0, 0), (0, 1), (1, 0)):
                            last = pe.matmul(out, hid[hp][:, f, k * P:(k + 1) * P],
                                             w2[wp][:, one, f, :].rearrange("p o d -> p (o d)"), start=False, stop=f == FT - 1 and hp == 1)
                    last.then_inc(s_y, 1)

            tiles_loop(pe, body)


def last_phase(nc, io, keep, sem):
    res, cf, cb, rows, bounds, kq, lncol = (keep[n] for n in ("res", "cf", "cb", "rows", "bounds", "kq", "lncol"))
    with ExitStack() as ctx:
        def sb(name, shape, dt=F32):
            return ctx.enter_context(nc.sbuf_tensor(name, shape, dt))

        win = sb("win", [P, KD, D])
        where = sb("where", [P, TOPK * QT], U32)
        yg = sb("yg", [P, TOPK, QT, D])
        ones = sb("ones", [P, S])
        halfneg = sb("halfneg_c", [P, QT])
        cx, junk = sb("cx", [P, QT, DC]), sb("junk", [P, QT, DC])
        ss, ra = sb("ss", [P, QT]), sb("ra", [P, 2, QT])
        u = sb("u", [P, 2, QT, D])
        eq, bnd_in = sb("eq", [P, QT, S]), sb("bnd_in", [P, QT, S], BF16)
        bnd, cum, plug = sb("bnd", [P, S]), sb("cum", [P, S]), sb("plug", [P, S])
        take = sb("take", [P, QT, S])
        mt = sb("mt", [P, QT, S])
        sth, mvh, rh = sb("sth", [P, QT, 6]), sb("mvh", [P, QT, 2]), sb("rh", [P, 7, QT])
        xh, nt = sb("xh_c", [P, QT, D]), sb("nt", [P, KD, S])
        x3 = sb("x3", [P, 2, QT, D])
        stq, mvq, rq = sb("stq", [P, QT, 6]), sb("mvq", [P, QT, 2]), sb("rq", [P, 2, QT])
        xb = sb("xb", [P, QT, D], BF16)
        qv, qe, qb, qsum = (sb(n, [P, QT, D]) for n in ("qv", "qe", "qb", "qsum"))
        qq = sb("qq", [P, QT, D], BF16)
        qt = sb("qt", [P, KD, S], BF16)
        y, ybias = sb("y", [P, QT, D], BF16), sb("ybias", [P, QT, D], BF16)
        out = sb("out_t", [P, QT, D])
        p_cnt, p_mt, p_t, p_h, p_q, p_y = (ctx.enter_context(nc.psum_tensor(n, [P, 512], F32)) for n in ("p_cnt", "p_mt", "p_t", "p_h", "p_q", "p_y"))

        s_load, s_cx, s_set, s_out = sem("l_load"), sem("l_ctx"), sem("l_set"), sem("l_out")
        s_seen = {e.engine: sem(f"l_seen_{n}") for e, n in ((nc.gpsimd, "pool"), (nc.vector, "dve"))}
        AD = Steps(sem("a_dve"), "eq bound u bnd cum plug take")
        AP_ = Steps(sem("a_pool"), "ms rms")
        AA = Steps(sem("a_act"), "square mt")
        AE = Steps(sem("a_pe"), "cnt mt")
        HD = Steps(sem("h_dve"), "sum1 sum2 stats aggr xh nt x3")
        GP = Steps(sem("g_pool"), "where")
        s_yg = sem("rows_gathered")
        HP = Steps(sem("h_pool"), "veps r1 r1sq v2 v2eps r2 r12")
        HE = Steps(sem("h_pe"), "t h")
        QD = Steps(sem("q_dve"), "stats aggr xb v exp big sum q")
        QP = Steps(sem("q_pool"), "veps rstd bias out")
        QA = Steps(sem("q_act"), "qt y")
        QE = Steps(sem("q_pe"), "t y")

        def passed(eng, steps, name, t, lag, back=0):
            if t.ref - lag - back >= 0:
                eng.wait_ge(steps.sem, steps.at(name, t.b(lag) - back))
                if t.loop and (eng is nc.gpsimd or name in ("stats", "sum2")):
                    eng.sem_inc(s_seen[eng.engine], 1)

        def parity(b):
            return bass.ds(b % 2, 1)

        block = ctx.enter_context(nc.Block())

        @block.sync
        def _(sp):
            sp.dma_start(win[:], io["win"].rearrange("(k p) n -> p k n", p=P)).then_inc(s_load, 16)

            def turn(t):
                if t.on(0):
                    passed(sp, AD, "u", t, 0, 1)
                    sp.dma_start(cx[:], io["ctx"][bass.ds(t.b(0), 1)].rearrange("o (t p) d -> p (o t) d", p=P)).then_inc(s_cx, 16)
                if t.on(2):
                    passed(sp, QP, "out", t, 2)
                    sp.dma_start(io["out"][bass.ds(t.b(2), 1)].rearrange("o (t p) d -> p (o t) d", p=P), out[:]).then_inc(s_out, 16)

            run_turns(sp, turn, lambda t: None)
            sp.wait_ge(s_out, 16 * B)

        @block.gpsimd
        def _(pool):
            pool.memset(halfneg[:], -0.5)
            pool.memset(ones[:], 1.0).then_inc(s_set, 1)
            pool.wait_ge(s_set, 1)

            def add_eps(dst, src, scale, steps, name):
                pool.tensor_scalar(dst, src, scale, EPS, ALU.mult, ALU.add).then_inc(steps.sem, 1)

            def turn(t):
                if t.on(2):
                    passed(pool, QD, "aggr", t, 2)
                    pool.tensor_scalar(rq[:, 0, :], mvq[:, :, 1], EPS, None, ALU.add).then_inc(QP.sem, 1)
                    passed(pool, QP, "veps", t, 2)
                    pool.tensor_tensor(rq[:, 1, :], rq[:, 0, :], halfneg[:], ALU.pow).then_inc(QP.sem, 1)
                if t.on(1):
                    v = mvh[:, :, 1]
                    passed(pool, HD, "aggr", t, 1)
                    pool.tensor_scalar(rh[:, 0, :], v, EPS, None, ALU.add).then_inc(HP.sem, 1)
                    passed(pool, HP, "veps", t, 1)
                    pool.tensor_tensor(rh[:, 1, :], rh[:, 0, :], halfneg[:], ALU.pow).then_inc(HP.sem, 1)
                    passed(pool, HP, "r1", t, 1)
                    pool.tensor_tensor(rh[:, 2, :], rh[:, 1, :], rh[:, 1, :], ALU.mult).then_inc(HP.sem, 1)
                    passed(pool, HP, "r1sq", t, 1)
                    pool.tensor_tensor(rh[:, 3, :], rh[:, 2, :], v, ALU.mult).then_inc(HP.sem, 1)
                    passed(pool, HP, "v2", t, 1)
                    pool.tensor_scalar(rh[:, 4, :], rh[:, 3, :], EPS, None, ALU.add).then_inc(HP.sem, 1)
                    passed(pool, HP, "v2eps", t, 1)
                    pool.tensor_tensor(rh[:, 5, :], rh[:, 4, :], halfneg[:], ALU.pow).then_inc(HP.sem, 1)
                    passed(pool, HP, "r2", t, 1)
                    pool.tensor_tensor(rh[:, 6, :], rh[:, 5, :], rh[:, 1, :], ALU.mult).then_inc(HP.sem, 1)
                if t.on(0):
                    passed(pool, AA, "square", t, 0)
                    pool.tensor_scalar(ra[:, 0, :], ss[:], 1.0 / DC, EPS, ALU.mult, ALU.add).then_inc(AP_.sem, 1)
                    passed(pool, AP_, "ms", t, 0)
                    pool.tensor_tensor(ra[:, 1, :], ra[:, 0, :], halfneg[:], ALU.pow).then_inc(AP_.sem, 1)
                if t.on(0):
                    if t.ref >= 1:
                        pool.wait_ge(s_yg, t.b(0) * (16 * TOPK * QT))
                        pool.sem_inc(s_seen[pool.engine], 1)
                    pool.tensor_copy(where[:].unsqueeze(1), keep["place_y"][:, bass.ds(t.b(0), 1), :]).then_inc(GP.sem, 1)
                    passed(pool, GP, "where", t, 0)
                    passed(pool, HD, "sum2", t, 0, 1)
                    for k in range(TOPK):
                        for tt in range(QT):
                            n = k * QT + tt
                            pool.indirect_dma_start(yg[:, k, tt, :], None, keep["ys"][:, :], bass.IndirectOffsetOnAxis(where[:, n:n + 1], 0))\
                                .then_inc(s_yg, 16)
                if t.on(2):
                    passed(pool, QA, "y", t, 2)
                    pool.tensor_tensor(ybias[:], y[:], keep["bias"][:].unsqueeze(1).broadcast_to((P, QT, D)), ALU.add).then_inc(QP.sem, 1)
                    passed(pool, QP, "bias", t, 2)
                    if t.ref - 2 >= 1:
                        pool.wait_ge(s_out, t.b(2) * 16)
                    pool.tensor_tensor(out[:].unsqueeze(1), x3[:, parity(t.b(2))], ybias[:].unsqueeze(1), ALU.add).then_inc(QP.sem, 1)

            run_turns(pool, turn, lambda t: None)

        @block.scalar
        def _(act):
            def turn(t):
                if t.on(0):
                    act.wait_ge(s_cx, (t.b(0) + 1) * 16)
                    passed(act, AP_, "ms", t, 0, 1)
                    for tt in range(QT):
                        last = act.activation(junk[:, tt, :], cx[:, tt, :], ACT.Square, accum_out=ss[:, tt:tt + 1])
                    last.then_inc(AA.sem, 1)
                if t.on(2):
                    passed(act, QE, "t", t, 2)
                    act.activation(qt[:].rearrange("p k s -> p (k s)"), p_q[:].bitcast(BF16)[:, 0:2 * S], ACT.Copy).then_inc(QA.sem, 1)
                if t.on(0):
                    passed(act, AE, "mt", t, 0)
                    passed(act, HE, "h", t, 0, 1)
                    act.activation(mt[:].rearrange("p t s -> p (t s)"), p_mt[:], ACT.Copy).then_inc(AA.sem, 1)
                if t.on(2):
                    passed(act, QE, "y", t, 2)
                    passed(act, QP, "bias", t, 2, 1)
                    act.activation(y[:].rearrange("p t d -> p (t d)"), p_y[:], ACT.Copy, scale=keep["s_out"][:, 0:1]).then_inc(QA.sem, 1)

            run_turns(act, turn, lambda t: None)

        @block.vector
        def _(v):
            v.wait_ge(s_set, 1)

            def turn(t):
                a, h, q = t.on(0), t.on(1), t.on(2)
                if q:
                    x3q = x3[:, parity(t.b(2))]
                    passed(v, HD, "x3", t, 2)
                    for tt in range(QT):
                        last = v.bn_stats(stq[:, tt, :], x3q[:, :, tt, :].rearrange("p o d -> p (o d)"))
                    last.then_inc(QD.sem, 1)
                if h:
                    tok = [res[:, bass.ds(t.b(1) * QT + tt, 1), :] for tt in range(QT)]
                    v.wait_ge(s_yg, t.b(0) * (16 * TOPK * QT))
                    for k, g in enumerate((keep["g1"], keep["g2"])):
                        if k == 1:
                            passed(v, HD, "sum1", t, 1)
                        for tt in range(QT):
                            last = v.scalar_tensor_tensor(out=tok[tt], in0=yg[:, k, tt, :].unsqueeze(1), scalar=g[:, bass.ds(t.b(1) * QT + tt, 1)],
                                                          in1=tok[tt], op0=ALU.mult, op1=ALU.add)
                        last.then_inc(HD.sem, 1)
                    passed(v, HD, "sum2", t, 1)
                    for tt in range(QT):
                        last = v.bn_stats(sth[:, tt, :], tok[tt].rearrange("p o d -> p (o d)"))
                    last.then_inc(HD.sem, 1)
                if q:
                    passed(v, QD, "stats", t, 2)
                    for tt in range(QT):
                        last = v.bn_aggr(mvq[:, tt, :], stq[:, tt, :])
                    last.then_inc(QD.sem, 1)
                if h:
                    passed(v, HD, "stats", t, 1)
                    for tt in range(QT):
                        last = v.bn_aggr(mvh[:, tt, :], sth[:, tt, :])
                    last.then_inc(HD.sem, 1)
                if a:
                    iota = cf[:, CF_IOTA:CF_IOTA + S]
                    where = lambda side, tt: bounds[:, side, tt, bass.ds(t.b(0), 1)]
                    passed(v, AE, "cnt", t, 0, 1)
                    for tt in range(QT):
                        last = v.tensor_scalar(eq[:, tt, :], iota, where(0, tt), None, ALU.is_equal)
                    last.then_inc(AD.sem, 1)
                    passed(v, AD, "eq", t, 0)
                    for tt in range(QT):
                        last = v.scalar_tensor_tensor(out=bnd_in[:, tt, :], in0=iota, scalar=where(1, tt), in1=eq[:, tt, :],
                                                      op0=ALU.is_equal, op1=ALU.add)
                    last.then_inc(AD.sem, 1)
                if q:
                    passed(v, QP, "rstd", t, 2)
                    for tt in range(QT):
                        last = v.tensor_scalar(xb[:, tt, :].unsqueeze(1), x3q[:, :, tt, :], mvq[:, tt, 0:1], rq[:, 1, tt:tt + 1], ALU.subtract, ALU.mult)
                    last.then_inc(QD.sem, 1)
                    passed(v, QD, "xb", t, 2)
                    v.tensor_scalar(qv[:], xb[:], keep["r_in"][:, 0:1], None, ALU.mult).then_inc(QD.sem, 1)
                if h:
                    passed(v, HP, "r12", t, 1)
                    passed(v, HE, "t", t, 1, 1)
                    for tt in range(QT):
                        last = v.tensor_scalar(xh[:, tt, :].unsqueeze(1), tok[tt], mvh[:, tt, 0:1], rh[:, 6, tt:tt + 1], ALU.subtract, ALU.mult)
                    last.then_inc(HD.sem, 1)
                if q:
                    passed(v, QD, "v", t, 2)
                    v.tensor_single_scalar(qe[:].bitcast(I32), qv[:].bitcast(I32), 0x7F800000, op=ALU.bitwise_and).then_inc(QD.sem, 1)
                    passed(v, QD, "exp", t, 2)
                    v.tensor_scalar(qb[:], qe[:], 2.0 ** -6, C20, ALU.max, ALU.mult).then_inc(QD.sem, 1)
                    passed(v, QD, "big", t, 2)
                    v.tensor_tensor(qsum[:], qv[:], qb[:], ALU.add).then_inc(QD.sem, 1)
                    passed(v, QD, "sum", t, 2)
                    passed(v, QE, "t", t, 2, 1)
                    v.tensor_tensor(qq[:], qsum[:], qb[:], ALU.subtract).then_inc(QD.sem, 1)
                if a:
                    passed(v, AP_, "rms", t, 0)
                    passed(v, HE, "h", t, 0, 2)
                    for tt in range(QT):
                        last = v.scalar_tensor_tensor(out=u[:, parity(t.b(0)), tt, :].rearrange("p o d -> p (o d)"), in0=cx[:, tt, 0:D],
                                                      scalar=ra[:, 1, tt:tt + 1], in1=keep["ginit"][:], op0=ALU.mult, op1=ALU.mult)
                    last.then_inc(AD.sem, 1)
                    passed(v, AE, "cnt", t, 0)
                    v.tensor_scalar(bnd[:], p_cnt[:, 0:S], 1.0, None, ALU.min).then_inc(AD.sem, 1)
                if h:
                    passed(v, HE, "t", t, 1)
                    pt = p_t[:].rearrange("p (k s) -> p k s", k=KD)
                    for k in range(KD):
                        last = v.tensor_scalar(nt[:, k, :], pt[:, k, :], lncol[:, 4, k:k + 1], None, ALU.mult)
                    last.then_inc(HD.sem, 1)
                if a:
                    passed(v, AD, "bnd", t, 0)
                    v.tensor_tensor_scan(cum[:], ones[:], bnd[:], 0.0, ALU.mult, ALU.add).then_inc(AD.sem, 1)
                    passed(v, AD, "cum", t, 0)
                    v.tensor_scalar(plug[:], cum[:], -1.0, 0.0, ALU.add, ALU.max).then_inc(AD.sem, 1)
                    passed(v, AD, "plug", t, 0)
                    passed(v, AE, "mt", t, 0, 1)
                    for tt in range(QT):
                        last = v.tensor_scalar(take[:, tt, :], plug[:], cf[:, CF_ROW + tt:CF_ROW + tt + 1], None, ALU.is_equal)
                    last.then_inc(AD.sem, 1)
                if h:
                    passed(v, HE, "h", t, 1)
                    passed(v, QP, "out", t, 1, 2)
                    v.tensor_tensor(x3[:, parity(t.b(1))].rearrange("p o t d -> p o (t d)"),
                                    p_h[:].unsqueeze(1),
                                    res[:, bass.ds(t.b(1) * QT, QT), :].rearrange("p t d -> p (t d)").unsqueeze(1), ALU.add).then_inc(HD.sem, 1)

            run_turns(v, turn, lambda t: None)

        @block.tensor
        def _(pe):
            idb, idf = cb[:, CB_ID:CB_ID + P], cf[:, CF_ID:CF_ID + P]
            ones3, onesb = cb[0:3, CB_ONE:CB_ONE + P], cb[:, CB_ONE:CB_ONE + P]
            pe.wait_ge(s_load, 16)

            def turn(t):
                a, h, q = t.on(0), t.on(1), t.on(2)
                if a:
                    passed(pe, AD, "bound", t, 0)
                    passed(pe, AD, "bnd", t, 0, 1)
                    for tt in range(QT):
                        last = pe.matmul(p_cnt[:, 0:S], onesb, bnd_in[:, tt, :], start=tt == 0, stop=tt == QT - 1)
                    last.then_inc(AE.sem, 1)
                if h:
                    passed(pe, HD, "xh", t, 1)
                    passed(pe, HD, "nt", t, 1, 1)
                    for k in range(KD):
                        for tt in range(QT):
                            last = pe.transpose(p_t[:, k * S + tt * P:k * S + (tt + 1) * P], xh[:, tt, k * P:(k + 1) * P], idf)
                    last.then_inc(HE.sem, 1)
                if q:
                    passed(pe, QD, "q", t, 2)
                    passed(pe, QA, "qt", t, 2, 1)
                    pq = p_q[:].bitcast(BF16)
                    for k in range(KD):
                        for tt in range(QT):
                            last = pe.transpose(pq[:, k * S + tt * P:k * S + (tt + 1) * P], qq[:, tt, k * P:(k + 1) * P], idb)
                    last.then_inc(QE.sem, 1)
                if h:
                    passed(pe, HD, "nt", t, 1)
                    passed(pe, AA, "mt", t, 1)
                    passed(pe, AD, "u", t, 1)
                    passed(pe, HD, "x3", t, 1, 1)
                    half = parity(t.b(1))
                    for tt in range(QT):
                        o = p_h[:, tt * D:(tt + 1) * D]
                        ts_ = slice(tt * P, (tt + 1) * P)
                        pe.matmul(o, ones3, rows[:, RW_IN:RW_IN + D], start=True, stop=False)
                        for k in range(KD):
                            pe.matmul(o, nt[:, k, ts_], win[:, k, :], start=False, stop=False)
                        for k in range(QT):
                            last = pe.matmul(o, mt[:, k, ts_], u[:, half, k, :].rearrange("p o d -> p (o d)"),
                                             start=False, stop=k == QT - 1)
                    last.then_inc(HE.sem, 1)
                if a:
                    passed(pe, AD, "take", t, 0)
                    passed(pe, AA, "mt", t, 0, 1)
                    l0, l1 = cf[:, CF_L0:CF_L0 + P], cf[:, CF_L1:CF_L1 + P]
                    pe.matmul(p_mt[:, 0:S], l0, take[:, 0, :], start=True, stop=False)
                    pe.matmul(p_mt[:, 0:S], l1, take[:, 1, :], start=False, stop=True)
                    pe.matmul(p_mt[:, S:2 * S], l0, take[:, 1, :], start=True, stop=True).then_inc(AE.sem, 1)
                if q:
                    passed(pe, QA, "qt", t, 2)
                    passed(pe, QA, "y", t, 2, 1)
                    for tt in range(QT):
                        for k in range(KD):
                            last = pe.matmul(p_y[:, tt * D:(tt + 1) * D], qt[:, k, tt * P:(tt + 1) * P], kq[:, k, :], start=k == 0, stop=k == KD - 1)
                    last.then_inc(QE.sem, 1)

            run_turns(pe, turn, lambda t: None)


def build(nc, io):
    with ExitStack() as ctx:
        def sb(name, shape, dt=F32):
            return ctx.enter_context(nc.sbuf_tensor(name, shape, dt))

        def sem(name):
            return ctx.enter_context(nc.semaphore(name))

        keep = {
            "res": sb("res", [P, NT, D]),
            "gap": sb("gap", [P, NT]), "base": sb("base", [P, E]), "place": sb("place", [P, B, TOPK * QT]), "place_y": sb("place_y", [P, B, TOPK * QT], U32),
            "g1": sb("g1", [P, NT]), "g2": sb("g2", [P, NT]),
            "xs": nc.dram_tensor("xs", (NROWS, D), F32, kind="Internal").ap(),
            "ys": nc.dram_tensor("ys", (NTILE * SLOTS, D), F32, kind="Internal").ap(),
            "cf": sb("cf", [P, CF_N]), "cb": sb("cb", [P, CB_N], BF16), "rows": sb("rows", [3, RW_N], BF16),
            "kext": sb("kext", [P, B, QT, 4], BF16),
            "any4": sb("any4", [P, B]), "kq": sb("kq", [P, KD, D], BF16), "bounds": sb("bounds", [P, 2, QT, B]),
            "bias": sb("bias", [P, D], BF16), "lncol": sb("lncol", [P, 5, KD]),
            "r_in": sb("r_in", [P, 1]), "s_out": sb("s_out", [P, 1]), "ginit": sb("ginit_s", [P, D]),
        }
        setup_phase(nc, io, keep, sem)
        attention_phase(nc, io, keep, sem)
        expert_phase(nc, io, keep, sem)
        last_phase(nc, io, keep, sem)


def constants(np, bf16):
    cf = np.zeros((P, CF_N), np.float32)
    i = np.arange(P)
    cf[:, CF_ID:CF_ID + P] = np.eye(P)
    cf[:, CF_IOTA:CF_IOTA + S] = np.arange(S)
    for t in range(QT):
        cf[:, CF_ROW + t] = i + t * P
    cf[:, CF_TRI:CF_TRI + P] = i[:, None] <= i[None, :]
    cf[:, CF_ONE:CF_ONE + P] = 1
    decay = -math.expm1(-PATCH_EPS)
    for at, off in ((CF_L0, 0), (CF_L1, P)):
        d = i[:, None] - i[None, :] + off
        cf[:, at:at + P] = np.where(d >= 0, decay ** np.clip(d, 0, 300).astype(np.float64), 0)
    cf[:, CF_REG:CF_REG + E + 1] = REGION * np.arange(E + 1)
    cb = np.zeros((P, CB_N), np.float32)
    cb[:, CB_TRI:CB_TRI + P] = i[:, None] <= i[None, :]
    cb[:, CB_ID:CB_ID + P] = np.eye(P)
    later = np.where(i[:, None] < i[None, :], -1e30, 0)
    cb[:, CB_MQ:CB_MQ + 2 * P] = np.tile(later, 2)
    cb[:, CB_MK:CB_MK + 2 * P] = np.tile(later.T, 2)
    cb[:, CB_ONE:CB_ONE + P] = 1
    return cf, cb.astype(bf16)


def kernel(**inputs):
    import numpy as np
    import concourse.bacc as bacc
    from concourse.bass_utils import run_bass_kernel_spmd as run

    a = {k: np.asarray(v) for k, v in inputs.items()}
    cf, cb = constants(np, a["L1_ffn_kernel"].dtype)
    rows = np.concatenate([a["L0_ffn_bqkv"], a["L0_ffn_bo"], a["L0_ffn_fc2_b"].reshape(-1), a["L1_xattn_b_in"]])
    data = {
        "cf": cf, "cb": cb, "x": a["x"], "ctx": a["ctx_2048"], "seq": a["itok_Bx1_68_817"].reshape(-1),
        "lens": a["mask_BxS2_if0"].T.reshape(QT, P, B).transpose(1, 0, 2), "b": a["L0_xattn_b"].reshape(QT, P).T, "rows": np.stack([rows] * 3),
        "wqkv": a["L0_ffn_Wqkv"], "wo": a["L0_ffn_Wo"], "wgate": a["L0_ffn_gate_W"],
        "lncol": np.stack([a["L0_ffn_ln1_w"], a["L0_ffn_ln1_b"], a["L0_ffn_ln2_w"], a["L0_ffn_ln2_b"], a["L1_xattn_g_res"]]).reshape(5, KD, P).transpose(2, 0, 1),
        "fc1": a["L0_ffn_fc1_w"].transpose(0, 2, 1), "fc1b": a["L0_ffn_fc1_b"].reshape(E * FT, P).T, "fc2": a["L0_ffn_fc2_w"].transpose(0, 2, 1),
        "win": a["L1_xattn_W_in"].T, "ginit": a["L1_xattn_g_init"][0:D],
        "kern": a["L1_ffn_kernel"], "s_in": a["L1_ffn_input_scale"], "s_k": a["L1_ffn_kernel_scale"], "bias": a["L1_ffn_bias"],
    }
    data = {k: np.ascontiguousarray(v) for k, v in data.items()}
    nc = bacc.Bacc("TRN2", target_bir_lowering=False, num_devices=1)
    io = {k: nc.dram_tensor(f"in_{k}", v.shape, mybir.dt.from_np(v.dtype), kind="ExternalInput").ap() for k, v in data.items()}
    io["out"] = nc.dram_tensor("out", (B, S, D), F32, kind="ExternalOutput").ap()
    build(nc, io)
    r = run(nc, [{f"in_{k}": v for k, v in data.items()}], core_ids=[0])
    return r.results[0]["out"]
```

```python
import math
from contextlib import ExitStack

import concourse.bass as bass
from concourse import mybir

F32 = mybir.dt.float32
BF16 = mybir.dt.bfloat16
I32 = mybir.dt.int32
U32 = mybir.dt.uint32
ALU = mybir.AluOpType
ACT = mybir.ActivationFunctionType
AX = mybir.AxisListType

P = 128
B, S, D = 16, 256, 256
DC = 512
H, DH = 16, 16
NT = B * S // P
QT = S // P
KD = D // P
E, F, TOPK = 8, 1024, 2
FT = F // P
HB = 64
GROUPS = 8
STEPS = 16
NPT = 4
SLOTS = 256
ST = SLOTS // P
NTILE = (TOPK * B * S + E * (SLOTS - 1)) // SLOTS
REGION = B * S + SLOTS
NROWS = E * REGION + NTILE * SLOTS
EPS = 1e-5
PATCH_EPS = 0.001
NEG_BIG = -1e12
C20 = 1.5 * 2.0 ** 20

CF_ID, CF_IOTA, CF_ROW, CF_TRI, CF_ONE, CF_L0, CF_L1, CF_REG, CF_N = 0, 128, 384, 386, 514, 642, 770, 898, 907
CB_ID, CB_MQ, CB_MK, CB_ONE, CB_TRI, CB_N = 0, 128, 384, 640, 768, 896
RW_QKV, RW_O, RW_FC2, RW_IN, RW_N = 0, 768, 1024, 1024 + 8 * 256, 1280 + 8 * 256


class Steps:

    def __init__(self, sem, names):
        self.sem, self.names, self.n = sem, names.split(), len(names.split())

    def at(self, name, b):
        return b * self.n + self.names.index(name) + 1


class Turn:

    def __init__(self, i, ref=None):
        self.i, self.ref = i, i if ref is None else ref
        self.loop = ref is not None

    def b(self, lag):
        return self.i - lag

    def on(self, lag):
        return self.loop or 0 <= self.i - lag < B

    def first(self, lag):
        return self.ref - lag == 0


T_USES = [
    ("x_kt0", 0, 0), ("x_kt1", 0, 1), ("x_qt0", 0, 0), ("x_qt1", 0, 1), ("c_m0", 2, 0), ("c_m1", 2, 1),
    ("r_cnt", 3, 1), ("c_xt", 1, 0), ("c_qk0", 1, 1), ("c_v", 1, 0), ("c_qk1", 1, 1),
    ("c_kt0", 1, 0), ("c_kt1", 1, 1), ("c_qt0", 1, 0), ("c_qt1", 1, 1), ("x_m0", 0, 0), ("x_m1", 0, 1),
    ("c_back0", 2, 0), ("c_back1", 2, 1), ("c_at", 2, 0), ("c_wo", 2, 1), ("c_nt", 2, 0), ("c_gate", 2, 1),
    ("x_back0", 0, 0), ("x_back1", 0, 1),
]


LAGS = 3


def ring_table(uses):
    table, count = {}, {}
    for i in range(B + LAGS):
        for name, lag, bank in uses:
            if 0 <= i - lag < B:
                table[name, i - lag] = count.get(bank, 0)
                count[bank] = count.get(bank, 0) + 1
    return table


O_USES = [("c", 2, 0), ("x", 0, 0)]
S1_USES = [("x", 0, 0), ("c", 1, 0)]
S2_USES = [("c", 2, 0), ("x", 0, 0)]


def attention_phase(nc, io, keep, sem):
    T_TAB = ring_table(T_USES)
    O_TAB, S1_TAB, S2_TAB = (ring_table(u) for u in (O_USES, S1_USES, S2_USES))
    bank_of = {name: bank for name, _, bank in T_USES}
    T_PER = [sum(bank == n for _, _, bank in T_USES) for n in range(2)]

    res, gap, place, base, cf, cb = (keep[n] for n in ("res", "gap", "place", "base", "cf", "cb"))
    xs = keep["xs"]
    rows, kext, any4, lncol = keep["rows"], keep["kext"], keep["any4"], keep["lncol"]

    with ExitStack() as ctx:
        def sb(name, shape, dt=F32):
            return ctx.enter_context(nc.sbuf_tensor(name, shape, dt))

        ctxb = sb("ctxb", [P, QT, DC])
        wqkv = sb("wqkv", [P, KD, 3 * D])
        wo = sb("wo", [P, KD, D])
        wgate = sb("wgate", [P, KD, E])
        halfneg, empty = sb("halfneg", [P, 2]), sb("empty", [P, D])

        qs = {k: sb(f"qs_{k}", [P, QT, H, HB], BF16) for k in "xc"}
        ks = {k: sb(f"ks_{k}", [P, QT, H, HB], BF16) for k in "xc"}
        qt = {k: sb(f"qt_{k}", [P, GROUPS, S], BF16) for k in "xc"}
        kt = {k: sb(f"kt_{k}", [P, GROUPS, S], BF16) for k in "xc"}
        v1 = {k: sb(f"v1_{k}", [P, QT, H, 32]) for k in "xc"}
        qf = {k: sb(f"qf_{k}", [P, QT, D]) for k in "xc"}
        negm = {k: sb(f"negm_{k}", [P, QT, H]) for k in "xc"}
        mres = {k: sb(f"mres_{k}", [P, QT, H]) for k in "xc"}
        att = {k: sb(f"att_{k}", [P, QT, D]) for k in "xc"}
        rden = {k: sb(f"rden_{k}", [P, QT, H]) for k in "xc"}
        ot = {k: sb(f"ot_{k}", [P, 4, S]) for k in "xc"}
        st = {k: sb(f"st_{k}", [P, QT, 6]) for k in "xc"}
        mv = {k: sb(f"mv_{k}", [P, QT, 2]) for k in "xc"}
        rs = {k: sb(f"rs_{k}", [P, 8, QT]) for k in "xc"}
        st2, mv2 = sb("st2", [P, QT, 6]), sb("mv2", [P, QT, 2])
        rs2 = sb("rs2", [P, 2, QT])
        kf = sb("kf", [P, QT, D])
        xin = sb("xin", [P, 2, QT, D])
        xh = sb("xh", [P, QT, D])
        nxt = sb("nxt", [P, KD, S])
        at = sb("at", [P, KD, S])
        xp = sb("xp", [P, QT, D])
        xh2 = sb("xh2", [P, QT, D])
        n2 = sb("n2", [P, KD, S])
        prob = sb("prob", [P, NPT, 2, S])
        logits = sb("logits", [P, QT, E])
        top, idx = sb("top", [P, QT, 8]), sb("idx", [P, QT, 8], U32)
        idf = sb("idf", [P, TOPK, QT])
        chosen, hot = sb("chosen", [P, TOPK, QT, E]), sb("hot", [P, QT, E], BF16)
        rank, picked = sb("rank", [P, QT, E]), sb("picked", [P, TOPK, QT, E])
        placef, placeu = sb("placef", [P, TOPK * QT]), sb("placeu", [P, TOPK * QT], U32)

        tb = [ctx.enter_context(nc.psum_tensor(f"tb{n}", [P, 512], F32)) for n in range(2)]
        s1 = [ctx.enter_context(nc.psum_tensor(f"s1_{n}", [P, 2, S], F32)) for n in range(2)]
        s2 = [ctx.enter_context(nc.psum_tensor(f"s2_{n}", [P, 2, S], F32)) for n in range(2)]
        ob = ctx.enter_context(nc.psum_tensor("ob", [P, 4, S], F32))

        s_load, s_ctx, s_set = sem("a_load"), sem("a_ctx"), sem("a_pool_setup")
        s_empty, s_x = sem("a_empty_rows"), sem("a_x")
        t_full, t_free = [sem(f"t_full{n}") for n in range(2)], [sem(f"t_free{n}") for n in range(2)]
        s1_full, s1_free = sem("s1_full"), sem("s1_free")
        s2_full = sem("s2_full")
        p_full, p_free = sem("p_full"), sem("p_free")
        o_free = sem("o_free")
        s_seen = {e.engine: sem(f"a_seen_{n}") for e, n in ((nc.gpsimd, "pool"), (nc.vector, "dve"))}
        XD0 = Steps(sem("x_dve_pre"), "stats aggr q klo qlo")
        XD1 = Steps(sem("x_dve"), "m_hi m_res m_mid m_lo rec0 rec1")
        XP0 = Steps(sem("x_pool_pre"), "veps rstd rq khi2 qhi2 kext")
        XP1 = Steps(sem("x_pool"), "v x1")
        XA0 = Steps(sem("x_act_pre"), "khi qhi")
        CD1 = Steps(sem("c1_dve"), "stats aggr xh xin klo qlo m_hi m_res m_mid m_lo")
        CD2 = Steps(sem("c2_dve"), "rec0 rec1 stats2 aggr2 xh2")
        CP1 = Steps(sem("c1_pool"), "veps r1 r1sq v2 v2eps r2 r12 khi2 qhi2")
        CP2 = Steps(sem("c2_pool"), "veps2 rstd2 x2")
        CA1 = Steps(sem("c1_act"), "khi qhi")
        RD = Steps(sem("r_dve"), "top idx idf gap chosen hot rank picked placef placeu place")
        s_rows = sem("rows_scattered")
        DVE_SPLIT, POOL_SPLIT, ACT_SPLIT = {"x": XD0, "c": CD1}, {"x": XP0, "c": CP1}, {"x": XA0, "c": CA1}
        DVE_MAX, DVE_OUT = {"x": XD1, "c": CD1}, {"x": XD1, "c": CD2}

        def wait(eng, s, value):
            if not isinstance(value, int) or value > 0:
                eng.wait_ge(s, value)

        def passed(eng, steps, name, t, lag, back=0):
            if t.ref - lag - back >= 0:
                eng.wait_ge(steps.sem, steps.at(name, t.b(lag) - back))
                if t.loop and (eng is nc.gpsimd or eng is nc.vector and name in ("stats", "stats2")):
                    eng.sem_inc(s_seen[eng.engine], 1)

        def t_use(t, name, lag, back=0):
            base = T_TAB[name, t.ref - lag - back]
            return base + (t.i - t.ref) * T_PER[bank_of[name]] if t.loop else base

        def t_wait_full(eng, t, name, lag, back=0):
            if t.ref - lag - back >= 0:
                eng.wait_ge(t_full[bank_of[name]], t_use(t, name, lag, back) + 1)

        def t_wait_free(eng, t, name, lag):
            wait(eng, t_free[bank_of[name]], t_use(t, name, lag))

        def t_wait_read(eng, t, name, lag, back=0):
            if t.ref - lag - back >= 0:
                eng.wait_ge(t_free[bank_of[name]], t_use(t, name, lag, back) + 1)

        def ring(table, t, kind, lag, k, back=0):
            base = table[kind, t.ref - lag - back]
            return (base + (t.i - t.ref) * 2 if t.loop else base) * STEPS + k

        def products_done(eng, k, t, lag, back=0):
            if t.ref - lag - back >= 0:
                eng.wait_ge(p_free, ring(S2_TAB, t, k, lag, STEPS - 1, back) + 1)

        def o_count(t, k, lag):
            base = O_TAB[k, t.ref - lag]
            return base + (t.i - t.ref) * 2 if t.loop else base

        def heads(g):
            return [4 * (g // 2) + g % 2, 4 * (g // 2) + g % 2 + 2]

        def parity(b):
            return bass.ds(b % 2, 1)

        TOK = lambda t, lag: bass.ds(t.b(lag) * QT, QT)

        block = ctx.enter_context(nc.Block())

        n_load = 3

        @block.sync
        def _(sp):
            def load_ctx(t, lag):
                passed(sp, XD0, "stats", t, lag, 1)
                sp.dma_start(res[:, TOK(t, lag), :], io["x"][bass.ds(t.b(lag), 1)].rearrange("o (t p) d -> p (o t) d", p=P)).then_inc(s_x, 16)
                passed(sp, XD0, "klo", t, lag, 1)
                passed(sp, XP1, "v", t, lag, 1)
                sp.dma_start(ctxb[:], io["ctx"][bass.ds(t.b(lag), 1)].rearrange("o (t p) d -> p (o t) d", p=P)).then_inc(s_ctx, 16)

            load_ctx(Turn(0), 0)
            for dst, src in (
                (wqkv[:], io["wqkv"].rearrange("(k p) n -> p k n", p=P)),
                (wo[:], io["wo"].rearrange("(k p) n -> p k n", p=P)),
                (wgate[:], io["wgate"].rearrange("(k p) n -> p k n", p=P)),
            ):
                sp.dma_start(dst, src).then_inc(s_load, 16)
            load_ctx(Turn(1), 0)
            sp.wait_ge(s_set, 2)
            spare = NTILE - TOPK * B * S // SLOTS
            for n in range(spare):
                sp.dma_start(xs[E * REGION + n * SLOTS:E * REGION + (n + 1) * SLOTS, :].rearrange("(s p) d -> p s d", p=P),
                             empty[:].unsqueeze(1).broadcast_to((P, ST, D))).then_inc(s_empty, 16)
            with sp.Fori(2, B) as b:
                load_ctx(Turn(b, 2), 0)
            sp.wait_ge(s_empty, 16 * spare)

        @block.gpsimd
        def _(pool):
            def set_up(k):
                done = 0 if k == "x" else 2
                pool.memset(qs[k][:], 0.0)
                pool.memset(ks[k][:], 0.0)
                pool.memset(v1[k][:], 0.0).then_inc(s_set, 1)
                pool.wait_ge(s_set, done + 1)
                pool.memset(qs[k][:, :, :, 48:52], 1.0)
                pool.memset(ks[k][:, :, :, 52:55], 1.0)
                if k == "x":
                    pool.memset(empty[:], 0.0)
                    pool.memset(halfneg[:], -0.5)
                pool.memset(v1[k][:, :, :, DH:DH + 1], 1.0).then_inc(s_set, 1)
                pool.wait_ge(s_set, done + 2)

            def x_norm(t, lag):
                r = rs["x"]
                passed(pool, XD0, "aggr", t, lag)
                pool.tensor_scalar(r[:, 0, :], mv["x"][:, :, 1], EPS, None, ALU.add).then_inc(XP0.sem, 1)
                passed(pool, XP0, "veps", t, lag)
                pool.tensor_tensor(r[:, 1, :], r[:, 0, :], halfneg[:], ALU.pow).then_inc(XP0.sem, 1)
                passed(pool, XP0, "rstd", t, lag)
                pool.tensor_tensor(r[:, 2, :], r[:, 1, :], any4[:, bass.ds(t.b(lag), 1)].broadcast_to((P, QT)), ALU.mult).then_inc(XP0.sem, 1)

            def split_copies(k, t, lag, order):
                for w in order:
                    if w == "k":
                        passed(pool, ACT_SPLIT[k], "khi", t, lag)
                        pool.tensor_copy(ks[k][:, :, :, DH:2 * DH], ks[k][:, :, :, 0:DH]).then_inc(POOL_SPLIT[k].sem, 1)
                    else:
                        passed(pool, ACT_SPLIT[k], "qhi", t, lag)
                        pool.tensor_copy(qs[k][:, :, :, 2 * DH:3 * DH], qs[k][:, :, :, 0:DH]).then_inc(POOL_SPLIT[k].sem, 1)

            def x_kext(t, lag):
                src = kext[:, bass.ds(t.b(lag), 1), :, :]
                for tt in range(QT):
                    last = pool.tensor_copy(ks["x"][:, tt, :, 48:52], src[:, :, tt, :].broadcast_to((P, H, 4)))
                last.then_inc(XP0.sem, 1)

            def x_v(t, lag):
                pool.wait_ge(s_ctx, (t.b(lag) + 1) * 16)
                products_done(pool, "x", t, lag, 1)
                pool.sem_inc(s_seen[pool.engine], 1)
                pool.tensor_copy(v1["x"][:, :, :, 0:DH],
                                 ctxb[:, :, D:DC].rearrange("p t (h d) -> p t h d", h=H)).then_inc(XP1.sem, 1)

            def x_sum(t, lag):
                t_wait_read(pool, t, "x_back1", lag)
                pool.tensor_tensor(res[:, TOK(t, lag), :], res[:, TOK(t, lag), :], att["x"][:], ALU.add).then_inc(XP1.sem, 1)

            def c_norm(t, lag):
                r, v = rs["c"], mv["c"][:, :, 1]
                passed(pool, CD1, "aggr", t, lag)
                pool.tensor_scalar(r[:, 0, :], v, EPS, None, ALU.add).then_inc(CP1.sem, 1)
                passed(pool, CP1, "veps", t, lag)
                pool.tensor_tensor(r[:, 1, :], r[:, 0, :], halfneg[:], ALU.pow).then_inc(CP1.sem, 1)
                passed(pool, CP1, "r1", t, lag)
                pool.tensor_tensor(r[:, 2, :], r[:, 1, :], r[:, 1, :], ALU.mult).then_inc(CP1.sem, 1)
                passed(pool, CP1, "r1sq", t, lag)
                pool.tensor_tensor(r[:, 3, :], r[:, 2, :], v, ALU.mult).then_inc(CP1.sem, 1)
                passed(pool, CP1, "v2", t, lag)
                pool.tensor_scalar(r[:, 4, :], r[:, 3, :], EPS, None, ALU.add).then_inc(CP1.sem, 1)
                passed(pool, CP1, "v2eps", t, lag)
                pool.tensor_tensor(r[:, 5, :], r[:, 4, :], halfneg[:], ALU.pow).then_inc(CP1.sem, 1)
                passed(pool, CP1, "r2", t, lag)
                pool.tensor_tensor(r[:, 6, :], r[:, 5, :], r[:, 1, :], ALU.mult).then_inc(CP1.sem, 1)

            def c_norm2(t, lag):
                passed(pool, CD2, "aggr2", t, lag)
                pool.tensor_scalar(rs2[:, 0, :], mv2[:, :, 1], EPS, None, ALU.add).then_inc(CP2.sem, 1)
                passed(pool, CP2, "veps2", t, lag)
                pool.tensor_tensor(rs2[:, 1, :], rs2[:, 0, :], halfneg[:], ALU.pow).then_inc(CP2.sem, 1)

            def c_sum(t, lag):
                t_wait_read(pool, t, "c_wo", lag)
                pool.tensor_tensor(res[:, TOK(t, lag), :], res[:, TOK(t, lag), :], xp[:], ALU.add).then_inc(CP2.sem, 1)

            def r_scatter(t, lag):
                passed(pool, RD, "placeu", t, lag)
                for k in range(TOPK):
                    for tt in range(QT):
                        n = k * QT + tt
                        pool.indirect_dma_start(xs[:, :], bass.IndirectOffsetOnAxis(placeu[:, n:n + 1], 0), xh2[:, tt, :], None)\
                            .then_inc(s_rows, 16)

            def turn(t):
                if t.on(0):
                    x_v(t, 0)
                if t.on(1):
                    c_norm(t, 1)
                if t.on(3):
                    r_scatter(t, 3)
                if t.on(1):
                    split_copies("c", t, 1, "kq")
                if t.on(-1):
                    x_norm(t, -1)
                    split_copies("x", t, -1, "kq")
                    x_kext(t, -1)
                if t.on(2):
                    c_norm2(t, 2)
                    c_sum(t, 2)
                if t.on(0):
                    x_sum(t, 0)

            set_up("x")
            run_turns(pool, turn, lambda t: (x_norm(t, 0), split_copies("x", t, 0, "kq"), x_kext(t, 0), set_up("c")))

        @block.scalar
        def _(act):
            act.wait_ge(s_set, 2)

            def split_hi(k, t, lag, which):
                if which == "k":
                    if k == "x":
                        act.wait_ge(s_ctx, (t.b(lag) + 1) * 16)
                    else:
                        t_wait_read(act, t, "c_qk1", lag)
                    t_wait_full(act, t, f"{k}_kt1", lag, 1)
                    src = ctxb[:, :, 0:D] if k == "x" else kf[:]
                    act.activation(ks[k][:, :, :, 0:DH], src.rearrange("p t (h d) -> p t h d", h=H), ACT.Copy).then_inc(ACT_SPLIT[k].sem, 1)
                else:
                    if k == "x":
                        passed(act, XD0, "q", t, lag)
                    else:
                        t_wait_read(act, t, "c_qk1", lag)
                    t_wait_full(act, t, f"{k}_m1", lag, 1)
                    act.activation(qs[k][:, :, :, 0:DH], qf[k][:].rearrange("p t (h d) -> p t h d", h=H), ACT.Copy).then_inc(ACT_SPLIT[k].sem, 1)

            def evac_pairs(dst, t, name, lag, half):
                t_wait_full(act, t, name, lag)
                act.activation(dst[:, 4 * half:4 * half + 4, :].rearrange("p g s -> p (g s)"),
                               tb[bank_of[name]][:].bitcast(BF16), ACT.Copy).then_inc(t_free[bank_of[name]], 1)

            def exps(k, t, lag, n):
                kk, c = n % 2, ring(S2_TAB, t, k, lag, n)
                act.wait_ge(s2_full, c + 1)
                wait(act, p_free, c + 1 - NPT)
                lo = P if k == "c" and kk else 0
                act.activation(prob[:, n % NPT, :, lo:S], s2[n % 2][:, :, lo:S], ACT.Exp).then_inc(p_full, 1)

            def o_evac(k, t, lag):
                products_done(act, k, t, lag)
                t_wait_full(act, t, f"{k}_back1", lag, 1)
                for n in range(2):
                    last = act.activation(ot[k][:, 2 * n:2 * n + 2, :], ob[:, 2 * n:2 * n + 2, :], ACT.Copy)
                last.then_inc(o_free, 1)

            def c_qk(t, lag, tt):
                name = f"c_qk{tt}"
                t_wait_full(act, t, name, lag)
                if tt == 0:
                    passed(act, CD1, "qlo", t, lag, 1)
                act.activation(qf["c"][:, tt, :], tb[bank_of[name]][:, 0:D], ACT.Copy, scale=DH ** -0.5)
                act.activation(kf[:, tt, :], tb[bank_of[name]][:, D:2 * D], ACT.Copy).then_inc(t_free[bank_of[name]], 1)

            def c_xt(t, lag):
                t_wait_full(act, t, "c_xt", lag)
                src = tb[bank_of["c_xt"]][:].rearrange("p (k s) -> p k s", k=KD)
                for k in range(KD):
                    last = act.activation(nxt[:, k, :], src[:, k, :], ACT.Identity, scale=lncol[:, 0, k:k + 1], bias=lncol[:, 1, k:k + 1])
                last.then_inc(t_free[bank_of["c_xt"]], 1)

            def c_at(t, lag):
                t_wait_full(act, t, "c_at", lag)
                act.activation(at[:].rearrange("p k s -> p (k s)"), tb[bank_of["c_at"]][:], ACT.Copy).then_inc(t_free[bank_of["c_at"]], 1)

            def c_gate(t, lag):
                t_wait_full(act, t, "c_gate", lag)
                passed(act, RD, "idx", t, lag, 1)
                act.activation(logits[:], tb[bank_of["c_gate"]][:, 0:QT * E].rearrange("p (t e) -> p t e", e=E),
                               ACT.Copy).then_inc(t_free[bank_of["c_gate"]], 1)

            def turn(t):
                x, c1, c2, x_next = t.on(0), t.on(1), t.on(2), t.on(-1)
                if t.ref == 1:
                    act.wait_ge(s_set, 4)
                if x:
                    evac_pairs(kt["x"], t, "x_kt1", 0, 1)
                    evac_pairs(qt["x"], t, "x_qt1", 0, 1)
                for n in range(STEPS):
                    if c2:
                        exps("c", t, 2, n)
                    if c1 and n == 6:
                        c_xt(t, 1)
                    if c1 and n == 9:
                        c_qk(t, 1, 0)
                    if c1 and n == 13:
                        c_qk(t, 1, 1)
                        split_hi("c", t, 1, "k")
                    if c1 and n == 14:
                        split_hi("c", t, 1, "q")
                if c2:
                    o_evac("c", t, 2)
                if c1:
                    evac_pairs(kt["c"], t, "c_kt1", 1, 1)
                    evac_pairs(qt["c"], t, "c_qt1", 1, 1)
                for n in range(STEPS):
                    if x:
                        exps("x", t, 0, n)
                    if x_next and n == 5:
                        split_hi("x", t, -1, "k")
                    if x_next and n == 7:
                        split_hi("x", t, -1, "q")
                    if c2 and n == 6:
                        c_at(t, 2)
                if x:
                    o_evac("x", t, 0)
                if c2:
                    c_gate(t, 2)

            run_turns(act, turn, lambda t: (split_hi("x", t, 0, "k"), split_hi("x", t, 0, "q")))

        @block.vector
        def _(v):
            v.wait_ge(s_set, 2)

            def stats(k, t, lag):
                if k == "x":
                    v.wait_ge(s_x, (t.b(lag) + 1) * 16)
                    if t.loop:
                        v.sem_inc(s_seen[v.engine], 1)
                for tt in range(QT):
                    last = v.bn_stats(st[k][:, tt, :], res[:, bass.ds(t.b(lag) * QT + tt, 1), :].rearrange("p o d -> p (o d)"))
                last.then_inc(DVE_SPLIT[k].sem, 1)

            def aggr(k, t, lag):
                passed(v, DVE_SPLIT[k], "stats", t, lag)
                for tt in range(QT):
                    last = v.bn_aggr(mv[k][:, tt, :], st[k][:, tt, :])
                last.then_inc(DVE_SPLIT[k].sem, 1)

            def x_q(t, lag):
                passed(v, XP0, "rq", t, lag)
                passed(v, XA0, "qhi", t, lag, 1)
                for tt in range(QT):
                    last = v.tensor_scalar(qf["x"][:, tt, :], res[:, bass.ds(t.b(lag) * QT + tt, 1), :], mv["x"][:, tt, 0:1],
                                           rs["x"][:, 2, tt:tt + 1], ALU.subtract, ALU.mult)
                last.then_inc(XD0.sem, 1)

            def split_lo(k, t, lag, which):
                if which == "k":
                    passed(v, ACT_SPLIT[k], "khi", t, lag)
                    src = ctxb[:, :, 0:D] if k == "x" else kf[:]
                    v.tensor_tensor(ks[k][:, :, :, 2 * DH:3 * DH], src.rearrange("p t (h d) -> p t h d", h=H),
                                    ks[k][:, :, :, 0:DH], ALU.subtract).then_inc(DVE_SPLIT[k].sem, 1)
                else:
                    passed(v, ACT_SPLIT[k], "qhi", t, lag)
                    v.tensor_tensor(qs[k][:, :, :, DH:2 * DH], qf[k][:].rearrange("p t (h d) -> p t h d", h=H),
                                    qs[k][:, :, :, 0:DH], ALU.subtract).then_inc(DVE_SPLIT[k].sem, 1)

            def evac_pairs(dst, t, name, lag, half):
                t_wait_full(v, t, name, lag)
                v.tensor_copy(dst[:, 4 * half:4 * half + 4, :].rearrange("p g s -> p (g s)"),
                              tb[bank_of[name]][:].bitcast(BF16)).then_inc(t_free[bank_of[name]], 1)

            def maxes(k, t, lag, n):
                qq, g = n // GROUPS, n % GROUPS
                v.wait_ge(s1_full, ring(S1_TAB, t, k, lag, n) + 1)
                keys = P if k == "c" and qq == 0 else S
                h0 = heads(g)[0]
                v.tensor_reduce(negm[k][:, qq, h0:h0 + 3:2], s1[n % 2][:, :, 0:keys], AX.X, ALU.max, negate=True).then_inc(s1_free, 1)

            def max_parts(k, t, lag):
                steps = DVE_MAX[k]
                hi, mid, lo = (qs[k][:, :, :, 52 + n] for n in range(3))
                v.wait_ge(s1_free, ring(S1_TAB, t, k, lag, STEPS - 1) + 1)
                v.tensor_copy(hi, negm[k][:]).then_inc(steps.sem, 1)
                passed(v, steps, "m_hi", t, lag)
                v.tensor_tensor(mres[k][:], negm[k][:], hi, ALU.subtract).then_inc(steps.sem, 1)
                passed(v, steps, "m_res", t, lag)
                v.tensor_copy(mid, mres[k][:]).then_inc(steps.sem, 1)
                passed(v, steps, "m_mid", t, lag)
                v.tensor_tensor(lo, mres[k][:], mid, ALU.subtract).then_inc(steps.sem, 1)

            def normalize(k, t, lag, tiles):
                for qq in tiles:
                    name = f"{k}_back{qq}"
                    t_wait_full(v, t, name, lag)
                    if qq == 0 and k == "x":
                        passed(v, XP1, "x1", t, lag, 1)
                    view = tb[bank_of[name]][:].rearrange("p (h d) -> p h d", d=32)
                    v.reciprocal(rden[k][:, qq, :], view[:, :, DH]).then_inc(DVE_OUT[k].sem, 1)
                    passed(v, DVE_OUT[k], f"rec{qq}", t, lag)
                    v.tensor_tensor(att[k][:, qq, :].rearrange("p (h d) -> p h d", h=H), view[:, :, 0:DH],
                                    rden[k][:, qq, :].unsqueeze(2).broadcast_to((P, H, DH)), ALU.mult).then_inc(t_free[bank_of[name]], 1)

            def c_stats(t, lag):
                passed(v, XP1, "x1", t, lag)
                stats("c", t, lag)
                aggr("c", t, lag)

            def c_center(t, lag, dst, factor):
                if factor == 6:
                    passed(v, CP1, "r12", t, lag)
                for tt in range(QT):
                    last = v.tensor_scalar(dst[:, :, tt, :], res[:, bass.ds(t.b(lag) * QT + tt, 1), :], mv["c"][:, tt, 0:1],
                                           rs["c"][:, factor, tt:tt + 1], ALU.subtract, ALU.mult)
                last.then_inc(CD1.sem, 1)

            def c_nt(t, lag):
                t_wait_full(v, t, "c_nt", lag)
                t_wait_full(v, t, "c_gate", lag, 1)
                src = tb[bank_of["c_nt"]][:].rearrange("p (k s) -> p k s", k=KD)
                for k in range(KD):
                    last = v.tensor_scalar(n2[:, k, :], src[:, k, :], lncol[:, 2, k:k + 1], lncol[:, 3, k:k + 1], ALU.mult, ALU.add)
                last.then_inc(t_free[bank_of["c_nt"]], 1)

            def c_v(t, lag):
                t_wait_full(v, t, "c_v", lag)
                products_done(v, "c", t, lag, 1)
                v.tensor_copy(v1["c"][:, :, :, 0:DH], tb[bank_of["c_v"]][:].rearrange("p (t h d) -> p t h d", t=QT, h=H))\
                    .then_inc(t_free[bank_of["c_v"]], 1)

            def c_xp(t, lag):
                t_wait_full(v, t, "c_wo", lag)
                passed(v, CP2, "x2", t, lag, 1)
                v.tensor_tensor(xp[:].rearrange("p t d -> p (t d)").unsqueeze(1), tb[bank_of["c_wo"]][:].unsqueeze(1),
                                xin[:, parity(t.b(lag))].rearrange("p o t d -> p o (t d)"), ALU.add).then_inc(t_free[bank_of["c_wo"]], 1)

            def c_stats2(t, lag):
                t_wait_read(v, t, "c_wo", lag)
                for tt in range(QT):
                    last = v.bn_stats(st2[:, tt, :], xp[:, tt, :])
                last.then_inc(CD2.sem, 1)

            def c_aggr2(t, lag):
                passed(v, CD2, "stats2", t, lag)
                for tt in range(QT):
                    last = v.bn_aggr(mv2[:, tt, :], st2[:, tt, :])
                last.then_inc(CD2.sem, 1)

            def c_xh2(t, lag):
                passed(v, CP2, "rstd2", t, lag)
                if t.ref - lag >= 1:
                    v.wait_ge(s_rows, t.b(lag) * (16 * TOPK * QT))
                for tt in range(QT):
                    last = v.tensor_scalar(xh2[:, tt, :], xp[:, tt, :], mv2[:, tt, 0:1], rs2[:, 1, tt:tt + 1], ALU.subtract, ALU.mult)
                last.then_inc(CD2.sem, 1)

            def r_choose(t, lag, piece):
                if piece == 0:
                    t_wait_read(v, t, "c_gate", lag)
                    if t.loop:
                        v.sem_inc(s_seen[v.engine], 1)
                    for tt in range(QT):
                        last = v.max(top[:, tt, :], logits[:, tt, :])
                    last.then_inc(RD.sem, 1)
                if piece == 1:
                    v.wait_ge(RD.sem, RD.at("top", t.b(lag)))
                    v.sem_inc(s_seen[v.engine], 1)
                    for tt in range(QT):
                        last = v.max_index(idx[:, tt, :], top[:, tt, :], logits[:, tt, :])
                    last.then_inc(RD.sem, 1)
                if piece == 2:
                    passed(v, RD, "idx", t, lag)
                    v.tensor_copy(idf[:], idx[:, :, 0:TOPK].rearrange("p t k -> p k t")).then_inc(RD.sem, 1)
                    v.tensor_tensor(gap[:, TOK(t, lag)], top[:, :, 1], top[:, :, 0], ALU.subtract).then_inc(RD.sem, 1)
                if piece == 3:
                    passed(v, RD, "idf", t, lag)
                    v.tensor_tensor(chosen[:].rearrange("p k t e -> p (k t) e"),
                                    cf[:, CF_IOTA:CF_IOTA + E].unsqueeze(1).broadcast_to((P, TOPK * QT, E)),
                                    idf[:].rearrange("p k t -> p (k t)").unsqueeze(2).broadcast_to((P, TOPK * QT, E)), ALU.is_equal).then_inc(RD.sem, 1)
                    passed(v, RD, "chosen", t, lag)
                    v.tensor_tensor(hot[:], chosen[:, 0], chosen[:, 1], ALU.add).then_inc(RD.sem, 1)

            def r_place(t, lag, piece):
                if piece == 0:
                    t_wait_full(v, t, "r_cnt", lag)
                    cnt = tb[bank_of["r_cnt"]][:, 0:(QT + 1) * E].rearrange("p (t e) -> p t e", e=E)
                    t_wait_read(v, t, "r_cnt", lag, 1)
                    v.tensor_tensor(rank[:], cnt[:, 0:QT, :], base[:].unsqueeze(1).broadcast_to((P, QT, E)), ALU.add).then_inc(RD.sem, 1)
                    passed(v, RD, "rank", t, lag)
                    v.tensor_tensor(base[:], cnt[:, QT, :], base[:], ALU.add).then_inc(t_free[bank_of["r_cnt"]], 1)
                    for k in range(TOPK):
                        last = v.tensor_tensor(picked[:, k], chosen[:, k], rank[:], ALU.mult)
                    last.then_inc(RD.sem, 1)
                if piece == 1:
                    passed(v, RD, "picked", t, lag)
                    v.tensor_reduce(placef[:], picked[:].rearrange("p k t e -> p (k t) e"), AX.X, ALU.add).then_inc(RD.sem, 1)
                if piece == 2:
                    passed(v, RD, "placef", t, lag)
                    if t.ref - lag >= 1:
                        v.wait_ge(s_rows, t.b(lag) * (16 * TOPK * QT))
                    v.tensor_scalar(placeu[:], placef[:], -1.0, None, ALU.add).then_inc(RD.sem, 1)
                    v.tensor_scalar(place[:, bass.ds(t.b(lag), 1), :], placef[:].unsqueeze(1), -1.0, None, ALU.add).then_inc(RD.sem, 1)

            def turn(t):
                x, c1, c2, r, x_next = t.on(0), t.on(1), t.on(2), t.on(3), t.on(-1)
                if t.ref == 1:
                    v.wait_ge(s_set, 4)
                if x:
                    evac_pairs(kt["x"], t, "x_kt0", 0, 0)
                    evac_pairs(qt["x"], t, "x_qt0", 0, 0)
                if c2:
                    evac_pairs(qt["c"], t, "c_m0", 2, 0)
                    evac_pairs(qt["c"], t, "c_m1", 2, 1)
                if c1:
                    c_stats(t, 1)
                for n in range(STEPS):
                    if x:
                        maxes("x", t, 0, n)
                    if r and n < 4:
                        r_choose(t, 3, n)
                    if c1 and n == 4:
                        c_center(t, 1, xh[:].unsqueeze(1), 6)
                    if r and 6 <= n < 9:
                        r_place(t, 3, n - 6)
                    if c1 and n == 10:
                        c_center(t, 1, xin[:, parity(t.b(1))], 1)
                if c1:
                    split_lo("c", t, 1, "k")
                    split_lo("c", t, 1, "q")
                    c_v(t, 1)
                if x:
                    max_parts("x", t, 0)
                if c1:
                    evac_pairs(kt["c"], t, "c_kt0", 1, 0)
                    evac_pairs(qt["c"], t, "c_qt0", 1, 0)
                if x:
                    evac_pairs(qt["x"], t, "x_m0", 0, 0)
                    evac_pairs(qt["x"], t, "x_m1", 0, 1)
                for n in range(STEPS):
                    if c1:
                        maxes("c", t, 1, n)
                    if x_next and n == 0:
                        stats("x", t, -1)
                    if x_next and n == 1:
                        aggr("x", t, -1)
                    if c2 and n in (2, 3):
                        normalize("c", t, 2, [n - 2])
                    if x_next and n == 5:
                        x_q(t, -1)
                    if c2 and n == 8:
                        c_xp(t, 2)
                    if c2 and n == 9:
                        c_stats2(t, 2)
                    if c2 and n == 10:
                        c_aggr2(t, 2)
                    if x_next and n == 11:
                        split_lo("x", t, -1, "k")
                    if x_next and n == 12:
                        split_lo("x", t, -1, "q")
                    if c2 and n == 13:
                        c_xh2(t, 2)
                if c2:
                    c_nt(t, 2)
                if c1:
                    max_parts("c", t, 1)
                if x:
                    normalize("x", t, 0, range(QT))

            run_turns(v, turn, lambda t: (stats("x", t, 0), aggr("x", t, 0), x_q(t, 0), split_lo("x", t, 0, "k"), split_lo("x", t, 0, "q")))

        @block.tensor
        def _(pe):
            idb = cb[:, CB_ID:CB_ID + P]
            idf = cf[:, CF_ID:CF_ID + P]
            ones3 = cb[0:3, CB_ONE:CB_ONE + P]

            def pairs(src, t, name, lag, half):
                t_wait_free(pe, t, name, lag)
                dst = tb[bank_of[name]][:].bitcast(BF16).rearrange("p (g s) -> p g s", g=4)
                for g in range(4):
                    for tt in range(QT):
                        pair = 4 * half + g
                        last = pe.transpose(dst[:, g, tt * P:(tt + 1) * P],
                                            src[:, tt, 2 * pair:2 * pair + 2, :].rearrange("p h r -> p (h r)"), idb)
                last.then_inc(t_full[bank_of[name]], 1)

            def k_pairs(k, t, lag):
                passed(pe, DVE_SPLIT[k], "klo", t, lag)
                passed(pe, POOL_SPLIT[k], "kext" if k == "x" else "khi2", t, lag)
                for half in range(2):
                    pairs(ks[k], t, f"{k}_kt{half}", lag, half)

            def q_pairs(k, t, lag):
                passed(pe, DVE_SPLIT[k], "qlo", t, lag)
                passed(pe, POOL_SPLIT[k], "qhi2", t, lag)
                for half in range(2):
                    pairs(qs[k], t, f"{k}_qt{half}", lag, half)

            def m_pairs(k, t, lag):
                passed(pe, DVE_MAX[k], "m_lo", t, lag)
                for half in range(2):
                    pairs(qs[k], t, f"{k}_m{half}", lag, half)

            def s1_step(k, t, lag, n):
                qq, g = n // GROUPS, n % GROUPS
                c = ring(S1_TAB, t, k, lag, n)
                if n == 0:
                    for w in ("qt0", "qt1"):
                        t_wait_read(pe, t, f"{k}_{w}", lag)
                wait(pe, s1_free, c - 1)
                out = s1[n % 2]
                r0 = HB * (g % 2)
                if k == "c":
                    cols = slice(qq * P, (qq + 1) * P)
                    pe.matmul(out[:, :, cols], idb, cb[:, CB_MQ:CB_MQ + 2 * P].rearrange("p (h s) -> p h s", h=2), start=True, stop=False)
                for j, h in enumerate(heads(g)):
                    q = qt[k][r0:r0 + 52, h // 2, qq * P:(qq + 1) * P]
                    for kk in range(QT):
                        if k == "c" and kk > qq:
                            continue
                        ks_ = slice(kk * P, (kk + 1) * P)
                        if k == "x":
                            if kk == 0:
                                last = pe.matmul(out[:, j, :], q, kt[k][r0:r0 + 52, h // 2, :], start=True, stop=True)
                        else:
                            last = pe.matmul(out[:, j, ks_], q, kt[k][r0:r0 + 52, h // 2, ks_], start=False, stop=j == 1 and kk == qq)
                last.then_inc(s1_full, 1)

            def s2_step(k, t, lag, n):
                g, kk = n // 2, n % 2
                c = ring(S2_TAB, t, k, lag, n)
                if n == 0:
                    t_wait_read(pe, t, f"{k}_m0", lag)
                    t_wait_read(pe, t, f"{k}_m1", lag)
                wait(pe, p_full, c - 1)
                out = s2[n % 2]
                r0 = HB * (g % 2)
                if k == "c":
                    pe.matmul(out[:, :, kk * P:(kk + 1) * P], idb, cb[:, CB_MK:CB_MK + 2 * P].rearrange("p (h s) -> p h s", h=2),
                              start=True, stop=False)
                for j, h in enumerate(heads(g)):
                    key = kt[k][r0:r0 + HB, h // 2, kk * P:(kk + 1) * P]
                    if k == "x":
                        last = pe.matmul(out[:, j, :], key, qt[k][r0:r0 + HB, h // 2, :], start=True, stop=True)
                    else:
                        for qq in range(kk, QT):
                            qs_ = slice(qq * P, (qq + 1) * P)
                            last = pe.matmul(out[:, j, qs_], key, qt[k][r0:r0 + HB, h // 2, qs_], start=False, stop=j == 1 and qq == QT - 1)
                last.then_inc(s2_full, 1)

            def pv_step(k, t, lag, n):
                g, kk = n // 2, n % 2
                c = ring(S2_TAB, t, k, lag, n)
                pe.wait_ge(p_full, c + 1)
                if n == 0:
                    if k == "x":
                        passed(pe, XP1, "v", t, lag)
                    else:
                        t_wait_read(pe, t, "c_v", lag)
                    wait(pe, o_free, o_count(t, k, lag))
                lo = P if k == "c" and kk else 0
                for j, h in enumerate(heads(g)):
                    col = 32 * (h % 4)
                    last = pe.matmul(ob[col:col + 32, h // 4, lo:S], v1[k][:, kk, h, :], prob[:, n % NPT, j, lo:S],
                                     start=kk == 0, stop=kk == 1)
                last.then_inc(p_free, 1)

            def back(k, t, lag):
                pe.wait_ge(o_free, o_count(t, k, lag) + 1)
                for qq in range(QT):
                    name = f"{k}_back{qq}"
                    t_wait_free(pe, t, name, lag)
                    for j in range(4):
                        last = pe.transpose(tb[bank_of[name]][:, j * P:(j + 1) * P], ot[k][:, j, qq * P:(qq + 1) * P], idf)
                    last.then_inc(t_full[bank_of[name]], 1)

            def turn_over(src, t, name, lag, waits):
                waits()
                t_wait_free(pe, t, name, lag)
                for k in range(KD):
                    for tt in range(QT):
                        last = pe.transpose(tb[bank_of[name]][:, k * S + tt * P:k * S + (tt + 1) * P], src[:, tt, k * P:(k + 1) * P], idf)
                last.then_inc(t_full[bank_of[name]], 1)

            def project(out, lhs, w, tt, lo, n, row):
                for k in range(KD):
                    pe.matmul(out, lhs[:, k, tt * P:(tt + 1) * P], w[:, k, lo:lo + n], start=k == 0, stop=False)
                return pe.matmul(out, ones3, rows[:, row:row + n], start=False, stop=True)

            def c_qk(t, lag, tt):
                name = f"c_qk{tt}"
                if tt == 0:
                    t_wait_read(pe, t, "c_xt", lag)
                t_wait_free(pe, t, name, lag)
                project(tb[bank_of[name]][:, 0:2 * D], nxt, wqkv, tt, 0, 2 * D, RW_QKV).then_inc(t_full[bank_of[name]], 1)

            def c_v(t, lag, tt):
                if tt == 0:
                    t_wait_free(pe, t, "c_v", lag)
                last = project(tb[bank_of["c_v"]][:, tt * D:(tt + 1) * D], nxt, wqkv, tt, 2 * D, D, RW_QKV + 2 * D)
                if tt == QT - 1:
                    last.then_inc(t_full[bank_of["c_v"]], 1)

            def c_wo(t, lag):
                t_wait_read(pe, t, "c_at", lag)
                t_wait_free(pe, t, "c_wo", lag)
                for tt in range(QT):
                    last = project(tb[bank_of["c_wo"]][:, tt * D:(tt + 1) * D], at, wo, tt, 0, D, RW_O)
                last.then_inc(t_full[bank_of["c_wo"]], 1)

            def c_gate(t, lag):
                t_wait_read(pe, t, "c_nt", lag)
                t_wait_free(pe, t, "c_gate", lag)
                for tt in range(QT):
                    for k in range(KD):
                        last = pe.matmul(tb[bank_of["c_gate"]][:, tt * E:(tt + 1) * E], n2[:, k, tt * P:(tt + 1) * P], wgate[:, k, :],
                                         start=k == 0, stop=k == KD - 1)
                last.then_inc(t_full[bank_of["c_gate"]], 1)

            def r_count(t, lag):
                passed(pe, RD, "hot", t, lag)
                t_wait_free(pe, t, "r_cnt", lag)
                tri, one = cb[:, CB_TRI:CB_TRI + P], cb[:, CB_ONE:CB_ONE + P]
                out = tb[bank_of["r_cnt"]]
                pe.matmul(out[:, 0:E], tri, hot[:, 0, :], start=True, stop=True)
                pe.matmul(out[:, E:2 * E], one, hot[:, 0, :], start=True, stop=False)
                pe.matmul(out[:, E:2 * E], tri, hot[:, 1, :], start=False, stop=True)
                pe.matmul(out[:, 2 * E:3 * E], one, hot[:, 0, :], start=True, stop=False)
                pe.matmul(out[:, 2 * E:3 * E], one, hot[:, 1, :], start=False, stop=True).then_inc(t_full[bank_of["r_cnt"]], 1)

            def turn(t):
                x, c1, c2 = t.on(0), t.on(1), t.on(2)
                if t.ref == 1:
                    pe.wait_ge(s_load, 16 * n_load)
                    pe.wait_ge(s_set, 4)
                if x:
                    k_pairs("x", t, 0)
                    q_pairs("x", t, 0)
                if c2:
                    m_pairs("c", t, 2)
                for n in range(STEPS):
                    if x:
                        s1_step("x", t, 0, n)
                    if c2:
                        s2_step("c", t, 2, n)
                        if n >= 2:
                            pv_step("c", t, 2, n - 2)
                    if t.on(3) and n == 4:
                        r_count(t, 3)
                    if c1 and n == 6:
                        turn_over(xh, t, "c_xt", 1, lambda: passed(pe, CD1, "xh", t, 1))
                    if c1 and n == 8:
                        c_qk(t, 1, 0)
                    if c1 and n == 12:
                        c_qk(t, 1, 1)
                if c1:
                    c_v(t, 1, 0)
                if c2:
                    pv_step("c", t, 2, STEPS - 2)
                if c1:
                    c_v(t, 1, 1)
                if c2:
                    pv_step("c", t, 2, STEPS - 1)
                if c1:
                    k_pairs("c", t, 1)
                    q_pairs("c", t, 1)
                if x:
                    m_pairs("x", t, 0)
                for n in range(STEPS):
                    if c1:
                        s1_step("c", t, 1, n)
                    if x:
                        s2_step("x", t, 0, n)
                        if n >= 2:
                            pv_step("x", t, 0, n - 2)
                    if c2 and n == 1:
                        back("c", t, 2)
                    if c2 and n == 5:
                        turn_over(att["c"], t, "c_at", 2, lambda: (t_wait_read(pe, t, "c_back1", 2), t_wait_read(pe, t, "c_back0", 2)))
                    if c2 and n == 7:
                        c_wo(t, 2)
                    if c2 and n == 14:
                        turn_over(xh2, t, "c_nt", 2, lambda: passed(pe, CD2, "xh2", t, 2))
                if x:
                    pv_step("x", t, 0, STEPS - 2)
                    pv_step("x", t, 0, STEPS - 1)
                if c2:
                    c_gate(t, 2)
                if x:
                    back("x", t, 0)

            run_turns(pe, turn, lambda t: None)


def run_turns(eng, turn, first):
    first(Turn(0))
    for i in range(LAGS + 1):
        turn(Turn(i))
    with eng.Fori(LAGS + 1, B - 1) as i:
        turn(Turn(i, LAGS + 1))
    for i in range(B - 1, B + LAGS):
        turn(Turn(i))


def setup_phase(nc, io, keep, sem):
    cf, cb, rows = keep["cf"], keep["cb"], keep["rows"]
    kext, any4, kq, bounds = keep["kext"], keep["any4"], keep["kq"], keep["bounds"]
    with ExitStack() as ctx:
        def sb(name, shape, dt=F32):
            return ctx.enter_context(nc.sbuf_tensor(name, shape, dt))

        rows_f, rows_r = sb("rows_f", [P, RW_N // P]), sb("rows_r", [P, RW_N // P])
        rows_m = sb("rows_m", [P, 3, RW_N // P], BF16)
        seq_i, seq_f = sb("seq_i", [P, B], I32), sb("seq_f", [P, B])
        any_f = sb("any_f", [P, B])
        bcol, bpf, bres = sb("bcol", [P, QT]), sb("bpf", [P, 3, QT]), sb("bres", [P, QT])
        bpart = sb("bpart", [P, 3, QT], BF16)
        msk = sb("msk", [P, QT, B])
        scales = sb("scales", [P, 2])
        rscale = sb("rscale", [P, 2])
        kw = sb("kw", [P, KD, D], BF16)
        kwf, kexp, kbig, ksum = sb("kwf", [P, KD, D]), sb("kexp", [P, KD, D]), sb("kbig", [P, KD, D]), sb("ksum", [P, KD, D])
        len_i, len_f = sb("len_i", [P, QT, B], I32), sb("len_f", [P, QT, B])
        ginit = sb("ginit", [P, D])
        ends = ctx.enter_context(nc.psum_tensor("ends", [P, QT, B], F32))
        s_load, s_dve, s_ends = sem("setup_load"), sem("setup_dve"), sem("setup_ends")
        s_parts = sem("setup_parts")
        rows_d = nc.dram_tensor("rows_d", (3, RW_N), BF16, kind="Internal").ap()
        loads = (
            (cf[:], io["cf"]), (cb[:], io["cb"]),
            (rows_f[:], io["rows"].rearrange("(p n) -> p n", p=P)), (seq_i[:], io["seq"].partition_broadcast(P)),
            (bcol[:], io["b"]),
            (scales[:, 0:1], io["s_in"].partition_broadcast(P)), (scales[:, 1:2], io["s_k"].partition_broadcast(P)),
            (kw[:], io["kern"].rearrange("(k p) n -> p k n", p=P)),
            (len_i[:], io["lens"]),
            (ginit[:], io["ginit"].partition_broadcast(P)),
            (keep["bias"][:], io["bias"].partition_broadcast(P)),
            (keep["lncol"][:], io["lncol"]),
        )
        block = ctx.enter_context(nc.Block())

        @block.sync
        def _(sp):
            for dst, src in loads:
                sp.dma_start(dst, src).then_inc(s_load, 16)
            sp.wait_ge(s_dve, 5)
            for part in range(3):
                sp.dma_start(rows_d[part].rearrange("(p n) -> p n", p=P), rows_m[:, part, :]).then_inc(s_parts, 16)
            sp.wait_ge(s_parts, 48)
            sp.dma_start(rows[:], rows_d[:, :]).then_inc(s_parts, 16)
            sp.wait_ge(s_parts, 64)

        @block.tensor
        def _(pe):
            pe.wait_ge(s_dve, 1)
            tri, one = cf[:, CF_TRI:CF_TRI + P], cf[:, CF_ONE:CF_ONE + P]
            pe.matmul(ends[:, 0, :], tri, len_f[:, 0, :], start=True, stop=True)
            pe.matmul(ends[:, 1, :], one, len_f[:, 0, :], start=True, stop=False)
            pe.matmul(ends[:, 1, :], tri, len_f[:, 1, :], start=False, stop=True).then_inc(s_ends, 1)

        @block.vector
        def _(v):
            count = [0]

            def after(ins):
                count[0] += 1
                ins.then_inc(s_dve, 1)
                v.wait_ge(s_dve, count[0])

            v.wait_ge(s_load, 16 * len(loads))
            after(v.tensor_copy(len_f[:], len_i[:]))
            after(v.tensor_copy(rows_m[:, 0, :], rows_f[:]))
            after(v.tensor_tensor(rows_r[:], rows_f[:], rows_m[:, 0, :], ALU.subtract))
            after(v.tensor_copy(rows_m[:, 1, :], rows_r[:]))
            after(v.tensor_tensor(rows_m[:, 2, :], rows_r[:], rows_m[:, 1, :], ALU.subtract))
            after(v.tensor_copy(seq_f[:], seq_i[:]))
            after(v.tensor_scalar(any4[:], seq_f[:], 0.0, DH ** -0.5, ALU.is_gt, ALU.mult))
            after(v.tensor_scalar(any_f[:], seq_f[:], 0.0, None, ALU.is_gt))
            after(v.tensor_copy(bpart[:, 0, :], bcol[:]))
            after(v.tensor_tensor(bres[:], bcol[:], bpart[:, 0, :], ALU.subtract))
            after(v.tensor_copy(bpart[:, 1, :], bres[:]))
            after(v.tensor_tensor(bpart[:, 2, :], bres[:], bpart[:, 1, :], ALU.subtract))
            after(v.tensor_copy(bpf[:], bpart[:]))
            for tt in range(QT):
                after(v.tensor_scalar(msk[:, tt, :], seq_f[:], cf[:, CF_ROW + tt:CF_ROW + tt + 1], NEG_BIG, ALU.is_le, ALU.mult))
                for part in range(3):
                    after(v.tensor_scalar(kext[:, :, tt, part], any_f[:], bpf[:, part, tt:tt + 1], None, ALU.mult))
                after(v.tensor_tensor(kext[:, :, tt, 3], msk[:, tt, :], any_f[:], ALU.mult))
            after(v.tensor_copy(keep["base"][:], cf[:, CF_REG:CF_REG + E]))
            after(v.reciprocal(rscale[:], scales[:]))
            after(v.tensor_copy(keep["r_in"][:], rscale[:, 0:1]))
            after(v.tensor_tensor(keep["s_out"][:], scales[:, 0:1], scales[:, 1:2], ALU.mult))
            after(v.tensor_scalar(kwf[:], kw[:], rscale[:, 1:2], None, ALU.mult))
            after(v.tensor_single_scalar(kexp[:].bitcast(I32), kwf[:].bitcast(I32), 0x7F800000, op=ALU.bitwise_and))
            after(v.tensor_scalar(kbig[:], kexp[:], 2.0 ** -6, C20, ALU.max, ALU.mult))
            after(v.tensor_tensor(ksum[:], kwf[:], kbig[:], ALU.add))
            after(v.tensor_tensor(kq[:], ksum[:], kbig[:], ALU.subtract))
            after(v.tensor_scalar(keep["ginit"][:], ginit[:], math.exp(-PATCH_EPS), None, ALU.mult))
            v.wait_ge(s_ends, 1)
            after(v.tensor_scalar(bounds[:, 0], ends[:], -1.0, None, ALU.add))
            after(v.tensor_scalar(bounds[:, 1], ends[:], -1.0 + S, None, ALU.add))


def expert_phase(nc, io, keep, sem):
    cf, cb, rows, lncol, base, xs, ys = (keep[n] for n in ("cf", "cb", "rows", "lncol", "base", "xs", "ys"))
    NH = 4
    CHUNK = F
    PARTS = (KD * F + FT * D) // CHUNK
    FILLED, TABLE = 1, 17
    PEEL, LAST = 3, 2
    with ExitStack() as ctx:
        def sb(name, shape, dt=F32):
            return ctx.enter_context(nc.sbuf_tensor(name, shape, dt))

        wf = sb("wf", [P, CHUNK])
        w1 = [sb(f"w1_{p}", [P, E, KD, F], BF16) for p in "hl"]
        w2 = [sb(f"w2_{p}", [P, E, FT, D], BF16) for p in "hl"]
        b1 = sb("b1", [P, E * FT])
        eg, den = sb("eg", [P, NT]), sb("den", [P, NT])
        fill, tiles_i, tiles, ends, starts = sb("region_fill", [P, E]), sb("tiles_i", [P, E], I32), sb("tiles", [P, E]), sb("tile_ends", [P, E]), sb("starts", [P, E + 1])
        one8, shift = sb("one8", [P, E]), sb("shift", [P, E])
        ex, is_ex, ex7, row = sb("ex", [1, NTILE]), sb("is_ex", [1, NTILE, E + 1]), sb("ex7", [1, NTILE], U32), sb("row", [1, NTILE])
        ended = is_ex[:, :, 0:E]
        row_u, pad_u = sb("row_u", [1, NTILE], U32), sb("pad_u", [1, E], U32)
        zeros = sb("zeros", [P, D])
        xt = [sb(f"xt{n}", [P, ST, D]) for n in range(2)]
        nf = sb("nf", [P, KD, SLOTS])
        move, moved = (nf[:, n, 0:B * TOPK * QT] for n in range(2))
        nx = [sb(f"nx_{p}", [P, KD, SLOTS], BF16) for p in "hl"]
        hf = sb("hf", [P, NH, SLOTS])
        hid = [sb(f"hid_{p}", [P, FT, SLOTS], BF16) for p in "hl"]
        yt = [sb(f"yt{n}", [P, ST, D]) for n in range(2)]
        pt = ctx.enter_context(nc.psum_tensor("pt", [P, KD, SLOTS], F32))
        hb = [ctx.enter_context(nc.psum_tensor(f"hb{n}", [P, 512], F32)) for n in range(NH)]
        yb = [ctx.enter_context(nc.psum_tensor(f"yb{n}", [P, 512], F32)) for n in range(ST)]

        s_b1, s_w, s_split, s_zero, s_padded = sem("b1_load"), sem("w_load"), sem("w_split"), sem("zeros_set"), sem("rows_padded")
        s_first, s_high0 = [sem(f"w_first{n}") for n in range(PARTS)], sem("w_first_high")
        s_eg, s_tab = sem("gate_exp"), sem("tile_table")
        s_xt, s_t, s_nf, s_nh, s_nl = [sem(f"x_tile{n}") for n in range(2)], sem("x_turned"), sem("x_weighed"), sem("x_high"), sem("x_low")
        s_h, s_gelu, s_hi, s_lo = sem("h_full"), sem("gelu"), sem("h_high"), sem("h_low")
        s_y, s_yt, s_out = sem("y_full"), sem("y_read"), [sem(f"y_stored{n}") for n in range(2)]
        s_seen_pe, s_w_seen = sem("e_seen_pe"), sem("e_seen_pool")
        block = ctx.enter_context(nc.Block())

        def wait(eng, s, value):
            if not isinstance(value, int) or value > 0:
                eng.wait_ge(s, value)

        def tiles_loop(eng, body):
            for j in range(PEEL):
                body(j, j % 2, j // 2)
            with eng.Fori(0, (NTILE - PEEL - LAST) // 2) as m:
                for k in range(2):
                    body(m * 2 + (PEEL + k), (PEEL + k) % 2, m + (PEEL + k) // 2)
            assert (NTILE - PEEL - LAST) % 2 == 0
            for j in range(NTILE - LAST, NTILE):
                body(j, j % 2, j // 2)

        def rows_of(a, r, n):
            return a[bass.ds(r, n), :].rearrange("(s p) d -> p s d", p=P)

        def weight_parts(e):
            one, rows_each = bass.ds(e, 1), CHUNK // D
            parts = [(io["fc1"][one, k * P:(k + 1) * P, :].rearrange("o p f -> p (o f)"), [w[:, one, k, :] for w in w1]) for k in range(KD)]
            for n in range(0, FT, rows_each):
                parts.append((io["fc2"][one, n * P:(n + rows_each) * P, :].rearrange("o (k p) d -> p (o k) d", p=P),
                              [w[:, one, n:n + rows_each, :] for w in w2]))
            return parts

        def as_part(buffer, n):
            return buffer if n < KD else buffer.rearrange("p (k d) -> p k d", d=D)

        first = [wf[:], hf[:].rearrange("p k s -> p (k s)")] + [h[:].rearrange("p k s -> p (k s)").bitcast(F32) for h in hid]

        def pad(eng, experts):
            eng.wait_ge(s_zero, 1)
            eng.wait_ge(s_tab, FILLED)
            for e in experts:
                r = eng.value_load(pad_u[0:1, e:e + 1], min_val=e * REGION, max_val=e * REGION + B * S)
                eng.dma_start(rows_of(xs, r, SLOTS), zeros[:].unsqueeze(1).broadcast_to((P, ST, D))).then_inc(s_padded, 16)

        @block.sync
        def _(sp):
            for n, (src, _) in enumerate(weight_parts(0)):
                sp.dma_start(as_part(first[n], n), src).then_inc(s_first[n], 16)
            sp.dma_start(b1[:], io["fc1b"]).then_inc(s_b1, 16)
            pad(sp, range(0, E // 2))
            sp.wait_ge(s_padded, 16 * E)
            sp.wait_ge(s_tab, TABLE)

            def load_x(j, n, h):
                r = sp.value_load(row_u[0:1, bass.ds(j, 1)], min_val=0, max_val=NROWS - SLOTS)
                wait(sp, s_t, j - 1)
                sp.dma_start(xt[n][:], rows_of(xs, r, SLOTS)).then_inc(s_xt[n], 16)

            tiles_loop(sp, load_x)
            for n in range(2):
                sp.wait_ge(s_out[n], 16 * ((NTILE + 1 - n) // 2))

        @block.gpsimd
        def _(pool):
            pool.memset(zeros[:], 0.0).then_inc(s_zero, 1)

            def split_weights(e):
                for n, (src, (high, low)) in enumerate(weight_parts(e)):
                    done = e * (2 * PARTS) + 2 * n
                    got = as_part(wf[:], n).unsqueeze(1)
                    pool.wait_ge(s_split, done)
                    pool.sem_inc(s_w_seen, 1)
                    pool.dma_start(as_part(wf[:], n), src).then_inc(s_w, 16)
                    pool.wait_ge(s_w, (e - 1) * (16 * PARTS) + 16 * (n + 1))
                    pool.sem_inc(s_w_seen, 1)
                    pool.tensor_copy(high, got).then_inc(s_split, 1)
                    pool.wait_ge(s_split, done + 1)
                    pool.sem_inc(s_w_seen, 1)
                    pool.tensor_tensor(low, got, high, ALU.subtract).then_inc(s_split, 1)

            split_weights(1)
            with pool.Fori(2, E) as e:
                split_weights(e)

        @block.scalar
        def _(act):
            act.activation(eg[:], keep["gap"][:], ACT.Exp).then_inc(s_eg, 1)
            pad(act, range(E // 2, E))
            for n, (_, (high, _)) in enumerate(weight_parts(0)):
                act.wait_ge(s_first[n], 16)
                act.activation(high, as_part(first[n], n).unsqueeze(1), ACT.Copy).then_inc(s_high0, 1)

            def x_high(j):
                act.wait_ge(s_nf, j + 1)
                act.activation(nx[0][:], nf[:], ACT.Copy).then_inc(s_nh, 1)

            x_high(0)
            act.wait_ge(s_b1, 16)
            act.wait_ge(s_split, 2 * PARTS)
            act.wait_ge(s_tab, TABLE)

            def body(j, n, h):
                e = act.value_load(ex7[0:1, bass.ds(j, 1)], min_val=0, max_val=E - 1)
                for f in range(FT):
                    act.wait_ge(s_h, j * FT + f + 1)
                    wait(act, s_lo, j * FT + f + 1 - NH)
                    act.activation(hf[:, f % NH, :], hb[f % NH][:, 0:SLOTS], ACT.Gelu, bias=b1[:, bass.ds(e * FT + f, 1)]).then_inc(s_gelu, 1)
                if not isinstance(j, int) or j + 1 < NTILE:
                    x_high(j + 1)
                wait(act, s_out[n], h * 16)
                for k in range(ST):
                    act.wait_ge(s_y, j * ST + k + 1)
                    act.activation(yt[n][:, k, :], yb[k][:, 0:D], ACT.Copy).then_inc(s_yt, 1)
                act.wait_ge(s_yt, j * ST + ST)
                act.dma_start(rows_of(ys, j * SLOTS, SLOTS), yt[n][:]).then_inc(s_out[n], 16)

            tiles_loop(act, body)

        @block.vector
        def _(v):
            count = [0]

            def after(ins):
                count[0] += 1
                ins.then_inc(s_tab, 1)
                v.wait_ge(s_tab, count[0])

            after(v.tensor_copy(pad_u[:], base[0:1, :]))
            after(v.memset(one8[:], 1.0))
            after(v.tensor_tensor(fill[:], base[:], cf[:, CF_REG:CF_REG + E], ALU.subtract))
            after(v.tensor_scalar(tiles_i[:], fill[:], float(SLOTS - 1), None, ALU.add))
            after(v.tensor_single_scalar(tiles_i[:], tiles_i[:], SLOTS.bit_length() - 1, op=ALU.arith_shift_right))
            after(v.tensor_copy(tiles[:], tiles_i[:]))
            after(v.tensor_tensor_scan(ends[:], one8[:], tiles[:], 0.0, ALU.mult, ALU.add))
            after(v.tensor_copy(starts[:, 0:1], cf[:, CF_REG:CF_REG + 1]))
            after(v.scalar_tensor_tensor(out=starts[:, 1:E + 1], in0=ends[:], scalar=-float(SLOTS), in1=cf[:, CF_REG + 1:CF_REG + E + 1],
                                         op0=ALU.mult, op1=ALU.add))
            number = cf[0:1, CF_IOTA:CF_IOTA + NTILE]
            after(v.tensor_tensor(ended, number.unsqueeze(2).broadcast_to((1, NTILE, E)),
                                  ends[0:1, :].unsqueeze(1).broadcast_to((1, NTILE, E)), ALU.is_ge))
            after(v.tensor_reduce(ex[:], ended, AX.X, ALU.add))
            after(v.tensor_tensor(is_ex[:], cf[0:1, CF_IOTA:CF_IOTA + E + 1].unsqueeze(1).broadcast_to((1, NTILE, E + 1)),
                                  ex[:].unsqueeze(2).broadcast_to((1, NTILE, E + 1)), ALU.is_equal))
            after(v.tensor_tensor(is_ex[:], is_ex[:], starts[0:1, :].unsqueeze(1).broadcast_to((1, NTILE, E + 1)), ALU.mult))
            after(v.tensor_reduce(row[:], is_ex[:], AX.X, ALU.add))
            after(v.scalar_tensor_tensor(out=row[:], in0=number, scalar=float(SLOTS), in1=row[:], op0=ALU.mult, op1=ALU.add))
            after(v.tensor_copy(row_u[:], row[:]))
            after(v.tensor_scalar(ex7[:], ex[:], float(E - 1), None, ALU.min))
            assert count[0] == TABLE
            for n, (_, (high, low)) in enumerate(weight_parts(0)):
                v.wait_ge(s_high0, n + 1)
                v.wait_ge(s_first[n], 16)
                v.tensor_tensor(low, as_part(first[n], n).unsqueeze(1), high, ALU.subtract).then_inc(s_split, 2)

            def weigh(j):
                v.wait_ge(s_t, j + 1)
                for k in range(KD):
                    last = v.tensor_scalar(nf[:, k, :], pt[:, k, :], lncol[:, 2, k:k + 1], lncol[:, 3, k:k + 1], ALU.mult, ALU.add)
                last.then_inc(s_nf, 1)
                v.wait_ge(s_nh, j + 1)
                v.tensor_tensor(nx[1][:], nf[:], nx[0][:], ALU.subtract).then_inc(s_nl, 1)

            def body(j, n, h):
                wait(v, s_y, j * ST)
                for f in range(FT + 1):
                    if f < FT:
                        v.wait_ge(s_gelu, j * FT + f + 1)
                        v.tensor_copy(hid[0][:, f, :], hf[:, f % NH, :]).then_inc(s_hi, 1)
                    if f >= 1:
                        v.wait_ge(s_hi, j * FT + f)
                        v.tensor_tensor(hid[1][:, f - 1, :], hf[:, (f - 1) % NH, :], hid[0][:, f - 1, :], ALU.subtract).then_inc(s_lo, 1)
                if not isinstance(j, int) or j + 1 < NTILE:
                    weigh(j + 1)

            weigh(0)
            tiles_loop(v, body)
            v.wait_ge(s_eg, 1)
            after(v.tensor_scalar(den[:], eg[:], 1.0, None, ALU.add))
            after(v.reciprocal(keep["g1"][:], den[:]))
            after(v.tensor_tensor(keep["g2"][:], eg[:], keep["g1"][:], ALU.mult))
            place = keep["place"][:].rearrange("p b n -> p (b n)")
            after(v.tensor_scalar(shift[:], tiles[:], float(SLOTS), -float(REGION), ALU.mult, ALU.add))
            after(v.tensor_copy(moved, place))
            for e in range(1, E):
                after(v.tensor_scalar(move, place, float(e * REGION), shift[:, e - 1:e], ALU.is_ge, ALU.mult))
                after(v.tensor_tensor(moved, moved, move, ALU.add))
            after(v.tensor_copy(keep["place_y"][:].rearrange("p b n -> p (b n)"), moved))

        @block.tensor
        def _(pe):
            ones3, idf = cb[0:3, CB_ONE:CB_ONE + P], cf[:, CF_ID:CF_ID + P]

            def turn_tile(j, n, h):
                pe.wait_ge(s_xt[n], h * 16 + 16)
                wait(pe, s_nf, j)
                for k in range(KD):
                    for s in range(ST):
                        last = pe.transpose(pt[:, k, s * P:(s + 1) * P], xt[n][:, s, k * P:(k + 1) * P], idf)
                last.then_inc(s_t, 1)

            pe.wait_ge(s_tab, TABLE)

            def body(j, n, h):
                e = pe.value_load(ex7[0:1, bass.ds(j, 1)], min_val=0, max_val=E - 1)
                one = bass.ds(e, 1)
                pe.wait_ge(s_split, (e + 1) * (2 * PARTS))
                pe.sem_inc(s_seen_pe, 1)
                pe.wait_ge(s_nl, j + 1)
                for f in range(FT):
                    wait(pe, s_gelu, j * FT + f + 1 - NH)
                    i = 0
                    for k in range(KD):
                        for wp, xp in ((0, 0), (0, 1), (1, 0)):
                            last = pe.matmul(hb[f % NH][:, 0:SLOTS], w1[wp][:, one, k, f * P:(f + 1) * P].rearrange("p o f -> p (o f)"),
                                             nx[xp][:, k, :], start=i == 0, stop=i == 3 * KD - 1)
                            i += 1
                    last.then_inc(s_h, 1)
                if not isinstance(j, int) or j + 1 < NTILE:
                    turn_tile(j + 1, 1 - n, h + n)
                for k in range(ST):
                    wait(pe, s_yt, (j - 1) * ST + k + 1)
                    out = yb[k][:, 0:D]
                    pe.sem_inc(s_seen_pe, 1)
                    pe.matmul(out, ones3, rows[:, bass.ds(e * D + RW_FC2, D)], start=True, stop=False)
                    for f in range(FT):
                        if k == 0:
                            pe.wait_ge(s_lo, j * FT + f + 1)
                        for hp, wp in ((0, 0), (0, 1), (1, 0)):
                            last = pe.matmul(out, hid[hp][:, f, k * P:(k + 1) * P],
                                             w2[wp][:, one, f, :].rearrange("p o d -> p (o d)"), start=False, stop=f == FT - 1 and hp == 1)
                    last.then_inc(s_y, 1)

            turn_tile(0, 0, 0)
            tiles_loop(pe, body)


def last_phase(nc, io, keep, sem):
    res, cf, cb, rows, bounds, kq, lncol = (keep[n] for n in ("res", "cf", "cb", "rows", "bounds", "kq", "lncol"))
    with ExitStack() as ctx:
        def sb(name, shape, dt=F32):
            return ctx.enter_context(nc.sbuf_tensor(name, shape, dt))

        win = sb("win", [P, KD, D])
        where = sb("where", [P, TOPK * QT], U32)
        yg = sb("yg", [P, TOPK, QT, D])
        ones = sb("ones", [P, S])
        halfneg = sb("halfneg_c", [P, QT])
        cx, junk = sb("cx", [P, 2, QT, DC]), sb("junk", [P, QT, DC])
        ss, ra = sb("ss", [P, QT]), sb("ra", [P, 2, QT])
        u = sb("u", [P, 2, QT, D])
        eq, bnd_in = sb("eq", [P, QT, S]), sb("bnd_in", [P, QT, S], BF16)
        bnd, cum, plug = sb("bnd", [P, S]), sb("cum", [P, S]), sb("plug", [P, S])
        take = sb("take", [P, QT, S])
        mt = sb("mt", [P, QT, S])
        sth, mvh, rh = sb("sth", [P, QT, 6]), sb("mvh", [P, QT, 2]), sb("rh", [P, 7, QT])
        xh, nt = sb("xh_c", [P, QT, D]), sb("nt", [P, KD, S])
        x3 = sb("x3", [P, 2, QT, D])
        stq, mvq, rq = sb("stq", [P, QT, 6]), sb("mvq", [P, QT, 2]), sb("rq", [P, 2, QT])
        xb = sb("xb", [P, QT, D], BF16)
        qv, qe, qb, qsum = (sb(n, [P, QT, D]) for n in ("qv", "qe", "qb", "qsum"))
        qq = sb("qq", [P, QT, D], BF16)
        qt = sb("qt", [P, KD, S], BF16)
        y, ybias = sb("y", [P, QT, D], BF16), sb("ybias", [P, QT, D], BF16)
        out = sb("out_t", [P, QT, D])
        p_cnt, p_mt, p_t, p_h, p_q, p_y = (ctx.enter_context(nc.psum_tensor(n, [P, 512], F32)) for n in ("p_cnt", "p_mt", "p_t", "p_h", "p_q", "p_y"))

        s_load, s_cx, s_set, s_out = sem("l_load"), sem("l_ctx"), sem("l_set"), sem("l_out")
        s_seen = {e.engine: sem(f"l_seen_{n}") for e, n in ((nc.gpsimd, "pool"), (nc.vector, "dve"))}
        AD = Steps(sem("a_dve"), "eq bound bnd cum plug take u")
        AP_ = Steps(sem("a_pool"), "ms rms")
        AA = Steps(sem("a_act"), "square mt")
        AE = Steps(sem("a_pe"), "cnt mt")
        SD = Steps(sem("s_dve"), "sum1 sum2 stats aggr")
        HD = Steps(sem("h_dve"), "xh x3")
        HA = Steps(sem("h_act"), "nt")
        GP = Steps(sem("g_pool"), "where")
        s_yg = sem("rows_gathered")
        HP = Steps(sem("s_pool"), "veps r1 r1sq v2 v2eps r2 r12")
        HE = Steps(sem("h_pe"), "t h")
        QD = Steps(sem("q_dve"), "stats aggr xb exp big sum q bias")
        QP = Steps(sem("q_pool"), "veps rstd out")
        QA = Steps(sem("q_act"), "v qt y")
        QE = Steps(sem("q_pe"), "t y")

        def passed(eng, steps, name, t, lag, back=0):
            if t.ref - lag - back >= 0:
                eng.wait_ge(steps.sem, steps.at(name, t.b(lag) - back))
                if t.loop and (eng is nc.gpsimd or eng is nc.vector and name in ("stats", "sum2", "xh")):
                    eng.sem_inc(s_seen[eng.engine], 1)

        def parity(b):
            return bass.ds(b % 2, 1)

        block = ctx.enter_context(nc.Block())

        @block.sync
        def _(sp):
            sp.dma_start(win[:], io["win"].rearrange("(k p) n -> p k n", p=P)).then_inc(s_load, 16)

            def turn(t):
                if t.on(0):
                    passed(sp, AD, "u", t, 0, 2)
                    passed(sp, AA, "square", t, 0, 1)
                    sp.dma_start(cx[:, parity(t.b(0))], io["ctx"][bass.ds(t.b(0), 1)].rearrange("o (t p) d -> p o t d", p=P)).then_inc(s_cx, 16)
                if t.on(3):
                    passed(sp, QP, "out", t, 3)
                    sp.dma_start(io["out"][bass.ds(t.b(3), 1)].rearrange("o (t p) d -> p (o t) d", p=P), out[:]).then_inc(s_out, 16)

            run_turns(sp, turn, lambda t: None)
            sp.wait_ge(s_out, 16 * B)

        @block.gpsimd
        def _(pool):
            pool.memset(halfneg[:], -0.5)
            pool.memset(ones[:], 1.0).then_inc(s_set, 1)
            pool.wait_ge(s_set, 1)

            def gather(t, lag):
                if t.ref - lag >= 1:
                    pool.wait_ge(s_yg, t.b(lag) * (16 * TOPK * QT))
                    pool.sem_inc(s_seen[pool.engine], 1)
                pool.tensor_copy(where[:].unsqueeze(1), keep["place_y"][:, bass.ds(t.b(lag), 1), :]).then_inc(GP.sem, 1)
                passed(pool, GP, "where", t, lag)
                passed(pool, SD, "sum2", t, lag, 1)
                for k in range(TOPK):
                    for tt in range(QT):
                        n = k * QT + tt
                        pool.indirect_dma_start(yg[:, k, tt, :], None, keep["ys"][:, :], bass.IndirectOffsetOnAxis(where[:, n:n + 1], 0))\
                            .then_inc(s_yg, 16)

            def turn(t):
                if t.on(3):
                    passed(pool, QD, "bias", t, 3)
                    if t.ref - 3 >= 1:
                        pool.wait_ge(s_out, t.b(3) * 16)
                    pool.tensor_tensor(out[:].unsqueeze(1), x3[:, parity(t.b(3))], ybias[:].unsqueeze(1), ALU.add).then_inc(QP.sem, 1)
                if t.on(2):
                    passed(pool, QD, "aggr", t, 2)
                    pool.tensor_scalar(rq[:, 0, :], mvq[:, :, 1], EPS, None, ALU.add).then_inc(QP.sem, 1)
                    passed(pool, QP, "veps", t, 2)
                    pool.tensor_tensor(rq[:, 1, :], rq[:, 0, :], halfneg[:], ALU.pow).then_inc(QP.sem, 1)
                if t.on(0):
                    passed(pool, AA, "square", t, 0)
                    pool.tensor_scalar(ra[:, 0, :], ss[:], 1.0 / DC, EPS, ALU.mult, ALU.add).then_inc(AP_.sem, 1)
                    passed(pool, AP_, "ms", t, 0)
                    passed(pool, AD, "u", t, 0, 1)
                    pool.tensor_tensor(ra[:, 1, :], ra[:, 0, :], halfneg[:], ALU.pow).then_inc(AP_.sem, 1)
                if t.on(-1):
                    gather(t, -1)
                if t.on(0):
                    v = mvh[:, :, 1]
                    passed(pool, SD, "aggr", t, 0)
                    pool.tensor_scalar(rh[:, 0, :], v, EPS, None, ALU.add).then_inc(HP.sem, 1)
                    passed(pool, HP, "veps", t, 0)
                    pool.tensor_tensor(rh[:, 1, :], rh[:, 0, :], halfneg[:], ALU.pow).then_inc(HP.sem, 1)
                    passed(pool, HP, "r1", t, 0)
                    pool.tensor_tensor(rh[:, 2, :], rh[:, 1, :], rh[:, 1, :], ALU.mult).then_inc(HP.sem, 1)
                    passed(pool, HP, "r1sq", t, 0)
                    pool.tensor_tensor(rh[:, 3, :], rh[:, 2, :], v, ALU.mult).then_inc(HP.sem, 1)
                    passed(pool, HP, "v2", t, 0)
                    pool.tensor_scalar(rh[:, 4, :], rh[:, 3, :], EPS, None, ALU.add).then_inc(HP.sem, 1)
                    passed(pool, HP, "v2eps", t, 0)
                    pool.tensor_tensor(rh[:, 5, :], rh[:, 4, :], halfneg[:], ALU.pow).then_inc(HP.sem, 1)
                    passed(pool, HP, "r2", t, 0)
                    passed(pool, HD, "xh", t, 1)
                    pool.tensor_tensor(rh[:, 6, :], rh[:, 5, :], rh[:, 1, :], ALU.mult).then_inc(HP.sem, 1)

            run_turns(pool, turn, lambda t: gather(t, 0))

        @block.scalar
        def _(act):
            def turn(t):
                if t.on(0):
                    act.wait_ge(s_cx, (t.b(0) + 1) * 16)
                    passed(act, AP_, "ms", t, 0, 1)
                    for tt in range(QT):
                        last = act.activation(junk[:, tt, :].unsqueeze(1), cx[:, parity(t.b(0)), tt, :], ACT.Square, accum_out=ss[:, tt:tt + 1])
                    last.then_inc(AA.sem, 1)
                if t.on(1):
                    passed(act, HE, "t", t, 1)
                    pt = p_t[:].rearrange("p (k s) -> p k s", k=KD)
                    passed(act, HE, "h", t, 1, 1)
                    for k in range(KD):
                        last = act.activation(nt[:, k, :], pt[:, k, :], ACT.Copy, scale=lncol[:, 4, k:k + 1])
                    last.then_inc(HA.sem, 1)
                if t.on(2):
                    passed(act, QD, "xb", t, 2)
                    act.activation(qv[:], xb[:], ACT.Copy, scale=keep["r_in"][:, 0:1]).then_inc(QA.sem, 1)
                if t.on(2):
                    passed(act, QE, "t", t, 2)
                    act.activation(qt[:].rearrange("p k s -> p (k s)"), p_q[:].bitcast(BF16)[:, 0:2 * S], ACT.Copy).then_inc(QA.sem, 1)
                if t.on(0):
                    passed(act, AE, "mt", t, 0)
                    passed(act, HE, "h", t, 0, 1)
                    act.activation(mt[:].rearrange("p t s -> p (t s)"), p_mt[:], ACT.Copy).then_inc(AA.sem, 1)
                if t.on(2):
                    passed(act, QE, "y", t, 2)
                    passed(act, QD, "bias", t, 2, 1)
                    act.activation(y[:].rearrange("p t d -> p (t d)"), p_y[:], ACT.Copy, scale=keep["s_out"][:, 0:1]).then_inc(QA.sem, 1)

            run_turns(act, turn, lambda t: None)

        @block.vector
        def _(v):
            v.wait_ge(s_set, 1)

            def turn(t):
                a, h, q = t.on(0), t.on(1), t.on(2)
                if h:
                    tok = [res[:, bass.ds(t.b(1) * QT + tt, 1), :] for tt in range(QT)]
                    passed(v, HP, "r12", t, 1)
                    passed(v, HE, "t", t, 1, 1)
                    for tt in range(QT):
                        last = v.tensor_scalar(xh[:, tt, :].unsqueeze(1), tok[tt], mvh[:, tt, 0:1], rh[:, 6, tt:tt + 1], ALU.subtract, ALU.mult)
                    last.then_inc(HD.sem, 1)
                if a:
                    iota = cf[:, CF_IOTA:CF_IOTA + S]
                    where = lambda side, tt: bounds[:, side, tt, bass.ds(t.b(0), 1)]
                    passed(v, AE, "cnt", t, 0, 1)
                    for tt in range(QT):
                        last = v.tensor_scalar(eq[:, tt, :], iota, where(0, tt), None, ALU.is_equal)
                    last.then_inc(AD.sem, 1)
                if t.on(3):
                    passed(v, QA, "y", t, 3)
                    passed(v, QP, "out", t, 3, 1)
                    v.tensor_tensor(ybias[:], y[:], keep["bias"][:].unsqueeze(1).broadcast_to((P, QT, D)), ALU.add).then_inc(QD.sem, 1)
                if q:
                    x3q = x3[:, parity(t.b(2))]
                    passed(v, HD, "x3", t, 2)
                    for tt in range(QT):
                        last = v.bn_stats(stq[:, tt, :], x3q[:, :, tt, :].rearrange("p o d -> p (o d)"))
                    last.then_inc(QD.sem, 1)
                if a:
                    passed(v, AD, "eq", t, 0)
                    for tt in range(QT):
                        last = v.scalar_tensor_tensor(out=bnd_in[:, tt, :], in0=iota, scalar=where(1, tt), in1=eq[:, tt, :],
                                                      op0=ALU.is_equal, op1=ALU.add)
                    last.then_inc(AD.sem, 1)
                if q:
                    passed(v, QD, "stats", t, 2)
                    for tt in range(QT):
                        last = v.bn_aggr(mvq[:, tt, :], stq[:, tt, :])
                    last.then_inc(QD.sem, 1)
                if a:
                    here = [res[:, bass.ds(t.b(0) * QT + tt, 1), :] for tt in range(QT)]

                    def add_rows(k, g):
                        for tt in range(QT):
                            last = v.scalar_tensor_tensor(out=here[tt], in0=yg[:, k, tt, :].unsqueeze(1), scalar=g[:, bass.ds(t.b(0) * QT + tt, 1)],
                                                          in1=here[tt], op0=ALU.mult, op1=ALU.add)
                        last.then_inc(SD.sem, 1)

                    v.wait_ge(s_yg, (t.b(0) + 1) * (16 * TOPK * QT))
                    add_rows(0, keep["g1"])
                    passed(v, AE, "cnt", t, 0)
                    v.tensor_scalar(bnd[:], p_cnt[:, 0:S], 1.0, None, ALU.min).then_inc(AD.sem, 1)
                    passed(v, SD, "sum1", t, 0)
                    add_rows(1, keep["g2"])
                    passed(v, AD, "bnd", t, 0)
                    v.tensor_tensor_scan(cum[:], ones[:], bnd[:], 0.0, ALU.mult, ALU.add).then_inc(AD.sem, 1)
                    passed(v, SD, "sum2", t, 0)
                    for tt in range(QT):
                        last = v.bn_stats(sth[:, tt, :], here[tt].rearrange("p o d -> p (o d)"))
                    last.then_inc(SD.sem, 1)
                    passed(v, AD, "cum", t, 0)
                    v.tensor_scalar(plug[:], cum[:], -1.0, 0.0, ALU.add, ALU.max).then_inc(AD.sem, 1)
                if q:
                    passed(v, QP, "rstd", t, 2)
                    for tt in range(QT):
                        last = v.tensor_scalar(xb[:, tt, :].unsqueeze(1), x3q[:, :, tt, :], mvq[:, tt, 0:1], rq[:, 1, tt:tt + 1], ALU.subtract, ALU.mult)
                    last.then_inc(QD.sem, 1)
                if a:
                    passed(v, SD, "stats", t, 0)
                    passed(v, HD, "xh", t, 1)
                    for tt in range(QT):
                        last = v.bn_aggr(mvh[:, tt, :], sth[:, tt, :])
                    last.then_inc(SD.sem, 1)
                    passed(v, AD, "plug", t, 0)
                    passed(v, AE, "mt", t, 0, 1)
                    for tt in range(QT):
                        last = v.tensor_scalar(take[:, tt, :], plug[:], cf[:, CF_ROW + tt:CF_ROW + tt + 1], None, ALU.is_equal)
                    last.then_inc(AD.sem, 1)
                if a:
                    passed(v, AP_, "rms", t, 0)
                    passed(v, HE, "h", t, 0, 2)
                    for tt in range(QT):
                        last = v.scalar_tensor_tensor(out=u[:, parity(t.b(0)), tt, :].rearrange("p o d -> p (o d)"), in0=cx[:, parity(t.b(0)), tt, 0:D].rearrange("p o d -> p (o d)"),
                                                      scalar=ra[:, 1, tt:tt + 1], in1=keep["ginit"][:], op0=ALU.mult, op1=ALU.mult)
                    last.then_inc(AD.sem, 1)
                if q:
                    passed(v, QA, "v", t, 2)
                    v.tensor_single_scalar(qe[:].bitcast(I32), qv[:].bitcast(I32), 0x7F800000, op=ALU.bitwise_and).then_inc(QD.sem, 1)
                    passed(v, QD, "exp", t, 2)
                    v.tensor_scalar(qb[:], qe[:], 2.0 ** -6, C20, ALU.max, ALU.mult).then_inc(QD.sem, 1)
                    passed(v, QD, "big", t, 2)
                    v.tensor_tensor(qsum[:], qv[:], qb[:], ALU.add).then_inc(QD.sem, 1)
                    passed(v, QD, "sum", t, 2)
                    passed(v, QE, "t", t, 2, 1)
                    v.tensor_tensor(qq[:], qsum[:], qb[:], ALU.subtract).then_inc(QD.sem, 1)
                if h:
                    passed(v, HE, "h", t, 1)
                    passed(v, QP, "out", t, 1, 2)
                    v.tensor_tensor(x3[:, parity(t.b(1))].rearrange("p o t d -> p o (t d)"),
                                    p_h[:].unsqueeze(1),
                                    res[:, bass.ds(t.b(1) * QT, QT), :].rearrange("p t d -> p (t d)").unsqueeze(1), ALU.add).then_inc(HD.sem, 1)

            run_turns(v, turn, lambda t: None)

        @block.tensor
        def _(pe):
            idb, idf = cb[:, CB_ID:CB_ID + P], cf[:, CF_ID:CF_ID + P]
            ones3, onesb = cb[0:3, CB_ONE:CB_ONE + P], cb[:, CB_ONE:CB_ONE + P]
            pe.wait_ge(s_load, 16)

            def turn(t):
                a, h, q = t.on(0), t.on(1), t.on(2)
                if h:
                    passed(pe, HD, "xh", t, 1)
                    passed(pe, HA, "nt", t, 1, 1)
                    for k in range(KD):
                        for tt in range(QT):
                            last = pe.transpose(p_t[:, k * S + tt * P:k * S + (tt + 1) * P], xh[:, tt, k * P:(k + 1) * P], idf)
                    last.then_inc(HE.sem, 1)
                if a:
                    passed(pe, AD, "bound", t, 0)
                    passed(pe, AD, "bnd", t, 0, 1)
                    for tt in range(QT):
                        last = pe.matmul(p_cnt[:, 0:S], onesb, bnd_in[:, tt, :], start=tt == 0, stop=tt == QT - 1)
                    last.then_inc(AE.sem, 1)
                if h:
                    passed(pe, HA, "nt", t, 1)
                    passed(pe, AA, "mt", t, 1)
                    passed(pe, AD, "u", t, 1)
                    passed(pe, HD, "x3", t, 1, 1)
                    half = parity(t.b(1))
                    for tt in range(QT):
                        o = p_h[:, tt * D:(tt + 1) * D]
                        ts_ = slice(tt * P, (tt + 1) * P)
                        pe.matmul(o, ones3, rows[:, RW_IN:RW_IN + D], start=True, stop=False)
                        for k in range(KD):
                            pe.matmul(o, nt[:, k, ts_], win[:, k, :], start=False, stop=False)
                        for k in range(QT):
                            last = pe.matmul(o, mt[:, k, ts_], u[:, half, k, :].rearrange("p o d -> p (o d)"),
                                             start=False, stop=k == QT - 1)
                    last.then_inc(HE.sem, 1)
                if q:
                    passed(pe, QD, "q", t, 2)
                    passed(pe, QA, "qt", t, 2, 1)
                    pq = p_q[:].bitcast(BF16)
                    for k in range(KD):
                        for tt in range(QT):
                            last = pe.transpose(pq[:, k * S + tt * P:k * S + (tt + 1) * P], qq[:, tt, k * P:(k + 1) * P], idb)
                    last.then_inc(QE.sem, 1)
                if a:
                    passed(pe, AD, "take", t, 0)
                    passed(pe, AA, "mt", t, 0, 1)
                    l0, l1 = cf[:, CF_L0:CF_L0 + P], cf[:, CF_L1:CF_L1 + P]
                    pe.matmul(p_mt[:, 0:S], l0, take[:, 0, :], start=True, stop=False)
                    pe.matmul(p_mt[:, 0:S], l1, take[:, 1, :], start=False, stop=True)
                    pe.matmul(p_mt[:, S:2 * S], l0, take[:, 1, :], start=True, stop=True).then_inc(AE.sem, 1)
                if q:
                    passed(pe, QA, "qt", t, 2)
                    passed(pe, QA, "y", t, 2, 1)
                    for tt in range(QT):
                        for k in range(KD):
                            last = pe.matmul(p_y[:, tt * D:(tt + 1) * D], qt[:, k, tt * P:(tt + 1) * P], kq[:, k, :], start=k == 0, stop=k == KD - 1)
                    last.then_inc(QE.sem, 1)

            run_turns(pe, turn, lambda t: None)


def build(nc, io):
    with ExitStack() as ctx:
        def sb(name, shape, dt=F32):
            return ctx.enter_context(nc.sbuf_tensor(name, shape, dt))

        def sem(name):
            return ctx.enter_context(nc.semaphore(name))

        keep = {
            "res": sb("res", [P, NT, D]),
            "gap": sb("gap", [P, NT]), "base": sb("base", [P, E]), "place": sb("place", [P, B, TOPK * QT]), "place_y": sb("place_y", [P, B, TOPK * QT], U32),
            "g1": sb("g1", [P, NT]), "g2": sb("g2", [P, NT]),
            "xs": nc.dram_tensor("xs", (NROWS, D), F32, kind="Internal").ap(),
            "ys": nc.dram_tensor("ys", (NTILE * SLOTS, D), F32, kind="Internal").ap(),
            "cf": sb("cf", [P, CF_N]), "cb": sb("cb", [P, CB_N], BF16), "rows": sb("rows", [3, RW_N], BF16),
            "kext": sb("kext", [P, B, QT, 4], BF16),
            "any4": sb("any4", [P, B]), "kq": sb("kq", [P, KD, D], BF16), "bounds": sb("bounds", [P, 2, QT, B]),
            "bias": sb("bias", [P, D], BF16), "lncol": sb("lncol", [P, 5, KD]),
            "r_in": sb("r_in", [P, 1]), "s_out": sb("s_out", [P, 1]), "ginit": sb("ginit_s", [P, D]),
        }
        setup_phase(nc, io, keep, sem)
        attention_phase(nc, io, keep, sem)
        expert_phase(nc, io, keep, sem)
        last_phase(nc, io, keep, sem)


def constants(np, bf16):
    cf = np.zeros((P, CF_N), np.float32)
    i = np.arange(P)
    cf[:, CF_ID:CF_ID + P] = np.eye(P)
    cf[:, CF_IOTA:CF_IOTA + S] = np.arange(S)
    for t in range(QT):
        cf[:, CF_ROW + t] = i + t * P
    cf[:, CF_TRI:CF_TRI + P] = i[:, None] <= i[None, :]
    cf[:, CF_ONE:CF_ONE + P] = 1
    decay = -math.expm1(-PATCH_EPS)
    for at, off in ((CF_L0, 0), (CF_L1, P)):
        d = i[:, None] - i[None, :] + off
        cf[:, at:at + P] = np.where(d >= 0, decay ** np.clip(d, 0, 300).astype(np.float64), 0)
    cf[:, CF_REG:CF_REG + E + 1] = REGION * np.arange(E + 1)
    cb = np.zeros((P, CB_N), np.float32)
    cb[:, CB_TRI:CB_TRI + P] = i[:, None] <= i[None, :]
    cb[:, CB_ID:CB_ID + P] = np.eye(P)
    later = np.where(i[:, None] < i[None, :], -1e30, 0)
    cb[:, CB_MQ:CB_MQ + 2 * P] = np.tile(later, 2)
    cb[:, CB_MK:CB_MK + 2 * P] = np.tile(later.T, 2)
    cb[:, CB_ONE:CB_ONE + P] = 1
    return cf, cb.astype(bf16)


def kernel(**inputs):
    import numpy as np
    import concourse.bacc as bacc
    from concourse.bass_utils import run_bass_kernel_spmd as run

    a = {k: np.asarray(v) for k, v in inputs.items()}
    cf, cb = constants(np, a["L1_ffn_kernel"].dtype)
    rows = np.concatenate([a["L0_ffn_bqkv"], a["L0_ffn_bo"], a["L0_ffn_fc2_b"].reshape(-1), a["L1_xattn_b_in"]])
    data = {
        "cf": cf, "cb": cb, "x": a["x"], "ctx": a["ctx_2048"], "seq": a["itok_Bx1_68_817"].reshape(-1),
        "lens": a["mask_BxS2_if0"].T.reshape(QT, P, B).transpose(1, 0, 2), "b": a["L0_xattn_b"].reshape(QT, P).T, "rows": rows,
        "wqkv": a["L0_ffn_Wqkv"], "wo": a["L0_ffn_Wo"], "wgate": a["L0_ffn_gate_W"],
        "lncol": np.stack([a["L0_ffn_ln1_w"], a["L0_ffn_ln1_b"], a["L0_ffn_ln2_w"], a["L0_ffn_ln2_b"], a["L1_xattn_g_res"]]).reshape(5, KD, P).transpose(2, 0, 1),
        "fc1": a["L0_ffn_fc1_w"].transpose(0, 2, 1), "fc1b": a["L0_ffn_fc1_b"].reshape(E * FT, P).T, "fc2": a["L0_ffn_fc2_w"].transpose(0, 2, 1),
        "win": a["L1_xattn_W_in"].T, "ginit": a["L1_xattn_g_init"][0:D],
        "kern": a["L1_ffn_kernel"], "s_in": a["L1_ffn_input_scale"], "s_k": a["L1_ffn_kernel_scale"], "bias": a["L1_ffn_bias"],
    }
    data = {k: np.ascontiguousarray(v) for k, v in data.items()}
    nc = bacc.Bacc("TRN2", target_bir_lowering=False, num_devices=1)
    io = {k: nc.dram_tensor(f"in_{k}", v.shape, mybir.dt.from_np(v.dtype), kind="ExternalInput").ap() for k, v in data.items()}
    io["out"] = nc.dram_tensor("out", (B, S, D), F32, kind="ExternalOutput").ap()
    build(nc, io)
    r = run(nc, [{f"in_{k}": v for k, v in data.items()}], core_ids=[0])
    return r.results[0]["out"]
```
